# Optimizing a Trainium2 kernel written in Bass

```python
import numpy as np
import jax
import jax.numpy as jnp

def _softmax(x, axis=-1):
    return jax.nn.softmax(x, axis=axis)

def _gelu(x):
    return jax.nn.gelu(x, approximate=True)

def _silu(x):
    return jax.nn.silu(x)

def _sigmoid(x):
    return jax.nn.sigmoid(x)

def _layernorm(x, axis=-1, eps=1e-05):
    m = jnp.mean(x, axis=axis, keepdims=True)
    v = jnp.var(x, axis=axis, keepdims=True)
    return (x - m) / jnp.sqrt(v + eps)

def _scatter_add(tgt, idx, src, axis=0):
    return tgt.at[idx].add(src)

def _segment_sum(src, seg, n):
    return jax.ops.segment_sum(src, seg, n)
kernel_name = 'mk_perceiver_d1_seqx_r4_3489e7'

def setup_inputs(seed: int=0):
    np.random.seed(seed)
    _w = jnp.asarray

    def _rec_inputs():
        import jax
        import jax.numpy as jnp
        _rk = jax.random.key(seed)
        x = -0.0002928 + 1 * jax.random.normal(jax.random.fold_in(_rk, 1), (32, 32, 512), jnp.float32)
        _lenS = 32 - jax.random.randint(jax.random.fold_in(_rk, 7), (32,), 0, max(1, 32 // 4) + 1, jnp.int32)
        _lenS2 = 257 - jax.random.randint(jax.random.fold_in(_rk, 8), (32,), 0, max(1, 257 // 4) + 1, jnp.int32)
        _ctx_512P = jax.random.normal(jax.random.fold_in(_rk, 11), (32, 16, 128), jnp.float32)
        _ctx_512c = jax.random.dirichlet(jax.random.fold_in(_rk, 511), 0.3 * jnp.ones((16,), jnp.float32), (32, 257))
        _ctx_512t = jnp.einsum('bsk,bkd->bsd', _ctx_512c, _ctx_512P)
        _ctx_512t = _ctx_512t * jax.lax.rsqrt(jnp.mean(jnp.square(_ctx_512t)) + 1e-12) * 0.953939
        ctx_512 = 0.000227908 + 0.99994 * (_ctx_512t + 0.3 * jax.random.normal(jax.random.fold_in(_rk, 611), (32, 257, 128), jnp.float32))
        return (x, ctx_512)
    x, ctx_512 = _rec_inputs()

    def _L0_xattn_setup():
        import jax, jax.numpy as jnp
        import numpy as np
        B, S, L = (2, 256, 256)
        DIM_Q, H, K, D_C, D_CQ, R = (512, 16, 128, 128, 384, 64)

        def _rope_tables(seq_len, dim, dtype):
            inv_freq = 1.0 / 10000.0 ** (jnp.arange(0, dim, 2, dtype=dtype) / dim)
            t = jnp.arange(seq_len, dtype=dtype)
            freqs = t[:, None] * inv_freq[None, :]
            sin = jnp.repeat(jnp.sin(freqs), 2, axis=-1)
            cos = jnp.repeat(jnp.cos(freqs), 2, axis=-1)
            return (sin, cos)

        def _rotate_half(x):
            h = x.shape[-1] // 2
            return jnp.concatenate([-x[..., h:], x[..., :h]], axis=-1)
        key = jax.random.key(seed)
        ks = jax.random.split(key, 8)
        s_in = 1.0 / np.sqrt(DIM_Q)
        s_k = 1.0 / np.sqrt(K)
        s_cq = 1.0 / np.sqrt(D_CQ)
        s_c = 1.0 / np.sqrt(D_C)
        return {'hidden_q': jax.random.normal(ks[0], (B, S, DIM_Q), jnp.float32), 'kv_c': jax.random.normal(ks[1], (B, L, D_C), jnp.float32), 'Wq': jax.random.normal(ks[2], (H * K, DIM_Q), jnp.float32) * s_in, 'w_kc_q': jax.random.normal(ks[3], (H, K, D_CQ), jnp.float32) * s_k, 'w_kc_kv': jax.random.normal(ks[4], (H, K, D_C), jnp.float32) * s_k, 'W_qr': jax.random.normal(ks[5], (H, D_CQ, R), jnp.float32) * s_cq / np.sqrt(R), 'W_kr': jax.random.normal(ks[6], (H, D_C, R), jnp.float32) * s_c, 'Wo': jax.random.normal(ks[7], (DIM_Q, H * K), jnp.float32) * s_k}
    _L0_xattn_all = _L0_xattn_setup()
    _L0_xattn_in = {k: v for k, v in _L0_xattn_all.items() if k in ('Wq', 'w_kc_q', 'w_kc_kv', 'W_qr', 'W_kr', 'Wo')}
    del _L0_xattn_all

    def _L0_attn_setup():
        import jax, jax.numpy as jnp
        import numpy as np
        B_SZ, SEQ, D_MODEL = (2, 512, 512)
        D_INNER, D_XB, INTER = (1024, 256, 2048)
        HEADDIM = 64
        DSTATE = 64
        NHEADS = D_INNER // HEADDIM
        N_XB = D_XB // HEADDIM
        REP = NHEADS // N_XB
        D_IN_PROJ = D_INNER + D_XB + D_XB + D_INNER + NHEADS
        EPS = 1e-05

        def _layernorm(x, w, b):
            mu = jnp.mean(x, -1, keepdims=True)
            var = jnp.mean((x - mu) ** 2, -1, keepdims=True)
            return (x - mu) * jax.lax.rsqrt(var + EPS) * w + b

        def _mamba2(hs, W_in, dt_bias, A_log, D, norm_w, W_out):
            B, L, _ = hs.shape
            zxbcdt = hs @ W_in
            splits = [D_INNER, D_INNER + D_XB, D_INNER + 2 * D_XB, D_INNER + 2 * D_XB + D_INNER]
            z, xb, Bp, Cp, dt = jnp.split(zxbcdt, splits, axis=-1)
            xh = jnp.repeat(xb.reshape(B, L, N_XB, HEADDIM), REP, axis=2)
            Bh = jnp.repeat(Bp.reshape(B, L, N_XB, DSTATE), REP, axis=2)
            Ch = Cp.reshape(B, L, NHEADS, DSTATE)
            dt = jax.nn.softplus(dt + dt_bias)
            A = -jnp.exp(A_log)
            dA = jnp.exp(dt * A)

            def step(state, inp):
                dA_t, dt_t, B_t, x_t, C_t = inp
                dBx = (dt_t[:, :, None] * x_t)[..., None] * B_t[:, :, None, :]
                state = state * dA_t[:, :, None, None] + dBx
                y_t = jnp.einsum('bhpn,bhn->bhp', state, C_t)
                return (state, y_t)
            xs = (jnp.swapaxes(dA, 0, 1), jnp.swapaxes(dt, 0, 1), jnp.swapaxes(Bh, 0, 1), jnp.swapaxes(xh, 0, 1), jnp.swapaxes(Ch, 0, 1))
            state0 = jnp.zeros((B, NHEADS, HEADDIM, DSTATE), hs.dtype)
            _, ys = jax.lax.scan(step, state0, xs)
            y = jnp.swapaxes(ys, 0, 1) + D[None, None, :, None] * xh
            y = y.reshape(B, L, D_INNER)
            yg = y * jax.nn.silu(z)
            yn = yg * jax.lax.rsqrt(jnp.mean(yg * yg, -1, keepdims=True) + EPS) * norm_w
            return yn @ W_out
        key = jax.random.key(seed)
        ks = jax.random.split(key, 10)
        s = 0.02
        return {'hidden_states': jax.random.normal(ks[0], (B_SZ, SEQ, D_MODEL), jnp.float32), 'ln_w': jnp.ones((D_MODEL,), jnp.float32), 'ln_b': jnp.zeros((D_MODEL,), jnp.float32), 'W_in': jax.random.normal(ks[1], (D_MODEL, D_IN_PROJ), jnp.float32) * s, 'dt_bias': jax.random.uniform(ks[2], (NHEADS,), jnp.float32, -4.0, -2.0), 'A_log': jnp.log(jnp.arange(1, NHEADS + 1, dtype=jnp.float32)), 'D': jnp.ones((NHEADS,), jnp.float32), 'norm_w': jnp.ones((D_INNER,), jnp.float32), 'W_out': jax.random.normal(ks[3], (D_INNER, D_MODEL), jnp.float32) * s, 'fc1_w': jax.random.normal(ks[4], (D_MODEL, INTER), jnp.float32) * s, 'fc1_b': jnp.zeros((INTER,), jnp.float32), 'fc2_w': jax.random.normal(ks[5], (INTER, D_MODEL), jnp.float32) * s, 'fc2_b': jnp.zeros((D_MODEL,), jnp.float32)}
    _L0_attn_all = _L0_attn_setup()
    _L0_attn_in = {k: v for k, v in _L0_attn_all.items() if k in ('ln_w', 'ln_b', 'W_in', 'dt_bias', 'A_log', 'D', 'norm_w', 'W_out', 'fc1_w', 'fc1_b', 'fc2_w', 'fc2_b')}
    del _L0_attn_all

    def _L0_ffn_setup():
        import jax, jax.numpy as jnp
        import numpy as np
        N_EXPERTS = 8
        TOP_K = 2
        N_GROUP = 4
        TOPK_GROUP = 2
        ROUTED_SCALE = 1.0

        def _group_limited_topk(scores):
            T, N = scores.shape
            E = N // N_GROUP
            group_scores = scores.reshape(T, N_GROUP, E).max(axis=-1)
            _, gidx = jax.lax.top_k(group_scores, TOPK_GROUP)
            gmask = jax.nn.one_hot(gidx, N_GROUP, dtype=scores.dtype).sum(1)
            smask = jnp.repeat(gmask, E, axis=1)
            masked = jnp.where(smask > 0, scores, jnp.zeros((), scores.dtype))
            topk_w, topk_i = jax.lax.top_k(masked, TOP_K)
            return (topk_w, topk_i)
        key = jax.random.key(seed)
        ks = jax.random.split(key, 8)
        B, S, H, F, FS, N = (2, 256, 512, 352, 704, N_EXPERTS)
        std = jnp.float32(0.02)
        return {'hidden_states': jax.random.normal(ks[0], (B, S, H), jnp.float32), 'gate_weight': jax.random.normal(ks[1], (N, H), jnp.float32) * std, 'gate_w': jax.random.normal(ks[2], (N, F, H), jnp.float32) * std, 'up_w': jax.random.normal(ks[3], (N, F, H), jnp.float32) * std, 'down_w': jax.random.normal(ks[4], (N, H, F), jnp.float32) * std, 'sh_gate_w': jax.random.normal(ks[5], (FS, H), jnp.float32) * std, 'sh_up_w': jax.random.normal(ks[6], (FS, H), jnp.float32) * std, 'sh_down_w': jax.random.normal(ks[7], (H, FS), jnp.float32) * std}
    _L0_ffn_all = _L0_ffn_setup()
    _L0_ffn_in = {k: v for k, v in _L0_ffn_all.items() if k in ('gate_weight', 'gate_w', 'up_w', 'down_w', 'sh_gate_w', 'sh_up_w', 'sh_down_w')}
    del _L0_ffn_all
    return {'x': x, 'ctx_512': ctx_512, 'L0_xattn_Wq': _L0_xattn_in['Wq'], 'L0_xattn_w_kc_q': _L0_xattn_in['w_kc_q'], 'L0_xattn_w_kc_kv': _L0_xattn_in['w_kc_kv'], 'L0_xattn_W_qr': _L0_xattn_in['W_qr'], 'L0_xattn_W_kr': _L0_xattn_in['W_kr'], 'L0_xattn_Wo': _L0_xattn_in['Wo'], 'L0_attn_ln_w': _L0_attn_in['ln_w'], 'L0_attn_ln_b': _L0_attn_in['ln_b'], 'L0_attn_W_in': _L0_attn_in['W_in'], 'L0_attn_dt_bias': _L0_attn_in['dt_bias'], 'L0_attn_A_log': _L0_attn_in['A_log'], 'L0_attn_D': _L0_attn_in['D'], 'L0_attn_norm_w': _L0_attn_in['norm_w'], 'L0_attn_W_out': _L0_attn_in['W_out'], 'L0_attn_fc1_w': _L0_attn_in['fc1_w'], 'L0_attn_fc1_b': _L0_attn_in['fc1_b'], 'L0_attn_fc2_w': _L0_attn_in['fc2_w'], 'L0_attn_fc2_b': _L0_attn_in['fc2_b'], 'L0_ffn_gate_weight': _L0_ffn_in['gate_weight'], 'L0_ffn_gate_w': _L0_ffn_in['gate_w'], 'L0_ffn_up_w': _L0_ffn_in['up_w'], 'L0_ffn_down_w': _L0_ffn_in['down_w'], 'L0_ffn_sh_gate_w': _L0_ffn_in['sh_gate_w'], 'L0_ffn_sh_up_w': _L0_ffn_in['sh_up_w'], 'L0_ffn_sh_down_w': _L0_ffn_in['sh_down_w']}

def reference(x, ctx_512, L0_xattn_Wq, L0_xattn_w_kc_q, L0_xattn_w_kc_kv, L0_xattn_W_qr, L0_xattn_W_kr, L0_xattn_Wo, L0_attn_ln_w, L0_attn_ln_b, L0_attn_W_in, L0_attn_dt_bias, L0_attn_A_log, L0_attn_D, L0_attn_norm_w, L0_attn_W_out, L0_attn_fc1_w, L0_attn_fc1_b, L0_attn_fc2_w, L0_attn_fc2_b, L0_ffn_gate_weight, L0_ffn_gate_w, L0_ffn_up_w, L0_ffn_down_w, L0_ffn_sh_gate_w, L0_ffn_sh_up_w, L0_ffn_sh_down_w):
    import jax
    import jax.numpy as jnp

    def _L0_xattn_ref(hidden_q, kv_c, Wq, w_kc_q, w_kc_kv, W_qr, W_kr, Wo):
        import jax, jax.numpy as jnp
        import numpy as np
        B, S, L = (2, 256, 256)
        DIM_Q, H, K, D_C, D_CQ, R = (512, 16, 128, 128, 384, 64)

        def _rope_tables(seq_len, dim, dtype):
            inv_freq = 1.0 / 10000.0 ** (jnp.arange(0, dim, 2, dtype=dtype) / dim)
            t = jnp.arange(seq_len, dtype=dtype)
            freqs = t[:, None] * inv_freq[None, :]
            sin = jnp.repeat(jnp.sin(freqs), 2, axis=-1)
            cos = jnp.repeat(jnp.cos(freqs), 2, axis=-1)
            return (sin, cos)

        def _rotate_half(x):
            h = x.shape[-1] // 2
            return jnp.concatenate([-x[..., h:], x[..., :h]], axis=-1)
        b, s, _ = hidden_q.shape
        l = kv_c.shape[1]
        q_hk = (hidden_q @ Wq.T).reshape(b, s, H, K)
        q_big = jnp.einsum('bshk,hkq->bshq', q_hk, w_kc_q)
        sin, cos = _rope_tables(l, D_C, kv_c.dtype)
        kv_rope = kv_c * cos[None] + _rotate_half(kv_c) * sin[None]
        q_r = jnp.einsum('bshq,hqr->bhsr', q_big, W_qr)
        k_r = jnp.einsum('bld,hdr->bhlr', kv_rope, W_kr)
        scores = jnp.einsum('bhsr,bhlr->bhsl', q_r, k_r)
        attn = jax.nn.softmax(scores, axis=-1)
        ctx_c = jnp.einsum('bhsl,bld->bhsd', attn, kv_rope)
        ctx_lat = jnp.einsum('bhsd,hkd->bshk', ctx_c, w_kc_kv)
        out = ctx_lat.reshape(b, s, H * K) @ Wo.T
        return out

    def _L0_attn_ref(hidden_states, ln_w, ln_b, W_in, dt_bias, A_log, D, norm_w, W_out, fc1_w, fc1_b, fc2_w, fc2_b):
        import jax, jax.numpy as jnp
        import numpy as np
        B_SZ, SEQ, D_MODEL = (2, 512, 512)
        D_INNER, D_XB, INTER = (1024, 256, 2048)
        HEADDIM = 64
        DSTATE = 64
        NHEADS = D_INNER // HEADDIM
        N_XB = D_XB // HEADDIM
        REP = NHEADS // N_XB
        D_IN_PROJ = D_INNER + D_XB + D_XB + D_INNER + NHEADS
        EPS = 1e-05

        def _layernorm(x, w, b):
            mu = jnp.mean(x, -1, keepdims=True)
            var = jnp.mean((x - mu) ** 2, -1, keepdims=True)
            return (x - mu) * jax.lax.rsqrt(var + EPS) * w + b

        def _mamba2(hs, W_in, dt_bias, A_log, D, norm_w, W_out):
            B, L, _ = hs.shape
            zxbcdt = hs @ W_in
            splits = [D_INNER, D_INNER + D_XB, D_INNER + 2 * D_XB, D_INNER + 2 * D_XB + D_INNER]
            z, xb, Bp, Cp, dt = jnp.split(zxbcdt, splits, axis=-1)
            xh = jnp.repeat(xb.reshape(B, L, N_XB, HEADDIM), REP, axis=2)
            Bh = jnp.repeat(Bp.reshape(B, L, N_XB, DSTATE), REP, axis=2)
            Ch = Cp.reshape(B, L, NHEADS, DSTATE)
            dt = jax.nn.softplus(dt + dt_bias)
            A = -jnp.exp(A_log)
            dA = jnp.exp(dt * A)

            def step(state, inp):
                dA_t, dt_t, B_t, x_t, C_t = inp
                dBx = (dt_t[:, :, None] * x_t)[..., None] * B_t[:, :, None, :]
                state = state * dA_t[:, :, None, None] + dBx
                y_t = jnp.einsum('bhpn,bhn->bhp', state, C_t)
                return (state, y_t)
            xs = (jnp.swapaxes(dA, 0, 1), jnp.swapaxes(dt, 0, 1), jnp.swapaxes(Bh, 0, 1), jnp.swapaxes(xh, 0, 1), jnp.swapaxes(Ch, 0, 1))
            state0 = jnp.zeros((B, NHEADS, HEADDIM, DSTATE), hs.dtype)
            _, ys = jax.lax.scan(step, state0, xs)
            y = jnp.swapaxes(ys, 0, 1) + D[None, None, :, None] * xh
            y = y.reshape(B, L, D_INNER)
            yg = y * jax.nn.silu(z)
            yn = yg * jax.lax.rsqrt(jnp.mean(yg * yg, -1, keepdims=True) + EPS) * norm_w
            return yn @ W_out
        residual = hidden_states
        hs = _layernorm(hidden_states, ln_w, ln_b)
        attn = _mamba2(hs, W_in, dt_bias, A_log, D, norm_w, W_out)
        mlp = jax.nn.gelu(hs @ fc1_w + fc1_b, approximate=True) @ fc2_w + fc2_b
        return attn + mlp + residual

    def _L0_ffn_ref(hidden_states, gate_weight, gate_w, up_w, down_w, sh_gate_w, sh_up_w, sh_down_w):
        import jax, jax.numpy as jnp
        import numpy as np
        N_EXPERTS = 8
        TOP_K = 2
        N_GROUP = 4
        TOPK_GROUP = 2
        ROUTED_SCALE = 1.0

        def _group_limited_topk(scores):
            T, N = scores.shape
            E = N // N_GROUP
            group_scores = scores.reshape(T, N_GROUP, E).max(axis=-1)
            _, gidx = jax.lax.top_k(group_scores, TOPK_GROUP)
            gmask = jax.nn.one_hot(gidx, N_GROUP, dtype=scores.dtype).sum(1)
            smask = jnp.repeat(gmask, E, axis=1)
            masked = jnp.where(smask > 0, scores, jnp.zeros((), scores.dtype))
            topk_w, topk_i = jax.lax.top_k(masked, TOP_K)
            return (topk_w, topk_i)
        B, S, H = hidden_states.shape
        h = hidden_states.reshape(-1, H)
        logits = h.astype(jnp.float32) @ gate_weight.astype(jnp.float32).T
        scores = jax.nn.softmax(logits, axis=-1)
        topk_w, topk_i = _group_limited_topk(scores)
        topk_w = (topk_w * ROUTED_SCALE).astype(h.dtype)
        wmat = (jax.nn.one_hot(topk_i, N_EXPERTS, dtype=topk_w.dtype) * topk_w[..., None]).sum(axis=1)
        g = jnp.einsum('th,nfh->ntf', h, gate_w)
        u = jnp.einsum('th,nfh->ntf', h, up_w)
        e = jnp.einsum('ntf,nhf->nth', jax.nn.silu(g) * u, down_w)
        routed = jnp.einsum('nth,tn->th', e, wmat)
        sg = h @ sh_gate_w.T
        su = h @ sh_up_w.T
        shared = jax.nn.silu(sg) * su @ sh_down_w.T
        return (routed + shared).reshape(B, S, H)
    x = x + _L0_xattn_ref(_layernorm(x, axis=-1), ctx_512, L0_xattn_Wq, L0_xattn_w_kc_q, L0_xattn_w_kc_kv, L0_xattn_W_qr, L0_xattn_W_kr, L0_xattn_Wo)
    x = x + _L0_attn_ref(_layernorm(x, axis=-1), L0_attn_ln_w, L0_attn_ln_b, L0_attn_W_in, L0_attn_dt_bias, L0_attn_A_log, L0_attn_D, L0_attn_norm_w, L0_attn_W_out, L0_attn_fc1_w, L0_attn_fc1_b, L0_attn_fc2_w, L0_attn_fc2_b)
    x = x + _L0_ffn_ref(_layernorm(x, axis=-1), L0_ffn_gate_weight, L0_ffn_gate_w, L0_ffn_up_w, L0_ffn_down_w, L0_ffn_sh_gate_w, L0_ffn_sh_up_w, L0_ffn_sh_down_w)
    return x

_drawn_inputs = setup_inputs


def setup_inputs(seed=0):
    import zlib

    import numpy as np

    out = dict(_drawn_inputs(seed))
    spreads = {'L0_attn_ln_w': (1.0, 0.2),
     'L0_attn_ln_b': (0.0, 0.1),
     'L0_attn_D': (1.0, 0.2),
     'L0_attn_norm_w': (1.0, 0.2),
     'L0_attn_fc1_b': (0.0, 0.453),
     'L0_attn_fc2_b': (0.0, 0.1)}
    factors = {'L0_ffn_gate_weight': 8.0,
     'L0_ffn_gate_w': 8.0,
     'L0_ffn_up_w': 8.0,
     'L0_ffn_down_w': 8.0,
     'L0_ffn_sh_gate_w': 2.976,
     'L0_ffn_sh_up_w': 2.886,
     'L0_ffn_sh_down_w': 2.909}
    for name, (base, spread) in spreads.items():
        noise = np.random.default_rng([zlib.crc32(name.encode()), seed]).standard_normal(out[name].shape)
        drawn = base * np.exp(spread * noise) if base else spread * noise
        out[name] = jnp.asarray(drawn.astype(out[name].dtype))
    for name, factor in factors.items():
        out[name] = (out[name] * factor).astype(out[name].dtype)
    return out
```

```python
from contextlib import ExitStack

import concourse.bass as bass
from concourse import mybir

F32 = mybir.dt.float32
F32R = mybir.dt.float32r
ALU = mybir.AluOpType
ACT = mybir.ActivationFunctionType
AX_X = mybir.AxisListType.X

P = 128
B, S, D = 32, 32, 512
L = 257
TOK = B * S
TT = TOK // P
DC = D // P
HALF = 512
NHALF = TOK // HALF
BPT = P // S
H, K, CQ, R = 16, 128, 384, 64
QC = CQ // P
HS = H * S
EPS = 1e-5


def wait(e, sem, value):
    if isinstance(value, int) and value <= 0:
        return
    e.wait_ge(sem, value)


def passes(e, out, hi_l, lo_l, hi_r, lo_r, first, last):
    e.matmul(out, hi_l, hi_r, start=first, stop=False)
    e.matmul(out, hi_l, lo_r, start=False, stop=False)
    return e.matmul(out, lo_l, hi_r, start=False, stop=last)


class Names:

    def __init__(self, nc, ctx, tag):
        self.nc, self.ctx, self.tag = nc, ctx, tag

    def sb(self, name, shape, dt=F32):
        return self.ctx.enter_context(self.nc.sbuf_tensor(f"{self.tag}_{name}", shape, dt))

    def sem(self, name):
        made = self.nc.alloc_semaphore(f"{self.tag}_{name}")
        SEMAPHORES.append(made)
        return made


SEMAPHORES = []


def clear_semaphores(nc):
    nc.clear_and_free_semaphores(list(SEMAPHORES))
    SEMAPHORES.clear()
    nc.all_engine_barrier()


def phase_context_tail(nc, d, g):
    with ExitStack() as ctx:
        n = Names(nc, ctx, "tail")
        row, turned, t2, cosr, sinr = (n.sb(x, [B, P]) for x in ("row", "turned", "t2", "cosr", "sinr"))
        hi, lo = n.sb("hi", [B, P], F32R), n.sb("lo", [B, P], F32R)
        loaded, rotated, split, turned_T, stored = (n.sem(x) for x in ("loaded", "rotated", "split", "turned_T", "stored"))
        ps = g["psum"]
        block = ctx.enter_context(nc.Block())

        @block.sync
        def _(sp):
            sp.dma_start(row[:], d["ctx"][:, L - 1, :]).then_inc(loaded, 16)
            sp.dma_start(cosr[:], d["cos_last"]).then_inc(loaded, 16)
            sp.dma_start(sinr[:], d["sin_last"]).then_inc(loaded, 16)
            sp.dma_start(g["ident"][:], d["ident"]).then_inc(loaded, 16)
            sp.wait_ge(split, 2)
            for r, part in enumerate((hi, lo, hi)):
                sp.dma_start(d["tail_rows"][:, r, :], part[:].bitcast(F32)).then_inc(stored, 16)
            sp.wait_ge(stored, 48)

        @block.vector
        def _(v):
            v.wait_ge(loaded, 64)
            v.tensor_tensor(turned[:], row[:], cosr[:], ALU.mult).then_inc(rotated, 1)
            v.tensor_tensor(t2[:, 0:64], row[:, 64:128], sinr[:, 0:64], ALU.mult).then_inc(rotated, 1)
            v.tensor_tensor(t2[:, 64:128], row[:, 0:64], sinr[:, 64:128], ALU.mult).then_inc(rotated, 1)
            v.wait_ge(rotated, 3)
            v.tensor_tensor(turned[:], turned[:], t2[:], ALU.add).then_inc(rotated, 1)
            v.wait_ge(rotated, 4)
            v.tensor_copy(hi[:], turned[:]).then_inc(split, 1)
            v.wait_ge(split, 1)
            v.tensor_tensor(lo[:], turned[:], hi[:].bitcast(F32), ALU.subtract).then_inc(split, 1)
            v.wait_ge(turned_T, 1)
            for c in range(2):
                v.tensor_copy(g["tailT_hi"][:, :, c], ps[:, 0, 0:B]).then_inc(split, 1)
            v.wait_ge(split, 4)
            for c in range(2):
                v.tensor_tensor(g["tailT_lo"][:, :, c], ps[:, 0, 0:B], g["tailT_hi"][:, :, 0].bitcast(F32),
                                ALU.subtract).then_inc(split, 1)

        @block.tensor
        def _(pe):
            pe.wait_ge(rotated, 4)
            pe.transpose(ps[:, 0, 0:B], turned[:], g["ident"][0:B, 0:B]).then_inc(turned_T, 1)


def phase_norm(nc, d, g, tag, load_x, affine):
    x, psum, ident = g["x"], g["psum"], g["ident"]
    xT_hi, xT_lo = g["xT_hi"], g["xT_lo"]
    rounds = 2 if affine else 1
    with ExitStack() as ctx:
        n = Names(nc, ctx, tag)
        stats = n.sb("stats", [P, TT, rounds, 6])
        mv = n.sb("mv", [P, TT, rounds, 2])
        var = n.sb("var", [P, TT, rounds])
        rstd = n.sb("rstd", [P, TT, rounds])
        power = n.sb("power", [P, TT])
        xn = n.sb("xn", [P, TT, D])
        if affine:
            wb = n.sb("wb", [P, 2, DC])
            tmp = n.sb("tmp", [P, 2, DC, P])
        loaded = [n.sem(f"loaded{t}") for t in range(TT if load_x else 0)]
        const_loaded, power_set = n.sem("const_loaded"), n.sem("power_set")
        stat_done, var_done, rstd_done = n.sem("stat_done"), n.sem("var_done"), n.sem("rstd_done")
        normed, x_added, transposed = n.sem("normed"), n.sem("x_added"), n.sem("transposed")
        scaled, hi_done, lo_done, aggr = n.sem("scaled"), n.sem("hi_done"), n.sem("lo_done"), n.sem("aggr")
        block = ctx.enter_context(nc.Block())

        @block.sync
        def _(sp):
            if load_x:
                for t in range(TT):
                    sp.dma_start(x[:, t, :], d["x"][t * P:(t + 1) * P, :]).then_inc(loaded[t], 16)
            if affine:
                sp.dma_start(wb[:], d["ln_wb"]).then_inc(const_loaded, 16)

        @block.gpsimd
        def _(pool):
            pool.memset(power[:], -0.5).then_inc(power_set, 1)
            pool.wait_ge(power_set, 1)
            for r in range(rounds):
                pool.wait_ge(var_done, r + 1)
                pool.tensor_tensor(rstd[:, :, r], var[:, :, r], power[:], ALU.pow).then_inc(rstd_done, 1)

        @block.vector
        def _(v):
            for r in range(rounds):
                src = xn if r else x
                for t in range(TT):
                    if load_x:
                        v.wait_ge(loaded[t], 16)
                    if r:
                        v.wait_ge(normed, t + 1)
                    v.bn_stats(stats[:, t, r, :], src[:, t, :]).then_inc(stat_done, 1)
                    if r:
                        v.tensor_tensor(x[:, t, :], x[:, t, :], xn[:, t, :], ALU.add).then_inc(x_added, 1)
                for t in range(TT):
                    v.wait_ge(stat_done, r * TT + t + 1)
                    v.bn_aggr(mv[:, t, r, :], stats[:, t, r, :]).then_inc(aggr, 1)
                v.wait_ge(aggr, (r + 1) * TT)
                v.tensor_scalar(var[:, :, r], mv[:, :, r, 1], EPS, None, ALU.add).then_inc(var_done, 1)
                v.wait_ge(rstd_done, r + 1)
                for t in range(TT):
                    if r:
                        v.wait_ge(x_added, t + 1)
                    v.tensor_scalar(xn[:, t, :], src[:, t, :], mv[:, t, r, 0:1], rstd[:, t, r:r + 1],
                                    ALU.subtract, ALU.mult).then_inc(normed, 1)
            for t in range(TT):
                bank = psum[:, t % 2, :].rearrange("p (c k) -> p c k", c=DC)
                if affine:
                    v.wait_ge(transposed, t + 1)
                    if t == 0:
                        v.wait_ge(const_loaded, 16)
                    if t >= 2:
                        v.wait_ge(hi_done, t - 1)
                        v.wait_ge(lo_done, t - 1)
                    for c in range(DC):
                        v.tensor_scalar(tmp[:, t % 2, c, :], bank[:, c, :], wb[:, 0, c:c + 1], wb[:, 1, c:c + 1],
                                        ALU.mult, ALU.add).then_inc(scaled, 1)
                    v.wait_ge(scaled, DC * (t + 1))
                    bank = tmp[:, t % 2, :, :]
                v.wait_ge(hi_done, t + 1)
                v.tensor_tensor(xT_lo[:, :, t * P:(t + 1) * P], bank,
                                xT_hi[:, :, t * P:(t + 1) * P].bitcast(F32), ALU.subtract).then_inc(lo_done, 1)

        @block.tensor
        def _(pe):
            for t in range(TT):
                pe.wait_ge(normed, (rounds - 1) * TT + t + 1)
                if t >= 2:
                    pe.wait_ge(lo_done, t - 1)
                for c in range(DC):
                    m = pe.transpose(psum[:, t % 2, c * P:(c + 1) * P], xn[:, t, c * P:(c + 1) * P], ident[:])
                m.then_inc(transposed, 1)

        @block.scalar
        def _(act):
            for t in range(TT):
                if affine:
                    act.wait_ge(scaled, DC * (t + 1))
                    src = tmp[:, t % 2, :, :]
                else:
                    act.wait_ge(transposed, t + 1)
                    src = psum[:, t % 2, :].rearrange("p (c k) -> p c k", c=DC)
                act.activation(xT_hi[:, :, t * P:(t + 1) * P], src, ACT.Copy).then_inc(hi_done, 1)


def phase_heads(nc, d, g, q, G_hi, G_lo):
    psum, xT_hi, xT_lo = g["psum"], g["xT_hi"], g["xT_lo"]
    M1, M2, CB, GB, QB = 0, 1, 2, 3, 4
    with ExitStack() as ctx:
        n = Names(nc, ctx, "heads")
        wq = n.sb("wq", [P, 2, D])
        kcqT = n.sb("kcqT", [P, 2, QC, P])
        wqrT = n.sb("wqrT", [R, 2, CQ])
        wkrT = n.sb("wkrT", [R, 2, P])
        kckv = n.sb("kckv", [P, 2, P])
        woT = n.sb("woT", [P, 2, D])
        m1 = n.sb("m1", [P, QC, P])
        m2 = n.sb("m2", [P, P])
        C_hi = n.sb("C_hi", [P, 2, DC, P], F32R)
        C_lo = n.sb("C_lo", [P, 2, DC, P], F32R)
        loaded = [n.sem(f"loaded{p}") for p in range(2)]
        m1_ready, m1_kept, m2_ready, m2_kept = (n.sem(x) for x in ("m1_ready", "m1_kept", "m2_ready", "m2_kept"))
        c_ready, c_hi_kept, c_kept = (n.sem(x) for x in ("c_ready", "c_hi_kept", "c_kept"))
        g_ready, g_hi_kept, g_kept = (n.sem(x) for x in ("g_ready", "g_hi_kept", "g_kept"))
        q_ready, q_kept = n.sem("q_ready"), n.sem("q_kept")
        block = ctx.enter_context(nc.Block())

        @block.sync
        def _(sp):
            def load(h, p):
                wait(sp, g_ready, h - 1)
                rows = bass.ds(h * P, P)
                for dst, src in ((wkrT[:, p, :], d["wkrT"][h]), (wqrT[:, p, :], d["wqrT"][h]),
                                 (kcqT[:, p, :, :], d["kcqT"][h].rearrange("(c p) k -> p c k", p=P)),
                                 (wq[:, p, :], d["wq"][rows, :]), (kckv[:, p, :], d["kckv"][h]),
                                 (woT[:, p, :], d["woT"][rows, :])):
                    sp.dma_start(dst, src).then_inc(loaded[p], 16)
            load(0, 0)
            load(1, 1)
            with sp.Fori(1, H // 2) as i:
                for p in range(2):
                    load(2 * i + p, p)

        def fold_m1(pe, h, p, k):
            pe.wait_ge(loaded[p], 96 * (k + 1))
            wait(pe, m1_kept, h)
            for c in range(QC):
                m = pe.matmul(psum[:, M1, c * P:(c + 1) * P], wqrT[:, p, c * P:(c + 1) * P], wkrT[:, p, :],
                              start=True, stop=True)
            m.then_inc(m1_ready, 1)

        def fold_m2(pe, h, p):
            pe.wait_ge(m1_kept, h + 1)
            for c in range(QC):
                m = pe.matmul(psum[:, M2, 0:P], kcqT[:, p, c, :], m1[:, c, :], start=(c == 0), stop=(c == QC - 1))
            m.then_inc(m2_ready, 1)

        def fold_cg(pe, h, p):
            pe.wait_ge(m2_kept, h + 1)
            wait(pe, c_kept, h)
            wait(pe, g_kept, h)
            for c in range(DC):
                m = pe.matmul(psum[:, CB, c * P:(c + 1) * P], wq[:, p, c * P:(c + 1) * P], m2[:], start=True, stop=True)
            m.then_inc(c_ready, 1)
            pe.matmul(psum[:, GB, :], kckv[:, p, :], woT[:, p, :], start=True, stop=True).then_inc(g_ready, 1)

        def project(pe, h, p, half):
            pe.wait_ge(c_kept, h + 1)
            wait(pe, q_kept, 2 * h + half - 1)
            for c in range(DC):
                cols = slice(half * HALF, (half + 1) * HALF)
                m = passes(pe, psum[:, QB + half, :], C_hi[:, p, c, :], C_lo[:, p, c, :],
                           xT_hi[:, c, cols], xT_lo[:, c, cols], c == 0, c == DC - 1)
            m.then_inc(q_ready, 1)

        @block.tensor
        def _(pe):
            def step(h, p, k_next, fold_next):
                if fold_next:
                    fold_m1(pe, h + 1, 1 - p, k_next)
                project(pe, h, p, 0)
                if fold_next:
                    fold_m2(pe, h + 1, 1 - p)
                project(pe, h, p, 1)
                if fold_next:
                    fold_cg(pe, h + 1, 1 - p)
            fold_m1(pe, 0, 0, 0)
            fold_m2(pe, 0, 0)
            fold_cg(pe, 0, 0)
            step(0, 0, 0, True)
            step(1, 1, 1, True)
            with pe.Fori(1, H // 2 - 1) as i:
                step(2 * i, 0, i, True)
                step(2 * i + 1, 1, i + 1, True)
            step(H - 2, 0, H // 2 - 1, True)
            step(H - 1, 1, 0, False)

        @block.scalar
        def _(act):
            def step(h, p):
                act.wait_ge(m1_ready, h + 1)
                wait(act, m2_ready, h)
                act.activation(m1[:], psum[:, M1, 0:CQ].rearrange("p (c k) -> p c k", c=QC), ACT.Copy).then_inc(m1_kept, 1)
                act.wait_ge(c_ready, h + 1)
                wait(act, q_ready, 2 * (h - 1))
                act.activation(C_hi[:, p, :, :], psum[:, CB, :].rearrange("p (c k) -> p c k", c=DC),
                               ACT.Copy).then_inc(c_hi_kept, 1)
            step(0, 0)
            step(1, 1)
            with act.Fori(1, H // 2) as i:
                step(2 * i, 0)
                step(2 * i + 1, 1)

        @block.vector
        def _(v):
            def keep_m2(h):
                v.wait_ge(m2_ready, h + 1)
                wait(v, c_ready, h)
                v.tensor_copy(m2[:], psum[:, M2, 0:P]).then_inc(m2_kept, 1)

            def keep_q(h, half):
                v.wait_ge(q_ready, 2 * h + half + 1)
                nb = HALF // S
                v.tensor_copy(q[:, half * nb:(half + 1) * nb, bass.ds(h * S, S)],
                              psum[:, QB + half, :].rearrange("p (b s) -> p b s", s=S)).then_inc(q_kept, 1)

            def step(h, p, fold_next):
                keep_q(h, 0)
                if fold_next:
                    keep_m2(h + 1)
                keep_q(h, 1)
                if fold_next:
                    split_cg(h + 1, 1 - p)

            def split_cg(h, p):
                v.wait_ge(c_hi_kept, h + 1)
                v.tensor_tensor(C_lo[:, p, :, :], psum[:, CB, :].rearrange("p (c k) -> p c k", c=DC),
                                C_hi[:, p, :, :].bitcast(F32), ALU.subtract).then_inc(c_kept, 1)
                v.wait_ge(g_ready, h + 1)
                gcols = bass.ds(h * D, D)
                v.tensor_copy(G_hi[:, gcols], psum[:, GB, :]).then_inc(g_hi_kept, 1)
                v.wait_ge(g_hi_kept, h + 1)
                v.tensor_tensor(G_lo[:, gcols], psum[:, GB, :], G_hi[:, gcols].bitcast(F32),
                                ALU.subtract).then_inc(g_kept, 1)
            keep_m2(0)
            split_cg(0, 0)
            step(0, 0, True)
            step(1, 1, True)
            with v.Fori(1, H // 2 - 1) as i:
                step(2 * i, 0, True)
                step(2 * i + 1, 1, True)
            step(H - 2, 0, True)
            step(H - 1, 1, False)


def phase_attention(nc, d, g, q, G_hi, G_lo):
    psum, x, ident = g["psum"], g["x"], g["ident"]
    SC, PT0, CT, KT = 0, 4, 6, 7
    LP = L + 1
    NJ = HS // P
    KVB = 4
    with ExitStack() as ctx:
        n = Names(nc, ctx, "att")
        cosb, sinb = n.sb("cosb", [P, 2, P]), n.sb("sinb", [P, 2, P])
        raw = n.sb("raw", [P, 2, P])
        turn = n.sb("turn", [P, 2, P])
        kvr = n.sb("kvr", [P, 2, 2, P])
        kv_hi, kv_lo = n.sb("kv_hi", [P, KVB, 2, P], F32R), n.sb("kv_lo", [P, KVB, 2, P], F32R)
        tail = n.sb("tail", [3, KVB, P], F32R)
        kvT_hi, kvT_lo = n.sb("kvT_hi", [P, 2, LP], F32R), n.sb("kvT_lo", [P, 2, LP], F32R)
        q_hi, q_lo = n.sb("q_hi", [P, 2, HS], F32R), n.sb("q_lo", [P, 2, HS], F32R)
        pr = n.sb("pr", [P, 2, NJ, LP + 2])
        prr = pr[:].bitcast(F32R)
        low = n.sb("low", [P, 2, NJ])
        total, scale = n.sb("total", [P, 2, NJ]), n.sb("scale", [P, 2, NJ])
        pT_hi, pT_lo = n.sb("pT_hi", [P, 2, HS], F32R), n.sb("pT_lo", [P, 2, HS], F32R)
        pT_tail = n.sb("pT_tail", [3, HS], F32R)
        cT_hi, cT_lo = n.sb("cT_hi", [P, H, P], F32R), n.sb("cT_lo", [P, H, P], F32R)
        S_ = n.sem
        tables, raw_in, rot, rot_mid, tail_in = S_("tables"), S_("raw_in"), S_("rot"), S_("rot_mid"), [S_(f"tail_in{i}") for i in range(KVB)]
        rot_a, tail_cols = S_("rot_a"), S_("tail_cols")
        kvT_ready, kvT_hi_ok, kvT_ok, kv_hi_ok, kv_ok = (S_(x) for x in ("kvT_ready", "kvT_hi_ok", "kvT_ok", "kv_hi_ok", "kv_ok"))
        q_hi_ok, q_ok = S_("q_hi_ok"), S_("q_ok")
        sc_ready, low_ok, exp_ok, inv_ok, pr_ok, p_split, p_tail = (S_(x) for x in (
            "sc_ready", "low_ok", "exp_ok", "inv_ok", "pr_ok", "p_split", "p_tail"))
        pt_ready, pt_hi_ok, pt_ok, ptail_ok = (S_(x) for x in ("pt_ready", "pt_hi_ok", "pt_ok", "ptail_ok"))
        c_ready, c_hi_ok, c_ok, o_ready, o_ok = (S_(x) for x in ("c_ready", "c_hi_ok", "c_ok", "o_ready", "o_ok"))
        block = ctx.enter_context(nc.Block())

        def run(e, step):
            for u in range(BPT):
                step(u, u)
            with e.Fori(1, B // BPT - 1) as i:
                for u in range(BPT):
                    step(BPT * i + u, u)
            for s in range(B - BPT, B + 3):
                step(s, s % BPT)

        def inside(s, lag):
            return not isinstance(s, int) or 0 <= s - lag < B

        @block.sync
        def _(sp):
            sp.dma_start(cosb[:], d["cos_main"]).then_inc(tables, 16)
            sp.dma_start(sinb[:], d["sin_main"]).then_inc(tables, 16)

            def load(b, u):
                wait(sp, rot_a, b)
                sp.dma_start(raw[:], d["ctx"][b, 0:2 * P, :].rearrange("(c p) k -> p c k", p=P)).then_inc(raw_in, 16)

            def load_tail(b, u):
                wait(sp, c_ready, b - KVB + 1)
                sp.dma_start(tail[:, u, :].bitcast(F32), d["tail_rows"][b]).then_inc(tail_in[u], 16)
            for b in range(2 * BPT):
                load(b, b % BPT)
                if b >= 2:
                    load_tail(b - 2, (b - 2) % BPT)
            with sp.Fori(2, B // BPT) as i:
                for u in range(BPT):
                    load(BPT * i + u, u)
                    load_tail(BPT * i + u - 2, (u - 2) % BPT)
            load_tail(B - 2, 2)
            load_tail(B - 1, 3)

        @block.gpsimd
        def _(pool):
            def rotate(b, u):
                p = u % 2
                pool.wait_ge(raw_in, 16 * (b + 1))
                wait(pool, kvT_ready, b - 1)
                wait(pool, kv_ok, b - 1)
                wait(pool, rot, b)
                pool.tensor_tensor(kvr[:, p, :, :], raw[:], cosb[:], ALU.mult).then_inc(rot_mid, 1)
                pool.tensor_tensor(turn[:, :, 0:64], raw[:, :, 64:128], sinb[:, :, 0:64], ALU.mult).then_inc(rot_mid, 1)
                pool.tensor_tensor(turn[:, :, 64:128], raw[:, :, 0:64], sinb[:, :, 64:128], ALU.mult).then_inc(rot_a, 1)
                pool.wait_ge(rot_mid, 2 * (b + 1))
                pool.wait_ge(rot_a, b + 1)
                pool.tensor_tensor(kvr[:, p, :, :], kvr[:, p, :, :], turn[:], ALU.add).then_inc(rot, 1)

            def low_parts(b, u):
                p = u % 2
                wait(pool, sc_ready, NJ * (b - 1))
                pool.tensor_copy(kvT_hi[:, p, 2 * P:LP], g["tailT_hi"][:, bass.ds(b, 1), :]).then_inc(tail_cols, 1)
                pool.tensor_copy(kvT_lo[:, p, 2 * P:LP], g["tailT_lo"][:, bass.ds(b, 1), :]).then_inc(tail_cols, 1)
                pool.wait_ge(q_hi_ok, b + 1)
                pool.tensor_tensor(q_lo[:, p, :], q[:, b, :], q_hi[:, p, :].bitcast(F32), ALU.subtract).then_inc(q_ok, 1)
                pool.wait_ge(kv_hi_ok, b + 1)
                pool.tensor_tensor(kv_lo[:, u, :, :], kvr[:, p, :, :], kv_hi[:, u, :, :].bitcast(F32),
                                   ALU.subtract).then_inc(kv_ok, 1)

            def step(s, u):
                if inside(s, -3):
                    rotate(s + 3, (u + 3) % BPT)
                if inside(s, -2):
                    low_parts(s + 2, (u + 2) % BPT)
            pool.wait_ge(tables, 32)
            rotate(0, 0)
            rotate(1, 1)
            low_parts(0, 0)
            rotate(2, 2)
            low_parts(1, 1)
            run(pool, step)

        @block.tensor
        def _(pe):
            def transpose_context(b, u):
                pe.wait_ge(rot, b + 1)
                wait(pe, kvT_ok, b)
                wait(pe, ptail_ok, b - 3)
                for c in range(2):
                    m = pe.transpose(psum[:, KT, c * P:(c + 1) * P], kvr[:, u % 2, c, :], ident[:])
                m.then_inc(kvT_ready, 1)

            def scores(b, u):
                p = u % 2
                pe.wait_ge(q_ok, b + 1)
                pe.wait_ge(kvT_ok, b + 1)
                pe.wait_ge(tail_cols, 2 * (b + 1))
                for j in range(NJ):
                    wait(pe, exp_ok, NJ * (b - 1) + j + 1)
                    rows = slice(j * P, (j + 1) * P)
                    passes(pe, psum[:, SC + j, 0:LP], q_hi[:, p, rows], q_lo[:, p, rows],
                           kvT_hi[:, p, :], kvT_lo[:, p, :], True, True).then_inc(sc_ready, 1)

            def transpose_probs(b, u):
                p = u % 2
                wait(pe, pt_ok, 2 * b)
                wait(pe, ptail_ok, b)
                pe.wait_ge(kvT_ok, b + 4 if not isinstance(b, int) else min(b + 4, B))
                pe.wait_ge(p_tail, b + 1)
                for j in range(NJ):
                    for c in range(2):
                        pe.transpose(psum[:, PT0 + c, j * P:(j + 1) * P], pr[:, p, j, c * P:(c + 1) * P], ident[:])
                    m = pe.transpose(psum[0:3, KT, j * P:(j + 1) * P], pr[:, p, j, 2 * P:2 * P + 3], ident[:])
                m.then_inc(pt_ready, 1)

            def context(b, u):
                pe.wait_ge(kv_ok, b + 1)
                pe.wait_ge(tail_in[u], 16 * (b // BPT + 1) if isinstance(b, int) else 4 * (b - u) + 16)
                pe.wait_ge(pt_ok, 2 * (b + 1))
                pe.wait_ge(ptail_ok, b + 1)
                wait(pe, c_ok, b)
                for c in range(2):
                    passes(pe, psum[:, CT, :], kv_hi[:, u, c, :], kv_lo[:, u, c, :], pT_hi[:, c, :], pT_lo[:, c, :],
                           c == 0, False)
                pe.matmul(psum[:, CT, :], tail[:, u, :], pT_tail[:], start=False, stop=True).then_inc(c_ready, 1)

            def output(t):
                pe.wait_ge(c_ok, BPT * (t + 1))
                pe.wait_ge(pt_ok, 2 * (BPT * (t + 1) + 1) if not isinstance(t, int) else min(2 * (BPT * (t + 1) + 1), 2 * B))
                for h in range(H):
                    m = passes(pe, psum[:, PT0, :], cT_hi[:, h, :], cT_lo[:, h, :], G_hi[:, h * D:(h + 1) * D],
                               G_lo[:, h * D:(h + 1) * D], h == 0, h == H - 1)
                m.then_inc(o_ready, 1)

            def step(s, u):
                if inside(s, 0):
                    scores(s, u)
                if inside(s, -2):
                    transpose_context(s + 2, (u + 2) % BPT)
                if u == 2 and (not isinstance(s, int) or s >= BPT):
                    t = s // BPT - 1 if isinstance(s, int) else (s - u) // BPT - 1
                    output(t)
                if inside(s, 2):
                    context(s - 2, (u - 2) % BPT)
                if inside(s, 1):
                    if u == 2 and (not isinstance(s, int) or s >= BPT):
                        pe.wait_ge(o_ok, s // BPT if isinstance(s, int) else (s - u) // BPT)
                    transpose_probs(s - 1, (u - 1) % BPT)
            transpose_context(0, 0)
            transpose_context(1, 1)
            run(pe, step)

        @block.scalar
        def _(act):
            def prepare(b, u):
                p = u % 2
                act.wait_ge(kvT_ready, b + 1)
                wait(act, sc_ready, NJ * (b - 1))
                act.activation(kvT_hi[:, p, 0:2 * P], psum[:, KT, 0:2 * P], ACT.Copy).then_inc(kvT_hi_ok, 1)
                act.activation(q_hi[:, p, :], q[:, b, :], ACT.Copy).then_inc(q_hi_ok, 1)

            def context_rows_hi(b, u):
                act.wait_ge(rot, b + 1)
                wait(act, c_ready, b - KVB + 1)
                act.activation(kv_hi[:, u, :, :], kvr[:, u % 2, :, :], ACT.Copy).then_inc(kv_hi_ok, 1)

            def exponentials(b, u):
                p = u % 2
                for j in range(NJ):
                    act.wait_ge(low_ok, NJ * b + j + 1)
                    if j == 0:
                        wait(act, pt_ready, b - 1)
                    act.activation(pr[:, p, j, 0:L], psum[:, SC + j, 0:L], ACT.Exp, bias=low[:, p, j:j + 1],
                                   accum_out=total[:, p, j:j + 1]).then_inc(exp_ok, 1)

            def probs_hi(b, u):
                act.wait_ge(pt_ready, b + 1)
                wait(act, c_ready, b)
                for c in range(2):
                    act.activation(pT_hi[:, c, :], psum[:, PT0 + c, :], ACT.Copy).then_inc(pt_hi_ok, 1)
                act.activation(pT_tail[:], psum[0:3, KT, :], ACT.Copy).then_inc(ptail_ok, 1)

            def context_hi(b, u):
                act.wait_ge(c_ready, b + 1)
                if u == 0:
                    wait(act, o_ready, b // BPT)
                act.activation(cT_hi[:, :, u * S:(u + 1) * S], psum[:, CT, :].rearrange("p (h s) -> p h s", s=S),
                               ACT.Copy).then_inc(c_hi_ok, 1)

            def step(s, u):
                if inside(s, 2):
                    probs_hi(s - 2, (u - 2) % BPT)
                if inside(s, 0):
                    exponentials(s, u)
                if inside(s, -2):
                    prepare(s + 2, (u + 2) % BPT)
                if inside(s, 2):
                    context_hi(s - 2, (u - 2) % BPT)
                if inside(s, -2):
                    context_rows_hi(s + 2, (u + 2) % BPT)
            for b in range(2):
                prepare(b, b)
                context_rows_hi(b, b)
            run(act, step)

        @block.vector
        def _(v):
            def prepare(b, u):
                p = u % 2
                v.wait_ge(kvT_hi_ok, b + 1)
                v.tensor_tensor(kvT_lo[:, p, 0:2 * P], psum[:, KT, 0:2 * P], kvT_hi[:, p, 0:2 * P].bitcast(F32),
                                ALU.subtract).then_inc(kvT_ok, 1)

            def maxima(b, u):
                p = u % 2
                for j in range(NJ):
                    v.wait_ge(sc_ready, NJ * b + j + 1)
                    v.tensor_reduce(low[:, p, j:j + 1], psum[:, SC + j, 0:L], AX_X, ALU.max, negate=True).then_inc(low_ok, 1)

            def normalise(b, u):
                p = u % 2
                v.wait_ge(exp_ok, NJ * (b + 1))
                v.reciprocal(scale[:, p, :], total[:, p, :]).then_inc(inv_ok, 1)
                v.wait_ge(inv_ok, b + 1)
                for j in range(NJ):
                    v.tensor_scalar(pr[:, p, j, 0:L], pr[:, p, j, 0:L], scale[:, p, j:j + 1], None,
                                    ALU.mult).then_inc(pr_ok, 1)
                v.wait_ge(pr_ok, NJ * (b + 1))
                v.tensor_copy(prr[:, p, :, 2 * P + 1:2 * P + 2], pr[:, p, :, 2 * P:2 * P + 1]).then_inc(p_split, 1)
                v.wait_ge(p_split, 2 * b + 1)
                v.tensor_tensor(pr[:, p, :, 2 * P + 2:2 * P + 3], pr[:, p, :, 2 * P:2 * P + 1],
                                pr[:, p, :, 2 * P + 1:2 * P + 2], ALU.subtract).then_inc(p_split, 1)
                v.wait_ge(p_split, 2 * b + 2)
                v.tensor_copy(pr[:, p, :, 2 * P:2 * P + 1], pr[:, p, :, 2 * P + 1:2 * P + 2]).then_inc(p_tail, 1)

            def probs_lo(b, u):
                for c in range(2):
                    v.wait_ge(pt_hi_ok, 2 * b + c + 1)
                    v.tensor_tensor(pT_lo[:, c, :], psum[:, PT0 + c, :], pT_hi[:, c, :].bitcast(F32),
                                    ALU.subtract).then_inc(pt_ok, 1)

            def context_lo(b, u):
                v.wait_ge(c_hi_ok, b + 1)
                cols = slice(u * S, (u + 1) * S)
                v.tensor_tensor(cT_lo[:, :, cols], psum[:, CT, :].rearrange("p (h s) -> p h s", s=S),
                                cT_hi[:, :, cols].bitcast(F32), ALU.subtract).then_inc(c_ok, 1)

            def step(s, u):
                if inside(s, 2):
                    probs_lo(s - 2, (u - 2) % BPT)
                if inside(s, 0):
                    maxima(s, u)
                if inside(s, -2):
                    prepare(s + 2, (u + 2) % BPT)
                if inside(s, 0):
                    normalise(s, u)
                if u == 2 and (not isinstance(s, int) or s >= BPT):
                    t = s // BPT - 1 if isinstance(s, int) else (s - u) // BPT - 1
                    v.wait_ge(o_ready, t + 1)
                    v.tensor_tensor(x[:, bass.ds(t, 1), :], x[:, bass.ds(t, 1), :],
                                    psum[:, PT0:PT0 + 1, :], ALU.add).then_inc(o_ok, 1)
                if inside(s, 2):
                    context_lo(s - 2, (u - 2) % BPT)
            prepare(0, 0)
            prepare(1, 1)
            run(v, step)


def phase_store(nc, d, g):
    with ExitStack() as ctx:
        n = Names(nc, ctx, "store")
        stored = n.sem("stored")
        block = ctx.enter_context(nc.Block())

        @block.sync
        def _(sp):
            sp.dma_start(d["out"].rearrange("(t p) d -> p t d", p=P), g["x"][:]).then_inc(stored, 16)
            sp.wait_ge(stored, 16)


DI, HD, NST, NH, NX = 1024, 64, 64, 16, 4
REP = NH // NX
ZC = DI // P
FEATS = 2 * ZC + 4
Z0, C0, X0, B0 = 0, ZC, 2 * ZC, 2 * ZC + 2


def phase_project(nc, d, g, feat, dc, cumT_hi, cumT_lo):
    psum, xT_hi, xT_lo, ident = g["psum"], g["xT_hi"], g["xT_lo"], g["ident"]
    DT, TR = 4, 6
    with ExitStack() as ctx:
        n = Names(nc, ctx, "proj")
        raw = n.sb("raw", [P, 2, DC, P])
        w_hi, w_lo = n.sb("w_hi", [P, 2, DC, P], F32R), n.sb("w_lo", [P, 2, DC, P], F32R)
        wdt = n.sb("wdt", [P, DC, NH])
        wdt_hi, wdt_lo = n.sb("wdt_hi", [P, DC, NH], F32R), n.sb("wdt_lo", [P, DC, NH], F32R)
        head = n.sb("head", [NH, 2])
        negA = n.sb("negA", [NH, 1])
        starts = n.sb("starts", [NH, TOK])
        b2 = n.sb("b2", [P, D])
        pre, mag, u, w1, wm, dt = (n.sb(x, [NH, TOK]) for x in ("pre", "mag", "u", "w1", "wm", "dt"))
        loaded, w_hi_ok, w_ok, f_ready, f_kept = [n.sem("loaded0"), n.sem("loaded1")], n.sem("w_hi_ok"), n.sem("w_ok"), n.sem("f_ready"), n.sem("f_kept")
        small, dt_w, dt_ready, b2_in, x_plus = n.sem("small"), n.sem("dt_w"), n.sem("dt_ready"), n.sem("b2_in"), n.sem("x_plus")
        chain, a_chain, tr_ready, tr_kept = n.sem("chain"), n.sem("a_chain"), n.sem("tr_ready"), n.sem("tr_kept")
        block = ctx.enter_context(nc.Block())

        @block.sync
        def _(sp):
            def load(k, p):
                wait(sp, w_ok, k - 1)
                sp.dma_start(raw[:, p, :, :], d["w_feat"][k]).then_inc(loaded[p], 16)
            load(0, 0)
            load(1, 1)
            for dst, src in ((wdt[:], d["w_dt"]), (head[:], d["head"]), (starts[:], d["starts"])):
                sp.dma_start(dst, src).then_inc(small, 16)
            sp.dma_start(b2[:], d["fc2_b"]).then_inc(b2_in, 16)
            with sp.Fori(1, FEATS // 2) as i:
                load(2 * i, 0)
                load(2 * i + 1, 1)

        @block.gpsimd
        def _(pool):
            pool.wait_ge(b2_in, 16)
            for t in range(TT):
                pool.tensor_tensor(g["x"][:, t, :], g["x"][:, t, :], b2[:], ALU.add).then_inc(x_plus, 1)

        @block.tensor
        def _(pe):
            pe.wait_ge(dt_w, 2)
            for half in range(NHALF):
                cols = slice(half * HALF, (half + 1) * HALF)
                for c in range(DC):
                    m = passes(pe, psum[0:NH, DT + half, :], wdt_hi[:, c, :], wdt_lo[:, c, :],
                               xT_hi[:, c, cols], xT_lo[:, c, cols], c == 0, c == DC - 1)
                m.then_inc(dt_ready, 1)

            def chunk(k, p):
                pe.wait_ge(w_ok, k + 1)
                for half in range(NHALF):
                    bank = 2 * p + half
                    wait(pe, f_kept, 2 * (k - 2) + half + 1)
                    cols = slice(half * HALF, (half + 1) * HALF)
                    for c in range(DC):
                        m = passes(pe, psum[:, bank, :], w_hi[:, p, c, :], w_lo[:, p, c, :],
                                   xT_hi[:, c, cols], xT_lo[:, c, cols], c == 0, c == DC - 1)
                    m.then_inc(f_ready, 1)
            chunk(0, 0)
            chunk(1, 1)
            with pe.Fori(1, FEATS // 2) as i:
                chunk(2 * i, 0)
                chunk(2 * i + 1, 1)
            pe.wait_ge(chain, DT_STEPS)
            for k, src in enumerate((dt, mag)):
                for t in range(TT):
                    m = pe.transpose(psum[:, TR + k, t * NH:(t + 1) * NH], src[:, t * P:(t + 1) * P], ident[0:NH, 0:NH])
                m.then_inc(tr_ready, 1)

        @block.scalar
        def _(act):
            def split(k, p):
                act.wait_ge(loaded[p], 16 * (k // 2 + 1) if isinstance(k, int) else 8 * (k - p) + 16)
                wait(act, f_ready, 2 * (k - 1))
                act.activation(w_hi[:, p, :, :], raw[:, p, :, :], ACT.Copy).then_inc(w_hi_ok, 1)

            def keep_z(k, p):
                for half in range(NHALF):
                    act.wait_ge(f_ready, 2 * k + half + 1)
                    act.activation(feat[:, k, half * HALF:(half + 1) * HALF], psum[:, 2 * p + half, :],
                                   ACT.Silu).then_inc(f_kept, 1)

            def keep(k, p):
                for half in range(NHALF):
                    act.wait_ge(f_ready, 2 * k + half + 1)
                    act.activation(feat[:, bass.ds(k, 1), half * HALF:(half + 1) * HALF],
                                   psum[:, 2 * p + half:2 * p + half + 1, :], ACT.Copy).then_inc(f_kept, 1)
            act.wait_ge(small, 48)
            act.activation(negA[:], head[:, 1:2], ACT.Exp).then_inc(a_chain, 1)
            act.wait_ge(chain, 2)
            act.activation(u[:], mag[:], ACT.Exp, scale=-1.0).then_inc(a_chain, 1)
            act.wait_ge(chain, 3)
            act.activation(wm[:], w1[:], ACT.Ln).then_inc(a_chain, 1)
            split(0, 0)
            split(1, 1)
            for k in range(ZC):
                keep_z(k, k % 2)
                split(k + 2, k % 2)
            with act.Fori(ZC // 2, FEATS // 2 - 1) as i:
                for p in range(2):
                    keep(2 * i + p, p)
                    split(2 * i + p + 2, p)
            keep(FEATS - 2, 0)
            keep(FEATS - 1, 1)

        @block.vector
        def _(v):
            v.wait_ge(small, 48)
            v.tensor_copy(wdt_hi[:], wdt[:]).then_inc(dt_w, 1)
            v.wait_ge(dt_w, 1)
            v.tensor_tensor(wdt_lo[:], wdt[:], wdt_hi[:].bitcast(F32), ALU.subtract).then_inc(dt_w, 1)

            def split(k, p):
                v.wait_ge(w_hi_ok, k + 1)
                v.tensor_tensor(w_lo[:, p, :, :], raw[:, p, :, :], w_hi[:, p, :, :].bitcast(F32),
                                ALU.subtract).then_inc(w_ok, 1)
            steps = [0]

            def link(i):
                steps[0] += 1
                i.then_inc(chain, 1)
                v.wait_ge(chain, steps[0])
            v.wait_ge(dt_ready, 2)
            v.tensor_scalar(pre[:].rearrange("h (a n) -> h a n", a=NHALF), psum[0:NH, DT:DT + NHALF, :], head[:, 0:1], None,
                            ALU.add).then_inc(chain, 1)
            v.wait_ge(chain, 1)
            steps[0] = 1
            link(v.scalar_tensor_tensor(out=mag[:], in0=pre[:], scalar=-1.0, in1=pre[:], op0=ALU.mult, op1=ALU.max))
            v.wait_ge(a_chain, 2)
            link(v.tensor_scalar(w1[:], u[:], 1.0, None, ALU.add))
            link(v.tensor_scalar(mag[:], w1[:], -1.0, None, ALU.add))
            v.wait_ge(a_chain, 3)
            link(v.tensor_tensor(wm[:], wm[:], u[:], ALU.mult))
            link(v.tensor_scalar(w1[:], mag[:], 0.0, None, ALU.is_equal))
            link(v.tensor_tensor(mag[:], mag[:], w1[:], ALU.add))
            link(v.reciprocal(mag[:], mag[:]))
            link(v.tensor_tensor(wm[:], wm[:], mag[:], ALU.mult))
            link(v.tensor_tensor(w1[:], w1[:], u[:], ALU.mult))
            link(v.tensor_tensor(wm[:], wm[:], w1[:], ALU.add))
            link(v.scalar_tensor_tensor(out=dt[:], in0=pre[:], scalar=0.0, in1=wm[:], op0=ALU.max, op1=ALU.add))
            link(v.tensor_scalar(pre[:], dt[:], negA[:, 0:1], -1.0, ALU.mult, ALU.mult))
            link(v.tensor_tensor_scan(mag[:], starts[:], pre[:], 0.0, ALU.mult, ALU.add))
            assert steps[0] == DT_STEPS
            link(v.memset(cumT_hi[:].bitcast(F32), 0.0))
            link(v.memset(cumT_lo[:].bitcast(F32), 0.0))
            link(v.tensor_copy(cumT_hi[0:NH, :], mag[:]))
            link(v.tensor_tensor(cumT_lo[0:NH, :], mag[:], cumT_hi[0:NH, :].bitcast(F32), ALU.subtract))
            split(0, 0)
            split(1, 1)
            with v.Fori(1, FEATS // 2) as i:
                split(2 * i, 0)
                split(2 * i + 1, 1)
            for k in range(2):
                v.wait_ge(tr_ready, k + 1)
                v.tensor_copy(dc[:, :, k, :], psum[:, TR + k, 0:TT * NH].rearrange("p (t h) -> p t h", h=NH)).then_inc(tr_kept, 1)


DT_STEPS = 14


def phase_scan(nc, d, g, feat, dc, cumT_hi, cumT_lo):
    psum, ident, x = g["psum"], g["ident"], g["x"]
    CU, SB, YB, OB, MB = 0, 2, 4, 6, 7
    with ExitStack() as ctx:
        n = Names(nc, ctx, "scan")
        wo_raw = n.sb("wo_raw", [P, 2, D])
        wo_hi, wo_lo = n.sb("wo_hi", [P, ZC, D], F32R), n.sb("wo_lo", [P, ZC, D], F32R)
        nw, dcol = n.sb("nw", [P, ZC]), n.sb("dcol", [P, ZC])
        mask = n.sb("mask", [P, P])
        pick = n.sb("pick", [P, NH], F32R)
        ones = n.sb("ones", [P, 2])
        power, ms, rs = n.sb("power", [P, 1]), n.sb("ms", [P, 2]), n.sb("rs", [P, 2])
        C_hi, C_lo = n.sb("C_hi", [P, ZC, P], F32R), n.sb("C_lo", [P, ZC, P], F32R)
        B_hi, B_lo = n.sb("B_hi", [P, 2, P], F32R), n.sb("B_lo", [P, 2, P], F32R)
        xs, dcs = n.sb("xs", [P, 2, P]), n.sb("dcs", [P, 2, 2, NH])
        xt_hi, xt_lo = n.sb("xt_hi", [P, 2 * P], F32R), n.sb("xt_lo", [P, 2 * P], F32R)
        E = n.sb("E", [P, 2, REP, P])
        W_hi, W_lo = n.sb("W_hi", [P, 2, REP, P], F32R), n.sb("W_lo", [P, 2, REP, P], F32R)
        y = n.sb("y", [P, 2, REP, P])
        sq = n.sb("sq", [P, 2, REP, P])
        y_hi, y_lo = n.sb("y_hi", [P, ZC, P], F32R), n.sb("y_lo", [P, ZC, P], F32R)
        S_ = n.sem
        consts, wo_in, wo_hi_ok, wo_ok, set_up = S_("consts"), [S_("wo_in0"), S_("wo_in1")], S_("wo_hi_ok"), S_("wo_ok"), S_("set_up")
        pick_ok = S_("pick_ok")
        cb_hi_ok, cb_ok, xs_ok, dcs_ok, xt_ready, xt_hi_ok, xt_ok = (S_(k) for k in ("cb_hi_ok", "cb_ok", "xs_ok", "dcs_ok", "xt_ready", "xt_hi_ok", "xt_ok"))
        cu_ready, s_ready, dm_ok, e_ok, w_ok, whi_ok, wlo_ok = (S_(k) for k in ("cu_ready", "s_ready", "dm_ok", "e_ok", "w_ok", "whi_ok", "wlo_ok"))
        y_ready, yd_ok, yg_ok, sq_ok, yhi_ok, ylo_ok = (S_(k) for k in ("y_ready", "yd_ok", "yg_ok", "sq_ok", "yhi_ok", "ylo_ok"))
        ss_ready, ms_ok, rs_ok, o_ready, o_ok = (S_(k) for k in ("ss_ready", "ms_ok", "rs_ok", "o_ready", "o_ok"))
        block = ctx.enter_context(nc.Block())

        def tiles(e, tile):
            tile(0, 0)
            tile(1, 1)
            with e.Fori(1, TT // 2) as i:
                tile(2 * i, 0)
                tile(2 * i + 1, 1)

        @block.sync
        def _(sp):
            for dst, src in ((nw[:], d["norm_w"]), (dcol[:], d["d_skip"]), (mask[:], d["mask"])):
                sp.dma_start(dst, src).then_inc(consts, 16)
            for c in range(ZC):
                wait(sp, wo_ok, c - 1)
                sp.dma_start(wo_raw[:, c % 2, :], d["w_out"][c]).then_inc(wo_in[c % 2], 16)

        @block.gpsimd
        def _(pool):
            pool.memset(power[:], -0.5).then_inc(set_up, 1)
            pool.memset(ones[:], 1.0).then_inc(set_up, 1)
            pool.wait_ge(set_up, 2)

            def tile(t, p):
                wait(pool, xt_ready, t)
                wait(pool, yd_ok, 2 * t)
                pool.tensor_copy(xs[:], feat[:, X0:X0 + 2, bass.ds(t * P, P)]).then_inc(xs_ok, 1)
                pool.wait_ge(ms_ok, t + 1)
                wait(pool, o_ok, t - 1)
                pool.tensor_tensor(rs[:, p:p + 1], ms[:, p:p + 1], power[:], ALU.pow).then_inc(rs_ok, 1)
            tiles(pool, tile)

        @block.scalar
        def _(act):
            act.wait_ge(consts, 48)
            for c in range(ZC):
                act.wait_ge(wo_in[c % 2], 16 * (c // 2 + 1))
                act.activation(wo_hi[:, c, :], wo_raw[:, c % 2, :], ACT.Copy, scale=nw[:, c:c + 1]).then_inc(wo_hi_ok, 1)

            def tile(t, p):
                wait(act, s_ready, NX * t)
                act.activation(C_hi[:], feat[:, C0:C0 + ZC, bass.ds(t * P, P)], ACT.Copy).then_inc(cb_hi_ok, 1)
                act.activation(B_hi[:], feat[:, B0:B0 + 2, bass.ds(t * P, P)], ACT.Copy).then_inc(cb_hi_ok, 1)
                act.wait_ge(xt_ready, t + 1)
                wait(act, y_ready, NX * t)
                act.activation(xt_hi[:], psum[:, MB, 0:2 * P], ACT.Copy).then_inc(xt_hi_ok, 1)

                def exponential(k):
                    act.wait_ge(dm_ok, REP * (NX * t + k + 1))
                    act.activation(E[:, k % 2, :, :], E[:, k % 2, :, :], ACT.Exp).then_inc(e_ok, 1)

                def weights_hi(k):
                    act.wait_ge(w_ok, REP * (NX * t + k + 1))
                    wait(act, y_ready, NX * t + k - 1)
                    act.activation(W_hi[:, k % 2, :, :], E[:, k % 2, :, :], ACT.Copy).then_inc(whi_ok, 1)

                def gated(m):
                    act.wait_ge(yg_ok, 2 * t + m + 1)
                    wait(act, ss_ready, t)
                    act.activation(sq[:, m, :, :], y[:, m, :, :], ACT.Square).then_inc(sq_ok, 1)
                    wait(act, o_ready, t)
                    act.activation(y_hi[:, REP * m:REP * (m + 1), :], y[:, m, :, :], ACT.Copy).then_inc(yhi_ok, 1)
                exponential(0)
                exponential(1)
                weights_hi(0)
                weights_hi(1)
                exponential(2)
                exponential(3)
                gated(0)
                weights_hi(2)
                weights_hi(3)
                gated(1)
            tiles(act, tile)

        @block.vector
        def _(v):
            v.wait_ge(consts, 48)
            v.tensor_copy(pick[:], ident[:, 0:NH]).then_inc(pick_ok, 1)
            for c in range(ZC):
                v.wait_ge(wo_hi_ok, c + 1)
                v.scalar_tensor_tensor(out=wo_lo[:, c, :], in0=wo_raw[:, c % 2, :], scalar=nw[:, c:c + 1],
                                       in1=wo_hi[:, c, :].bitcast(F32), op0=ALU.mult, op1=ALU.subtract).then_inc(wo_ok, 1)

            def tile(t, p):
                v.wait_ge(w_ok, REP * NX * t) if not (isinstance(t, int) and t == 0) else None
                v.tensor_copy(dcs[:, p, :, :], dc[:, bass.ds(t, 1), :, :]).then_inc(dcs_ok, 1)
                v.wait_ge(cb_hi_ok, 2 * t + 1)
                v.tensor_tensor(C_lo[:], feat[:, C0:C0 + ZC, bass.ds(t * P, P)], C_hi[:].bitcast(F32), ALU.subtract).then_inc(cb_ok, 1)
                v.wait_ge(cb_hi_ok, 2 * t + 2)
                v.tensor_tensor(B_lo[:], feat[:, B0:B0 + 2, bass.ds(t * P, P)], B_hi[:].bitcast(F32), ALU.subtract).then_inc(cb_ok, 1)
                v.wait_ge(xt_hi_ok, t + 1)
                v.tensor_tensor(xt_lo[:], psum[:, MB, 0:2 * P], xt_hi[:].bitcast(F32), ALU.subtract).then_inc(xt_ok, 1)
                v.wait_ge(dcs_ok, t + 1)

                def head(k, j):
                    return k * REP + j

                def decay(k):
                    v.wait_ge(cu_ready, NX * t + k + 1)
                    wait(v, wlo_ok, NX * t + k - 1)
                    for j in range(REP):
                        h = head(k, j)
                        v.scalar_tensor_tensor(out=E[:, k % 2, j, :], in0=psum[:, CU + k % 2, j * P:(j + 1) * P],
                                               scalar=dcs[:, p, 1, h:h + 1], in1=mask[:], op0=ALU.subtract,
                                               op1=ALU.add).then_inc(dm_ok, 1)

                def weigh(k):
                    v.wait_ge(e_ok, NX * t + k + 1)
                    v.wait_ge(s_ready, NX * t + k + 1)
                    for j in range(REP):
                        h = head(k, j)
                        v.scalar_tensor_tensor(out=E[:, k % 2, j, :], in0=psum[:, SB + k % 2, j * P:(j + 1) * P],
                                               scalar=dcs[:, p, 0, h:h + 1], in1=E[:, k % 2, j, :], op0=ALU.mult,
                                               op1=ALU.mult).then_inc(w_ok, 1)

                def weights_lo(k):
                    v.wait_ge(whi_ok, NX * t + k + 1)
                    v.tensor_tensor(W_lo[:, k % 2, :, :], E[:, k % 2, :, :], W_hi[:, k % 2, :, :].bitcast(F32),
                                    ALU.subtract).then_inc(wlo_ok, 1)

                def gate(m):
                    v.wait_ge(y_ready, NX * t + 2 * m + 2)
                    wait(v, sq_ok, 2 * t + m - 1)
                    for r in range(2):
                        rows = slice(64 * r, 64 * (r + 1))
                        for j in range(REP):
                            i = v.scalar_tensor_tensor(
                                out=y[rows, m, j, :], in0=xs[rows, m, :], scalar=dcol[rows, REP * m + j:REP * m + j + 1],
                                in1=psum[rows, YB + r, j * P:(j + 1) * P], op0=ALU.mult, op1=ALU.add)
                    i.then_inc(yd_ok, 1)
                    v.wait_ge(yd_ok, 2 * t + m + 1)
                    v.tensor_tensor(y[:, m, :, :], y[:, m, :, :], feat[:, REP * m:REP * (m + 1), bass.ds(t * P, P)],
                                    ALU.mult).then_inc(yg_ok, 1)

                def gated_lo(m):
                    v.wait_ge(yhi_ok, 2 * t + m + 1)
                    v.tensor_tensor(y_lo[:, REP * m:REP * (m + 1), :], y[:, m, :, :],
                                    y_hi[:, REP * m:REP * (m + 1), :].bitcast(F32), ALU.subtract).then_inc(ylo_ok, 1)
                decay(0)
                decay(1)
                weigh(0)
                weigh(1)
                weights_lo(0)
                weights_lo(1)
                decay(2)
                decay(3)
                gate(0)
                weigh(2)
                weigh(3)
                gated_lo(0)
                weights_lo(2)
                weights_lo(3)
                gate(1)
                gated_lo(1)
                v.wait_ge(ss_ready, t + 1)
                v.tensor_scalar(ms[:, p:p + 1], psum[:, MB, 256:257], 1.0 / DI, EPS, ALU.mult, ALU.add).then_inc(ms_ok, 1)
                v.wait_ge(o_ready, t + 1)
                v.wait_ge(rs_ok, t + 1)
                v.scalar_tensor_tensor(out=x[:, bass.ds(t, 1), :], in0=psum[:, OB:OB + 1, :], scalar=rs[:, p:p + 1],
                                       in1=x[:, bass.ds(t, 1), :], op0=ALU.mult, op1=ALU.add).then_inc(o_ok, 1)
            tiles(v, tile)

        @block.tensor
        def _(pe):
            pe.wait_ge(set_up, 2)
            pe.wait_ge(pick_ok, 1)

            def tile(t, p):
                pe.wait_ge(xs_ok, t + 1)
                wait(pe, ms_ok, t)
                for c in range(2):
                    m = pe.transpose(psum[:, MB, c * P:(c + 1) * P], xs[:, c, :], ident[:])
                m.then_inc(xt_ready, 1)
                def sums(k):
                    wait(pe, dm_ok, REP * (NX * t + k - 1))
                    for j in range(REP):
                        h = k * REP + j
                        one = pick[:, h:h + 1].to_broadcast([P, P])
                        out = psum[:, CU + k % 2, j * P:(j + 1) * P]
                        pe.matmul(out, one, cumT_hi[:, bass.ds(t * P, P)], start=True, stop=False)
                        i = pe.matmul(out, one, cumT_lo[:, bass.ds(t * P, P)], start=False, stop=True)
                    i.then_inc(cu_ready, 1)

                def scores(k):
                    pe.wait_ge(cb_ok, 2 * (t + 1))
                    wait(pe, w_ok, REP * (NX * t + k - 1))
                    r, m = 64 * (k % 2), k // 2
                    rows, ch = slice(r, r + 64), slice(REP * m, REP * (m + 1))
                    passes(pe, psum[:, SB + k % 2, :], B_hi[rows, m, :], B_lo[rows, m, :], C_hi[rows, ch, :],
                           C_lo[rows, ch, :], True, True).then_inc(s_ready, 1)

                def outputs(k):
                    pe.wait_ge(xt_ok, t + 1)
                    pe.wait_ge(wlo_ok, NX * t + k + 1)
                    wait(pe, yd_ok, 2 * t + k // 2)
                    cols = slice((k // 2) * P, (k // 2 + 1) * P)
                    passes(pe, psum[:, YB + k % 2, :], xt_hi[:, cols], xt_lo[:, cols], W_hi[:, k % 2, :, :],
                           W_lo[:, k % 2, :, :], True, True).then_inc(y_ready, 1)

                def project(m):
                    pe.wait_ge(ylo_ok, 2 * t + m + 1)
                    if m == 0:
                        wait(pe, o_ok, t)
                    for c in range(REP * m, REP * (m + 1)):
                        i = passes(pe, psum[:, OB, :], y_hi[:, c, :], y_lo[:, c, :], wo_hi[:, c, :], wo_lo[:, c, :],
                                   c == 0, c == ZC - 1)
                    if m == 1:
                        i.then_inc(o_ready, 1)

                def squares():
                    pe.wait_ge(sq_ok, 2 * (t + 1))
                    for c in range(ZC):
                        i = pe.matmul(psum[:, MB, 256:257], sq[:, c // REP, c % REP, :], ones[:, 0:1], start=(c == 0),
                                      stop=(c == ZC - 1))
                    i.then_inc(ss_ready, 1)
                sums(0)
                sums(1)
                scores(0)
                scores(1)
                sums(2)
                sums(3)
                outputs(0)
                outputs(1)
                scores(2)
                scores(3)
                if isinstance(t, int) and t == 0:
                    pe.wait_ge(wo_ok, ZC)
                outputs(2)
                outputs(3)
                project(0)
                squares()
                project(1)
            tiles(pe, tile)


MG, MC = 8, 2


def phase_ffn(nc, d, g, tag, groups, widths, gated, w1_names, w2_name, tok_w=None, bias=None):
    psum, x, xT_hi, xT_lo = g["psum"], g["x"], g["xT_hi"], g["xT_lo"]
    NC, F, NW = len(widths), sum(widths), len(w1_names)
    UP, DN = 0, 4
    with ExitStack() as ctx:
        n = Names(nc, ctx, tag)
        raw1 = n.sb("raw1", [P, NW, DC, F])
        raw2 = n.sb("raw2", [P, NC, D])
        w1_hi, w1_lo = n.sb("w1_hi", [P, 2, NW, DC, F], F32R), n.sb("w1_lo", [P, 2, NW, DC, F], F32R)
        w2_hi, w2_lo = n.sb("w2_hi", [P, 2, NC, D], F32R), n.sb("w2_lo", [P, 2, NC, D], F32R)
        side = n.sb("side", [P, 2, TT])
        h_hi, h_lo = n.sb("h_hi", [P, NC, TOK], F32R), n.sb("h_lo", [P, NC, TOK], F32R)
        s1 = n.sb("s1", [P, 2, HALF])
        hh = n.sb("hh", [P, 2, HALF]) if gated else s1
        if bias is not None:
            b_all = n.sb("b_all", [P, groups, NC])
        S_ = n.sem
        bias_in, in1, in2 = S_("bias_in"), S_("in1"), S_("in2")
        w_hi_ok, w_ok, side_ok = S_("w_hi_ok"), S_("w_ok"), S_("side_ok")
        up_ready, act_ok, hh_ok, hhi_ok, h_ok = S_("up_ready"), S_("act_ok"), S_("hh_ok"), S_("hhi_ok"), S_("h_ok")
        dn_ready, dn_ok = S_("dn_ready"), S_("dn_ok")
        block = ctx.enter_context(nc.Block())
        NWS = NW + 1
        U = NC * NHALF
        UB = 4 // NW

        def loop(e, group):
            group(0, 0)
            group(1, 1)
            if groups > 4:
                with e.Fori(1, groups // 2 - 1) as i:
                    group(2 * i, 0)
                    group(2 * i + 1, 1)
            group(groups - 2, 0)
            group(groups - 1, 1)

        @block.sync
        def _(sp):
            if bias is not None:
                sp.dma_start(b_all[:], d[bias]).then_inc(bias_in, 16)

            def load(k):
                wait(sp, w_ok, NWS * k)
                for i, name in enumerate(w1_names):
                    sp.dma_start(raw1[:, i, :, :], d[name][k]).then_inc(in1, 16)
                for c, wd in enumerate(widths):
                    sp.dma_start(raw2[0:wd, c, :], d[w2_name][k, c * P:c * P + wd, :]).then_inc(in2, 16)
            load(0)
            with sp.Fori(1, groups) as k:
                load(k)

        @block.scalar
        def _(act):
            def split(k, p):
                act.wait_ge(in1, 16 * NW * (k + 1))
                wait(act, dn_ready, TT * (k - 1))
                for i in range(NW):
                    act.activation(w1_hi[:, p, i, :, :], raw1[:, i, :, :], ACT.Copy).then_inc(w_hi_ok, 1)
                act.wait_ge(in2, 16 * NC * (k + 1))
                full = sum(1 for wd in widths if wd == P)
                last = act.activation(w2_hi[:, p, 0:full, :], raw2[:, 0:full, :], ACT.Copy)
                if full < NC:
                    last = act.activation(w2_hi[0:widths[-1], p, full, :], raw2[0:widths[-1], full, :], ACT.Copy)
                last.then_inc(w_hi_ok, 1)

            def half_step(k, p, half):
                for c, wd in enumerate(widths):
                    m = half * NC + c
                    act.wait_ge(up_ready, U * k + m + 1)
                    if gated:
                        wait(act, hh_ok, U * k + m - 1)
                        act.activation(s1[0:wd, m % 2, :], psum[0:wd, UP + 2 * (m % 2), :], ACT.Silu).then_inc(act_ok, 1)
                    else:
                        wait(act, h_ok, U * k + m - 1)
                        act.wait_ge(side_ok, k + 1)
                        act.activation(s1[0:wd, m % 2, :], psum[0:wd, UP + m % 4, :], ACT.Gelu_apprx_tanh,
                                       bias=side[0:wd, p, c:c + 1]).then_inc(act_ok, 1)
                        act.wait_ge(act_ok, U * k + m + 1)
                    if m % NC == 0 and not (isinstance(k, int) and k == 0):
                        act.wait_ge(dn_ready, TT * (k - 1) + (half + 1) * (TT // 2))
                    if gated:
                        act.wait_ge(hh_ok, U * k + m + 1)
                    act.activation(h_hi[0:wd, c, half * HALF:(half + 1) * HALF], hh[0:wd, m % 2, :],
                                   ACT.Copy).then_inc(hhi_ok, 1)

            def group(k, p):
                half_step(k, p, 0)
                if not (isinstance(k, int) and k == groups - 1):
                    split(k + 1, 1 - p)
                half_step(k, p, 1)
            split(0, 0)
            loop(act, group)

        @block.vector
        def _(v):
            def split(k, p):
                if tok_w is not None:
                    wait(v, dn_ok, TT * (k - 1))
                    v.tensor_copy(side[:, p, :], tok_w[:, :, bass.ds(k, 1)]).then_inc(side_ok, 1)
                else:
                    if isinstance(k, int) and k == 0:
                        v.wait_ge(bias_in, 16)
                    wait(v, act_ok, U * (k - 1))
                    v.tensor_copy(side[:, p, 0:NC], b_all[:, bass.ds(k, 1), :]).then_inc(side_ok, 1)
                for i in range(NW):
                    v.wait_ge(w_hi_ok, NWS * k + i + 1)
                    v.tensor_tensor(w1_lo[:, p, i, :, :], raw1[:, i, :, :], w1_hi[:, p, i, :, :].bitcast(F32),
                                    ALU.subtract).then_inc(w_ok, 1)
                v.wait_ge(w_hi_ok, NWS * (k + 1))
                full = sum(1 for wd in widths if wd == P)
                last = v.tensor_tensor(w2_lo[:, p, 0:full, :], raw2[:, 0:full, :], w2_hi[:, p, 0:full, :].bitcast(F32),
                                       ALU.subtract)
                if full < NC:
                    wd = widths[-1]
                    last = v.tensor_tensor(w2_lo[0:wd, p, full, :], raw2[0:wd, full, :], w2_hi[0:wd, p, full, :].bitcast(F32),
                                           ALU.subtract)
                last.then_inc(w_ok, 1)

            def half_step(k, p, half):
                for c, wd in enumerate(widths):
                    m = half * NC + c
                    if gated:
                        v.wait_ge(act_ok, U * k + m + 1)
                        wait(v, h_ok, U * k + m - 1)
                        v.tensor_tensor(hh[0:wd, m % 2, :], s1[0:wd, m % 2, :], psum[0:wd, UP + 2 * (m % 2) + 1, :],
                                        ALU.mult).then_inc(hh_ok, 1)
                    v.wait_ge(hhi_ok, U * k + m + 1)
                    v.tensor_tensor(h_lo[0:wd, c, half * HALF:(half + 1) * HALF], hh[0:wd, m % 2, :],
                                    h_hi[0:wd, c, half * HALF:(half + 1) * HALF].bitcast(F32), ALU.subtract).then_inc(h_ok, 1)

            def down(k, p):
                for t in range(TT):
                    v.wait_ge(dn_ready, TT * k + t + 1)
                    if tok_w is not None:
                        if t == 0:
                            v.wait_ge(side_ok, k + 1)
                        v.scalar_tensor_tensor(out=x[:, t, :], in0=psum[:, DN + t % 4, :], scalar=side[:, p, t:t + 1],
                                               in1=x[:, t, :], op0=ALU.mult, op1=ALU.add).then_inc(dn_ok, 1)
                    else:
                        v.tensor_tensor(x[:, t, :], x[:, t, :], psum[:, DN + t % 4, :], ALU.add).then_inc(dn_ok, 1)

            def group(k, p):
                half_step(k, p, 0)
                if not (isinstance(k, int) and k == groups - 1):
                    split(k + 1, 1 - p)
                half_step(k, p, 1)
                down(k, p)
            split(0, 0)
            loop(v, group)

        @block.tensor
        def _(pe):
            def group(k, p):
                pe.wait_ge(w_ok, NWS * (k + 1))
                for half in range(NHALF):
                    cols = slice(half * HALF, (half + 1) * HALF)
                    f0 = 0
                    for c, wd in enumerate(widths):
                        m = half * NC + c
                        wait(pe, hh_ok if gated else act_ok, U * k + m - UB + 1)
                        for i in range(NW):
                            bank = UP + (2 * (m % 2) + i if gated else m % 4)
                            for dc in range(DC):
                                last = passes(pe, psum[0:wd, bank, :], w1_hi[:, p, i, dc, f0:f0 + wd],
                                              w1_lo[:, p, i, dc, f0:f0 + wd], xT_hi[:, dc, cols], xT_lo[:, dc, cols],
                                              dc == 0, dc == DC - 1)
                        last.then_inc(up_ready, 1)
                        f0 += wd
                for t in range(TT):
                    pe.wait_ge(h_ok, U * k + (NC if t < TT // 2 else U))
                    wait(pe, dn_ok, TT * k + t - 3)
                    toks = slice(t * P, (t + 1) * P)
                    for c, wd in enumerate(widths):
                        last = passes(pe, psum[:, DN + t % 4, :], h_hi[0:wd, c, toks], h_lo[0:wd, c, toks],
                                      w2_hi[0:wd, p, c, :], w2_lo[0:wd, p, c, :], c == 0, c == NC - 1)
                    last.then_inc(dn_ready, 1)
            loop(pe, group)


NE, NG, FE, NSH = 8, 4, 352, 2
NEX = NE + NSH


def phase_route(nc, d, g, tok_w):
    psum, xT_hi, xT_lo = g["psum"], g["xT_hi"], g["xT_lo"]
    with ExitStack() as ctx:
        n = Names(nc, ctx, "route")
        gw = n.sb("gw", [P, DC, NE])
        gw_hi, gw_lo = n.sb("gw_hi", [P, DC, NE], F32R), n.sb("gw_lo", [P, DC, NE], F32R)
        before = n.sb("before", [P, NE, NE])
        lg, best, total = n.sb("lg", [P, TT, NE]), n.sb("best", [P, TT]), n.sb("total", [P, TT])
        grp, grank, masked, rank = n.sb("grp", [P, TT, NG]), n.sb("grank", [P, TT, NG]), n.sb("masked", [P, TT, NE]), n.sb("rank", [P, TT, NE])
        gt, eq = n.sb("gt", [P, TT, NE, NE]), n.sb("eq", [P, TT, NE, NE])
        loaded, split, ready, chain, exp_ok = n.sem("loaded"), n.sem("split"), n.sem("ready"), n.sem("chain"), n.sem("exp_ok")
        block = ctx.enter_context(nc.Block())

        @block.sync
        def _(sp):
            sp.dma_start(gw[:], d["gate_weight"]).then_inc(loaded, 16)
            sp.dma_start(before[:], d["before"]).then_inc(loaded, 16)

        @block.tensor
        def _(pe):
            pe.wait_ge(split, 2)
            for t in range(TT):
                toks = slice(t * P, (t + 1) * P)
                for c in range(DC):
                    m = passes(pe, psum[:, 0, t * NE:(t + 1) * NE], xT_hi[:, c, toks], xT_lo[:, c, toks], gw_hi[:, c, :],
                               gw_lo[:, c, :], c == 0, c == DC - 1)
            m.then_inc(ready, 1)

        @block.scalar
        def _(act):
            act.wait_ge(chain, 2)
            act.activation(lg[:], lg[:], ACT.Exp).then_inc(exp_ok, 1)

        @block.vector
        def _(v):
            steps = [0]

            def link(i):
                steps[0] += 1
                i.then_inc(chain, 1)
                v.wait_ge(chain, steps[0])
            v.wait_ge(loaded, 32)
            v.tensor_copy(gw_hi[:], gw[:]).then_inc(split, 1)
            v.wait_ge(split, 1)
            v.tensor_tensor(gw_lo[:], gw[:], gw_hi[:].bitcast(F32), ALU.subtract).then_inc(split, 1)
            v.wait_ge(ready, 1)
            logits = psum[:, 0, 0:TT * NE].rearrange("p (t e) -> p t e", e=NE)

            def per_tile(a, m):
                return a[:].rearrange("p (t o) -> p t o", o=1).to_broadcast([P, TT, m])
            link(v.tensor_reduce(best[:], logits, AX_X, ALU.max))
            link(v.tensor_tensor(lg[:], logits, per_tile(best, NE), ALU.subtract))
            v.wait_ge(exp_ok, 1)
            link(v.tensor_reduce(total[:], lg[:], AX_X, ALU.add))
            link(v.reciprocal(total[:], total[:]))
            link(v.tensor_tensor(lg[:], lg[:], per_tile(total, NE), ALU.mult))
            link(v.tensor_reduce(grp[:], lg[:].rearrange("p t (g e) -> p t g e", e=NE // NG), AX_X, ALU.max))

            def ranks(out, s, m):
                other = s[:].rearrange("p t (o f) -> p t o f", o=1).to_broadcast([P, TT, m, m])
                own = s[:].rearrange("p t (e o) -> p t e o", o=1).to_broadcast([P, TT, m, m])
                low = before[:, 0:m, 0:m].rearrange("p (o e) f -> p o e f", o=1).to_broadcast([P, TT, m, m])
                a, b = gt[:, :, 0:m, 0:m], eq[:, :, 0:m, 0:m]
                link(v.tensor_tensor(a, other, own, ALU.is_gt))
                link(v.tensor_tensor(b, other, own, ALU.is_equal))
                link(v.tensor_tensor(b, b, low, ALU.mult))
                link(v.tensor_tensor(a, a, b, ALU.add))
                link(v.tensor_reduce(out[:], a, AX_X, ALU.add))
            ranks(grank, grp, NG)
            link(v.tensor_scalar(grank[:], grank[:], 2.0, None, ALU.is_lt))
            link(v.tensor_tensor(masked[:].rearrange("p t (g e) -> p t g e", e=NE // NG),
                                 lg[:].rearrange("p t (g e) -> p t g e", e=NE // NG),
                                 grank[:].rearrange("p t (g o) -> p t g o", o=1).to_broadcast([P, TT, NG, NE // NG]), ALU.mult))
            ranks(rank, masked, NE)
            link(v.tensor_scalar(rank[:], rank[:], 2.0, None, ALU.is_lt))
            v.tensor_tensor(tok_w[:, :, 0:NE], rank[:], masked[:], ALU.mult).then_inc(split, 1)
            v.memset(tok_w[:, :, NE:NEX], 1.0).then_inc(split, 1)


def phase_rest(nc, d, g):
    with ExitStack() as mix:
        a = Names(nc, mix, "mix")
        feat = a.sb("feat", [P, FEATS, TOK])
        dc = a.sb("dc", [P, TT, 2, NH])
        cumT_hi, cumT_lo = a.sb("cumT_hi", [P, TOK], F32R), a.sb("cumT_lo", [P, TOK], F32R)
        with ExitStack() as inner:
            m = Names(nc, inner, "second")
            g["xT_hi"], g["xT_lo"] = m.sb("xT_hi", [P, DC, TOK], F32R), m.sb("xT_lo", [P, DC, TOK], F32R)
            phase_norm(nc, d, g, "norm2", False, True)
            phase_ffn(nc, d, g, "mlp", MG, [P] * MC, False, ["fc1"], "fc2", bias="fc1_b")
            phase_project(nc, d, g, feat, dc, cumT_hi, cumT_lo)
        phase_scan(nc, d, g, feat, dc, cumT_hi, cumT_lo)
    with ExitStack() as moe:
        a = Names(nc, moe, "moe")
        g["xT_hi"], g["xT_lo"] = a.sb("xT_hi", [P, DC, TOK], F32R), a.sb("xT_lo", [P, DC, TOK], F32R)
        tok_w = a.sb("tok_w", [P, TT, NEX])
        phase_norm(nc, d, g, "norm3", False, False)
        phase_route(nc, d, g, tok_w)
        phase_ffn(nc, d, g, "experts", NEX, [P, P, FE - 2 * P], True, ["eg", "eu"], "ed", tok_w=tok_w)


def more_layout(w):
    import numpy as np
    f32 = np.float32

    def chunk_k(a):
        return a.reshape(DC, P, -1).transpose(1, 0, 2)
    w_in = w["L0_attn_W_in"]
    o = np.cumsum([0, DI, NX * HD, NX * NST, DI, NH])
    z, xb, bp, cp, dtw = (w_in[:, o[i]:o[i + 1]] for i in range(5))
    order = [[REP * 2 * m + j, REP * (2 * m + 1) + j] for m in range(2) for j in range(REP)]
    cols = np.array([[h * HD + i for h in pair for i in range(HD)] for pair in order])
    feats = [z[:, c] for c in cols] + [cp[:, c] for c in cols] + [xb[:, :P], xb[:, P:], bp[:, :P], bp[:, P:]]
    t = np.arange(P)
    mask = np.where((t[:, None] // S == t[None, :] // S) & (t[:, None] <= t[None, :]), 0.0, -1e30).astype(f32)
    starts = np.ones((NH, TOK), f32)
    starts[:, ::S] = 0
    per = lambda a: a[cols].T
    return {
        "ln_wb": np.stack([w["L0_attn_ln_w"].reshape(DC, P).T, w["L0_attn_ln_b"].reshape(DC, P).T], 1),
        "w_feat": np.stack([chunk_k(f) for f in feats]),
        "w_dt": chunk_k(dtw),
        "head": np.stack([w["L0_attn_dt_bias"], w["L0_attn_A_log"]], 1),
        "starts": starts,
        "norm_w": per(w["L0_attn_norm_w"]),
        "d_skip": per(np.repeat(w["L0_attn_D"], HD)),
        "mask": mask,
        "w_out": w["L0_attn_W_out"][cols],
        "fc1": w["L0_attn_fc1_w"].reshape(DC, P, MG, MC * P).transpose(2, 1, 0, 3),
        "fc1_b": w["L0_attn_fc1_b"].reshape(MG, MC, P).transpose(2, 0, 1),
        "fc2": w["L0_attn_fc2_w"].reshape(MG, MC * P, D),
        "fc2_b": np.tile(w["L0_attn_fc2_b"], (P, 1)),
        "gate_weight": chunk_k(w["L0_ffn_gate_weight"].T),
        "before": np.tile((np.arange(NE)[None, :] < np.arange(NE)[:, None]).astype(f32)[None], (P, 1, 1)),
        "eg": experts_in(w["L0_ffn_gate_w"], w["L0_ffn_sh_gate_w"]),
        "eu": experts_in(w["L0_ffn_up_w"], w["L0_ffn_sh_up_w"]),
        "ed": np.concatenate([w["L0_ffn_down_w"].transpose(0, 2, 1), w["L0_ffn_sh_down_w"].T.reshape(NSH, FE, D)]),
    }


def experts_in(routed, shared):
    import numpy as np
    a = np.concatenate([routed, shared.reshape(NSH, FE, D)])
    return a.transpose(0, 2, 1).reshape(NEX, DC, P, FE).transpose(0, 2, 1, 3)


def build(nc, d):
    SEMAPHORES.clear()
    with ExitStack() as top:
        n = Names(nc, top, "all")
        d["tail_rows"] = nc.dram_tensor("tail_rows", [B, 3, P], F32, kind="Internal").ap()
        g = {"psum": top.enter_context(nc.psum_tensor("psum", [P, 8, 512], F32)),
             "x": n.sb("x", [P, TT, D]), "ident": n.sb("ident", [P, P]),
             "tailT_hi": n.sb("tailT_hi", [P, B, 2], F32R), "tailT_lo": n.sb("tailT_lo", [P, B, 2], F32R)}
        phase_context_tail(nc, d, g)
        with ExitStack() as ctx:
            a = Names(nc, ctx, "q")
            q = a.sb("q", [P, B, HS])
            G_hi, G_lo = a.sb("G_hi", [P, H * D], F32R), a.sb("G_lo", [P, H * D], F32R)
            with ExitStack() as inner:
                m = Names(nc, inner, "first")
                g["xT_hi"], g["xT_lo"] = m.sb("xT_hi", [P, DC, TOK], F32R), m.sb("xT_lo", [P, DC, TOK], F32R)
                phase_norm(nc, d, g, "norm1", True, False)
                phase_heads(nc, d, g, q, G_hi, G_lo)
            phase_attention(nc, d, g, q, G_hi, G_lo)
        clear_semaphores(nc)
        phase_rest(nc, d, g)
        phase_store(nc, d, g)


def kernel(**inputs):
    import numpy as np
    import concourse.bacc as bacc
    from concourse.bass_utils import run_bass_kernel_spmd as run

    w = {k: np.asarray(v) for k, v in inputs.items()}
    f32 = np.float32
    inv_freq = (f32(1.0) / np.power(f32(10000.0), np.arange(0, P, 2, dtype=f32) / f32(P), dtype=f32)).astype(f32)
    angle = np.repeat(np.arange(L, dtype=f32)[:, None] * inv_freq[None, :], 2, axis=-1).astype(np.float64)
    cos, sin = np.cos(angle).astype(f32), np.sin(angle).astype(f32)
    sin[:, :P // 2] *= -1
    t = {
        "x": w["x"].reshape(TOK, D),
        "ctx": w["ctx_512"],
        "cos_main": cos[:2 * P].reshape(2, P, P).transpose(1, 0, 2),
        "sin_main": sin[:2 * P].reshape(2, P, P).transpose(1, 0, 2),
        "cos_last": np.tile(cos[L - 1], (B, 1)), "sin_last": np.tile(sin[L - 1], (B, 1)),
        "ident": np.eye(P, dtype=f32),
        "wq": w["L0_xattn_Wq"],
        "kcqT": w["L0_xattn_w_kc_q"].transpose(0, 2, 1),
        "wqrT": w["L0_xattn_W_qr"].transpose(0, 2, 1),
        "wkrT": w["L0_xattn_W_kr"].transpose(0, 2, 1),
        "kckv": w["L0_xattn_w_kc_kv"],
        "woT": w["L0_xattn_Wo"].T,
    }
    t.update(more_layout(w))
    nc = bacc.Bacc("TRN2", target_bir_lowering=False, num_devices=1)
    arrays, d = {}, {}
    for name, a in t.items():
        arrays[f"in_{name}"] = np.ascontiguousarray(a)
        d[name] = nc.dram_tensor(f"in_{name}", a.shape, mybir.dt.from_np(a.dtype), kind="ExternalInput").ap()
    d["out"] = nc.dram_tensor("out", (TOK, D), F32, kind="ExternalOutput").ap()
    build(nc, d)
    r = run(nc, [arrays], core_ids=[0])
    return r.results[0]["out"].reshape(B, S, D)
```

```python
from contextlib import ExitStack

import concourse.bass as bass
from concourse import mybir

F32 = mybir.dt.float32
F32R = mybir.dt.float32r
ALU = mybir.AluOpType
ACT = mybir.ActivationFunctionType
AX_X = mybir.AxisListType.X

P = 128
B, S, D = 32, 32, 512
L = 257
TOK = B * S
TT = TOK // P
DC = D // P
HALF = 512
NHALF = TOK // HALF
BPT = P // S
H, K, CQ, R = 16, 128, 384, 64
QC = CQ // P
HS = H * S
EPS = 1e-5


def wait(e, sem, value):
    if isinstance(value, int) and value <= 0:
        return
    e.wait_ge(sem, value)


def passes(e, out, hi_l, lo_l, hi_r, lo_r, first, last):
    e.matmul(out, hi_l, hi_r, start=first, stop=False)
    e.matmul(out, hi_l, lo_r, start=False, stop=False)
    return e.matmul(out, lo_l, hi_r, start=False, stop=last)


class Names:

    def __init__(self, nc, ctx, tag):
        self.nc, self.ctx, self.tag = nc, ctx, tag

    def sb(self, name, shape, dt=F32):
        return self.ctx.enter_context(self.nc.sbuf_tensor(f"{self.tag}_{name}", shape, dt))

    def sem(self, name):
        made = self.nc.alloc_semaphore(f"{self.tag}_{name}")
        SEMAPHORES.append(made)
        return made


class Parts:
    pass


SEMAPHORES = []


def clear_semaphores(nc):
    nc.clear_and_free_semaphores(list(SEMAPHORES))
    SEMAPHORES.clear()
    nc.all_engine_barrier()


def phase_context_tail(nc, d, g):
    with ExitStack() as ctx:
        n = Names(nc, ctx, "tail")
        row, turned, t2, cosr, sinr = (n.sb(x, [B, P]) for x in ("row", "turned", "t2", "cosr", "sinr"))
        hi, lo = n.sb("hi", [B, P], F32R), n.sb("lo", [B, P], F32R)
        loaded, rotated, split, turned_T = (n.sem(x) for x in ("loaded", "rotated", "split", "turned_T"))
        ps = g["psum"]
        block = ctx.enter_context(nc.Block())

        @block.sync
        def _(sp):
            sp.dma_start(row[:], d["ctx"][:, L - 1, :]).then_inc(loaded, 16)
            sp.dma_start(cosr[:], d["cos_last"]).then_inc(loaded, 16)
            sp.dma_start(sinr[:], d["sin_last"]).then_inc(loaded, 16)
            sp.dma_start(g["ident"][:], d["ident"]).then_inc(loaded, 16)
            for t in range(TT):
                sp.dma_start(g["x"][:, t, :], d["x"][t * P:(t + 1) * P, :]).then_inc(g["x_loaded"][t], 16)
            sp.wait_ge(split, 2)
            for r, part in enumerate((hi, lo, hi)):
                sp.dma_start(d["tail_rows"][:, r, :], part[:].bitcast(F32)).then_inc(g["tail_stored"], 16)

        @block.vector
        def _(v):
            v.wait_ge(loaded, 64)
            v.tensor_tensor(turned[:], row[:], cosr[:], ALU.mult).then_inc(rotated, 1)
            v.tensor_tensor(t2[:, 0:64], row[:, 64:128], sinr[:, 0:64], ALU.mult).then_inc(rotated, 1)
            v.tensor_tensor(t2[:, 64:128], row[:, 0:64], sinr[:, 64:128], ALU.mult).then_inc(rotated, 1)
            v.wait_ge(rotated, 3)
            v.tensor_tensor(turned[:], turned[:], t2[:], ALU.add).then_inc(rotated, 1)
            v.wait_ge(rotated, 4)
            v.tensor_copy(hi[:], turned[:]).then_inc(split, 1)
            v.wait_ge(split, 1)
            v.tensor_tensor(lo[:], turned[:], hi[:].bitcast(F32), ALU.subtract).then_inc(split, 1)
            v.wait_ge(turned_T, 1)
            for c in range(2):
                v.tensor_copy(g["tailT_hi"][:, :, c], ps[:, 0, 0:B]).then_inc(split, 1)
            v.wait_ge(split, 4)
            for c in range(2):
                v.tensor_tensor(g["tailT_lo"][:, :, c], ps[:, 0, 0:B], g["tailT_hi"][:, :, 0].bitcast(F32),
                                ALU.subtract).then_inc(split, 1)

        @block.tensor
        def _(pe):
            pe.wait_ge(rotated, 4)
            pe.transpose(ps[:, 0, 0:B], turned[:], g["ident"][0:B, 0:B]).then_inc(turned_T, 1)


class Norm:
    BANK = 6

    def __init__(self, n, g, xn, loaded=(), affine=None):
        self.g, self.xn, self.loaded, self.affine = g, xn, loaded, affine
        self.rounds = 2 if affine else 1
        self.stats, self.mv = n.sb("stats", [P, TT, 6]), n.sb("mv", [P, TT, 2])
        self.var, self.rstd = n.sb("var", [P, TT, self.rounds]), n.sb("rstd", [P, TT, self.rounds])
        self.power = n.sb("power", [P, TT * self.rounds])
        if affine:
            self.wb = n.sb("wb", [P, 2, DC])
        (self.wb_in, self.power_set, self.stat_done, self.aggr, self.var_done, self.rstd_done, self.first_done, self.normed,
         self.x_added, self.transposed, self.scaled, self.hi_done, self.lo_done) = (n.sem(k) for k in (
             "wb_in", "power_set", "stat_done", "aggr", "var_done", "rstd_done", "first_done", "normed", "x_added",
             "transposed", "scaled", "hi_done", "lo_done"))

    def bank(self, t):
        return self.g["psum"][:, self.BANK + t % 2, :].rearrange("p (c k) -> p c k", c=DC)

    def load(self, sp):
        if self.affine:
            sp.dma_start(self.wb[:], self.affine[2]).then_inc(self.wb_in, 16)

    def roots(self, pool):
        pool.memset(self.power[:], -0.5).then_inc(self.power_set, 1)
        pool.wait_ge(self.power_set, 1)
        for half in range(2):
            tiles = slice(half * TT // 2, (half + 1) * TT // 2)
            pool.wait_ge(self.var_done, self.rounds * (half + 1))
            pool.tensor_tensor(self.rstd[:, tiles, :], self.var[:, tiles, :],
                               self.power[:].rearrange("p (t r) -> p t r", r=self.rounds)[:, tiles, :],
                               ALU.pow).then_inc(self.rstd_done, 1)
        if self.affine:
            x = self.g["x"]
            for t in range(TT):
                pool.wait_ge(self.first_done, t + 1)
                pool.wait_ge(self.normed, t + 1)
                pool.tensor_tensor(x[:, t, :], x[:, t, :], self.affine[0][:, t, :], ALU.add).then_inc(self.x_added, 1)

    def statistics(self, v):
        for half in range(2):
            tiles = range(half * TT // 2, (half + 1) * TT // 2)
            for t in tiles:
                if self.loaded:
                    v.wait_ge(self.loaded[t], 16)
                v.bn_stats(self.stats[:, t, :], self.g["x"][:, t, :]).then_inc(self.stat_done, 1)
            for t in tiles:
                v.wait_ge(self.stat_done, t + 1)
                v.bn_aggr(self.mv[:, t, :], self.stats[:, t, :]).then_inc(self.aggr, 1)
            v.wait_ge(self.aggr, (half + 1) * TT // 2)
            these = slice(tiles[0], tiles[-1] + 1)
            v.tensor_scalar(self.var[:, these, 0], self.mv[:, these, 1], EPS, None, ALU.add).then_inc(self.var_done, 1)
            if self.affine:
                v.tensor_scalar(self.var[:, these, 1], self.mv[:, these, 1], 1.0 + EPS, EPS * EPS, ALU.mult,
                                ALU.add).then_inc(self.var_done, 1)

    def normalise(self, v):
        x = self.g["x"]

        def rows(t):
            v.wait_ge(self.rstd_done, 1 + t // (TT // 2))
            for r in range(self.rounds):
                out, done = (self.xn, self.normed) if r == self.rounds - 1 else (self.affine[0], self.first_done)
                v.tensor_scalar(out[:, t, :], x[:, t, :], self.mv[:, t, 0:1], self.rstd[:, t, r:r + 1],
                                ALU.subtract, ALU.mult).then_inc(done, 1)

        def low_part(t):
            toks = slice(t * P, (t + 1) * P)
            src = self.affine[1][:, t, :, :] if self.affine else self.bank(t)
            v.wait_ge(self.hi_done, t + 1)
            v.tensor_tensor(self.g["xT_lo"][:, :, toks], src, self.g["xT_hi"][:, :, toks].bitcast(F32),
                            ALU.subtract).then_inc(self.lo_done, 1)
        lag = 3
        for t in range(TT + lag):
            if t < TT:
                rows(t)
            if t >= lag:
                low_part(t - lag)

    def transpose(self, pe):
        for t in range(TT):
            pe.wait_ge(self.normed, t + 1)
            wait(pe, self.hi_done, t - 1)
            wait(pe, self.lo_done, t - 1)
            for c in range(DC):
                m = pe.transpose(self.g["psum"][:, self.BANK + t % 2, c * P:(c + 1) * P], self.xn[:, t, c * P:(c + 1) * P],
                                 self.g["ident"][:])
            m.then_inc(self.transposed, 1)

    def high_parts(self, act):
        if self.affine:
            act.wait_ge(self.wb_in, 16)
        for t in range(TT):
            act.wait_ge(self.transposed, t + 1)
            src = self.bank(t)
            if self.affine:
                for c in range(DC):
                    act.activation(self.affine[1][:, t, c, :], src[:, c, :], ACT.Identity, scale=self.wb[:, 0, c:c + 1],
                                   bias=self.wb[:, 1, c:c + 1]).then_inc(self.scaled, 1)
                act.wait_ge(self.scaled, DC * (t + 1))
                src = self.affine[1][:, t, :, :]
            act.activation(self.g["xT_hi"][:, :, t * P:(t + 1) * P], src, ACT.Copy).then_inc(self.hi_done, 1)


def phase_heads(nc, d, g, q, G_hi, G_lo):
    psum, xT_hi, xT_lo = g["psum"], g["xT_hi"], g["xT_lo"]
    M1, M2, CB, GB, QB = 0, 1, 2, 3, 4
    with ExitStack() as ctx:
        n = Names(nc, ctx, "heads")
        norm = Norm(n, g, q, loaded=g["x_loaded"])
        wq = n.sb("wq", [P, 2, D])
        kcqT = n.sb("kcqT", [P, 2, QC, P])
        wqrT = n.sb("wqrT", [R, 2, CQ])
        wkrT = n.sb("wkrT", [R, 2, P])
        kckv = n.sb("kckv", [P, 2, P])
        woT = n.sb("woT", [P, 2, D])
        m1 = n.sb("m1", [P, QC, P])
        m2 = n.sb("m2", [P, P])
        C_hi = n.sb("C_hi", [P, 2, DC, P], F32R)
        C_lo = n.sb("C_lo", [P, 2, DC, P], F32R)
        loaded = [n.sem(f"loaded{p}") for p in range(2)]
        m1_ready, m1_kept, m2_ready, m2_kept = (n.sem(x) for x in ("m1_ready", "m1_kept", "m2_ready", "m2_kept"))
        c_ready, c_hi_kept, c_kept = (n.sem(x) for x in ("c_ready", "c_hi_kept", "c_kept"))
        g_ready, g_hi_kept, g_kept = (n.sem(x) for x in ("g_ready", "g_hi_kept", "g_kept"))
        q_ready, q_kept = n.sem("q_ready"), n.sem("q_kept")
        block = ctx.enter_context(nc.Block())

        @block.gpsimd
        def _(pool):
            norm.roots(pool)

        @block.sync
        def _(sp):
            def load(h, p):
                wait(sp, g_ready, h - 1)
                rows = bass.ds(h * P, P)
                for dst, src in ((wkrT[:, p, :], d["wkrT"][h]), (wqrT[:, p, :], d["wqrT"][h]),
                                 (kcqT[:, p, :, :], d["kcqT"][h].rearrange("(c p) k -> p c k", p=P)),
                                 (wq[:, p, :], d["wq"][rows, :]), (kckv[:, p, :], d["kckv"][h]),
                                 (woT[:, p, :], d["woT"][rows, :])):
                    sp.dma_start(dst, src).then_inc(loaded[p], 16)
            load(0, 0)
            load(1, 1)
            with sp.Fori(1, H // 2) as i:
                for p in range(2):
                    load(2 * i + p, p)

        def fold_m1(pe, h, p, k):
            pe.wait_ge(loaded[p], 96 * (k + 1))
            wait(pe, m1_kept, h)
            for c in range(QC):
                m = pe.matmul(psum[:, M1, c * P:(c + 1) * P], wqrT[:, p, c * P:(c + 1) * P], wkrT[:, p, :],
                              start=True, stop=True)
            m.then_inc(m1_ready, 1)

        def fold_m2(pe, h, p):
            pe.wait_ge(m1_kept, h + 1)
            for c in range(QC):
                m = pe.matmul(psum[:, M2, 0:P], kcqT[:, p, c, :], m1[:, c, :], start=(c == 0), stop=(c == QC - 1))
            m.then_inc(m2_ready, 1)

        def fold_cg(pe, h, p):
            pe.wait_ge(m2_kept, h + 1)
            wait(pe, c_kept, h)
            wait(pe, g_kept, h)
            for c in range(DC):
                m = pe.matmul(psum[:, CB, c * P:(c + 1) * P], wq[:, p, c * P:(c + 1) * P], m2[:], start=True, stop=True)
            m.then_inc(c_ready, 1)
            pe.matmul(psum[:, GB, :], kckv[:, p, :], woT[:, p, :], start=True, stop=True).then_inc(g_ready, 1)

        def project(pe, h, p, half):
            pe.wait_ge(c_kept, h + 1)
            wait(pe, q_kept, 2 * h + half - 1)
            for c in range(DC):
                cols = slice(half * HALF, (half + 1) * HALF)
                m = passes(pe, psum[:, QB + half, :], C_hi[:, p, c, :], C_lo[:, p, c, :],
                           xT_hi[:, c, cols], xT_lo[:, c, cols], c == 0, c == DC - 1)
            m.then_inc(q_ready, 1)

        @block.tensor
        def _(pe):
            def step(h, p, k_next, fold_next):
                if fold_next:
                    fold_m1(pe, h + 1, 1 - p, k_next)
                project(pe, h, p, 0)
                if fold_next:
                    fold_m2(pe, h + 1, 1 - p)
                project(pe, h, p, 1)
                if fold_next:
                    fold_cg(pe, h + 1, 1 - p)
            fold_m1(pe, 0, 0, 0)
            fold_m2(pe, 0, 0)
            fold_cg(pe, 0, 0)
            norm.transpose(pe)
            pe.wait_ge(norm.lo_done, TT)
            step(0, 0, 0, True)
            step(1, 1, 1, True)
            with pe.Fori(1, H // 2 - 1) as i:
                step(2 * i, 0, i, True)
                step(2 * i + 1, 1, i + 1, True)
            step(H - 2, 0, H // 2 - 1, True)
            step(H - 1, 1, 0, False)

        @block.scalar
        def _(act):
            def step(h, p):
                act.wait_ge(m1_ready, h + 1)
                wait(act, m2_ready, h)
                act.activation(m1[:], psum[:, M1, 0:CQ].rearrange("p (c k) -> p c k", c=QC), ACT.Copy).then_inc(m1_kept, 1)
                act.wait_ge(c_ready, h + 1)
                wait(act, q_ready, 2 * (h - 1))
                act.activation(C_hi[:, p, :, :], psum[:, CB, :].rearrange("p (c k) -> p c k", c=DC),
                               ACT.Copy).then_inc(c_hi_kept, 1)
            step(0, 0)
            norm.high_parts(act)
            step(1, 1)
            with act.Fori(1, H // 2) as i:
                step(2 * i, 0)
                step(2 * i + 1, 1)

        @block.vector
        def _(v):
            def keep_m2(h):
                v.wait_ge(m2_ready, h + 1)
                wait(v, c_ready, h)
                v.tensor_copy(m2[:], psum[:, M2, 0:P]).then_inc(m2_kept, 1)

            def keep_q(h, half):
                v.wait_ge(q_ready, 2 * h + half + 1)
                nb = HALF // S
                v.tensor_copy(q[:, half * nb:(half + 1) * nb, bass.ds(h * S, S)],
                              psum[:, QB + half, :].rearrange("p (b s) -> p b s", s=S)).then_inc(q_kept, 1)

            def step(h, p, fold_next):
                keep_q(h, 0)
                if fold_next:
                    keep_m2(h + 1)
                keep_q(h, 1)
                if fold_next:
                    split_cg(h + 1, 1 - p)

            def split_cg(h, p):
                v.wait_ge(c_hi_kept, h + 1)
                v.tensor_tensor(C_lo[:, p, :, :], psum[:, CB, :].rearrange("p (c k) -> p c k", c=DC),
                                C_hi[:, p, :, :].bitcast(F32), ALU.subtract).then_inc(c_kept, 1)
                v.wait_ge(g_ready, h + 1)
                gcols = bass.ds(h * D, D)
                v.tensor_copy(G_hi[:, gcols], psum[:, GB, :]).then_inc(g_hi_kept, 1)
                v.wait_ge(g_hi_kept, h + 1)
                v.tensor_tensor(G_lo[:, gcols], psum[:, GB, :], G_hi[:, gcols].bitcast(F32),
                                ALU.subtract).then_inc(g_kept, 1)
            norm.statistics(v)
            keep_m2(0)
            split_cg(0, 0)
            norm.normalise(v)
            step(0, 0, True)
            step(1, 1, True)
            with v.Fori(1, H // 2 - 1) as i:
                step(2 * i, 0, True)
                step(2 * i + 1, 1, True)
            step(H - 2, 0, True)
            step(H - 1, 1, False)


def phase_attention(nc, d, g, q, G_hi, G_lo):
    psum, x, ident = g["psum"], g["x"], g["ident"]
    SC, PT0, CT, KT = 0, 4, 6, 7
    LP = L + 1
    NJ = HS // P
    KVB = 4
    with ExitStack() as ctx:
        n = Names(nc, ctx, "att")
        cosb, sinb = n.sb("cosb", [P, 2, P]), n.sb("sinb", [P, 2, P])
        raw = n.sb("raw", [P, 2, P])
        turn = n.sb("turn", [P, 2, P])
        kvr = n.sb("kvr", [P, 2, 2, P])
        kv_hi, kv_lo = n.sb("kv_hi", [P, KVB, 2, P], F32R), n.sb("kv_lo", [P, KVB, 2, P], F32R)
        tail = n.sb("tail", [3, KVB, P], F32R)
        kvT_hi, kvT_lo = n.sb("kvT_hi", [P, 2, LP], F32R), n.sb("kvT_lo", [P, 2, LP], F32R)
        q_hi, q_lo = n.sb("q_hi", [P, 2, HS], F32R), n.sb("q_lo", [P, 2, HS], F32R)
        pr = n.sb("pr", [P, 2, NJ, LP + 2])
        prr = pr[:].bitcast(F32R)
        low = n.sb("low", [P, 2, NJ])
        total, scale = n.sb("total", [P, 2, NJ]), n.sb("scale", [P, 2, NJ])
        pT_hi, pT_lo = n.sb("pT_hi", [P, 2, HS], F32R), n.sb("pT_lo", [P, 2, HS], F32R)
        pT_tail = n.sb("pT_tail", [3, HS], F32R)
        cT_hi, cT_lo = n.sb("cT_hi", [P, H, P], F32R), n.sb("cT_lo", [P, H, P], F32R)
        S_ = n.sem
        tables, raw_in, rot, rot_mid, tail_in = S_("tables"), S_("raw_in"), S_("rot"), S_("rot_mid"), [S_(f"tail_in{i}") for i in range(KVB)]
        rot_a, tail_cols = S_("rot_a"), S_("tail_cols")
        kvT_ready, kvT_hi_ok, kvT_ok, kv_hi_ok, kv_ok = (S_(x) for x in ("kvT_ready", "kvT_hi_ok", "kvT_ok", "kv_hi_ok", "kv_ok"))
        q_hi_ok, q_ok = S_("q_hi_ok"), S_("q_ok")
        sc_ready, low_ok, exp_ok, inv_ok, pr_ok, p_split, p_tail = (S_(x) for x in (
            "sc_ready", "low_ok", "exp_ok", "inv_ok", "pr_ok", "p_split", "p_tail"))
        pt_ready, pt_hi_ok, pt_ok, ptail_ok = (S_(x) for x in ("pt_ready", "pt_hi_ok", "pt_ok", "ptail_ok"))
        c_ready, c_hi_ok, c_ok, o_ready, o_ok = (S_(x) for x in ("c_ready", "c_hi_ok", "c_ok", "o_ready", "o_ok"))
        block = ctx.enter_context(nc.Block())

        def run(e, step):
            for u in range(BPT):
                step(u, u)
            with e.Fori(1, B // BPT - 1) as i:
                for u in range(BPT):
                    step(BPT * i + u, u)
            for s in range(B - BPT, B + 3):
                step(s, s % BPT)

        def inside(s, lag):
            return not isinstance(s, int) or 0 <= s - lag < B

        @block.sync
        def _(sp):
            sp.dma_start(cosb[:], d["cos_main"]).then_inc(tables, 16)
            sp.dma_start(sinb[:], d["sin_main"]).then_inc(tables, 16)
            sp.wait_ge(g["tail_stored"], 48)

            def load(b, u):
                wait(sp, rot_a, b)
                sp.dma_start(raw[:], d["ctx"][b, 0:2 * P, :].rearrange("(c p) k -> p c k", p=P)).then_inc(raw_in, 16)

            def load_tail(b, u):
                wait(sp, c_ready, b - KVB + 1)
                sp.dma_start(tail[:, u, :].bitcast(F32), d["tail_rows"][b]).then_inc(tail_in[u], 16)
            for b in range(2 * BPT):
                load(b, b % BPT)
                if b >= 2:
                    load_tail(b - 2, (b - 2) % BPT)
            with sp.Fori(2, B // BPT) as i:
                for u in range(BPT):
                    load(BPT * i + u, u)
                    load_tail(BPT * i + u - 2, (u - 2) % BPT)
            load_tail(B - 2, 2)
            load_tail(B - 1, 3)

        @block.gpsimd
        def _(pool):
            def rotate(b, u):
                p = u % 2
                pool.wait_ge(raw_in, 16 * (b + 1))
                wait(pool, kvT_ready, b - 1)
                wait(pool, kv_ok, b - 1)
                wait(pool, rot, b)
                pool.tensor_tensor(kvr[:, p, :, :], raw[:], cosb[:], ALU.mult).then_inc(rot_mid, 1)
                pool.tensor_tensor(turn[:, :, 0:64], raw[:, :, 64:128], sinb[:, :, 0:64], ALU.mult).then_inc(rot_mid, 1)
                pool.tensor_tensor(turn[:, :, 64:128], raw[:, :, 0:64], sinb[:, :, 64:128], ALU.mult).then_inc(rot_a, 1)
                pool.wait_ge(rot_mid, 2 * (b + 1))
                pool.wait_ge(rot_a, b + 1)
                pool.tensor_tensor(kvr[:, p, :, :], kvr[:, p, :, :], turn[:], ALU.add).then_inc(rot, 1)

            def low_parts(b, u):
                p = u % 2
                wait(pool, sc_ready, NJ * (b - 1))
                pool.tensor_copy(kvT_hi[:, p, 2 * P:LP], g["tailT_hi"][:, bass.ds(b, 1), :]).then_inc(tail_cols, 1)
                pool.tensor_copy(kvT_lo[:, p, 2 * P:LP], g["tailT_lo"][:, bass.ds(b, 1), :]).then_inc(tail_cols, 1)
                pool.wait_ge(q_hi_ok, b + 1)
                pool.tensor_tensor(q_lo[:, p, :], q[:, b, :], q_hi[:, p, :].bitcast(F32), ALU.subtract).then_inc(q_ok, 1)
                pool.wait_ge(kv_hi_ok, b + 1)
                pool.tensor_tensor(kv_lo[:, u, :, :], kvr[:, p, :, :], kv_hi[:, u, :, :].bitcast(F32),
                                   ALU.subtract).then_inc(kv_ok, 1)

            def step(s, u):
                if inside(s, -3):
                    rotate(s + 3, (u + 3) % BPT)
                if inside(s, -2):
                    low_parts(s + 2, (u + 2) % BPT)
            pool.wait_ge(tables, 32)
            rotate(0, 0)
            rotate(1, 1)
            low_parts(0, 0)
            rotate(2, 2)
            low_parts(1, 1)
            run(pool, step)

        @block.tensor
        def _(pe):
            def transpose_context(b, u):
                pe.wait_ge(rot, b + 1)
                wait(pe, kvT_ok, b)
                wait(pe, ptail_ok, b - 3)
                for c in range(2):
                    m = pe.transpose(psum[:, KT, c * P:(c + 1) * P], kvr[:, u % 2, c, :], ident[:])
                m.then_inc(kvT_ready, 1)

            def scores(b, u):
                p = u % 2
                pe.wait_ge(q_ok, b + 1)
                pe.wait_ge(kvT_ok, b + 1)
                pe.wait_ge(tail_cols, 2 * (b + 1))
                for j in range(NJ):
                    wait(pe, exp_ok, NJ * (b - 1) + j + 1)
                    rows = slice(j * P, (j + 1) * P)
                    passes(pe, psum[:, SC + j, 0:LP], q_hi[:, p, rows], q_lo[:, p, rows],
                           kvT_hi[:, p, :], kvT_lo[:, p, :], True, True).then_inc(sc_ready, 1)

            def transpose_probs(b, u):
                p = u % 2
                wait(pe, pt_ok, 2 * b)
                wait(pe, ptail_ok, b)
                pe.wait_ge(kvT_ok, b + 4 if not isinstance(b, int) else min(b + 4, B))
                pe.wait_ge(p_tail, b + 1)
                for j in range(NJ):
                    for c in range(2):
                        pe.transpose(psum[:, PT0 + c, j * P:(j + 1) * P], pr[:, p, j, c * P:(c + 1) * P], ident[:])
                    m = pe.transpose(psum[0:3, KT, j * P:(j + 1) * P], pr[:, p, j, 2 * P:2 * P + 3], ident[:])
                m.then_inc(pt_ready, 1)

            def context(b, u):
                pe.wait_ge(kv_ok, b + 1)
                pe.wait_ge(tail_in[u], 16 * (b // BPT + 1) if isinstance(b, int) else 4 * (b - u) + 16)
                pe.wait_ge(pt_ok, 2 * (b + 1))
                pe.wait_ge(ptail_ok, b + 1)
                wait(pe, c_ok, b)
                for c in range(2):
                    passes(pe, psum[:, CT, :], kv_hi[:, u, c, :], kv_lo[:, u, c, :], pT_hi[:, c, :], pT_lo[:, c, :],
                           c == 0, False)
                pe.matmul(psum[:, CT, :], tail[:, u, :], pT_tail[:], start=False, stop=True).then_inc(c_ready, 1)

            def output(t):
                pe.wait_ge(c_ok, BPT * (t + 1))
                pe.wait_ge(pt_ok, 2 * (BPT * (t + 1) + 1) if not isinstance(t, int) else min(2 * (BPT * (t + 1) + 1), 2 * B))
                for h in range(H):
                    m = passes(pe, psum[:, PT0, :], cT_hi[:, h, :], cT_lo[:, h, :], G_hi[:, h * D:(h + 1) * D],
                               G_lo[:, h * D:(h + 1) * D], h == 0, h == H - 1)
                m.then_inc(o_ready, 1)

            def step(s, u):
                if inside(s, 0):
                    scores(s, u)
                if inside(s, -2):
                    transpose_context(s + 2, (u + 2) % BPT)
                if u == 2 and (not isinstance(s, int) or s >= BPT):
                    t = s // BPT - 1 if isinstance(s, int) else (s - u) // BPT - 1
                    output(t)
                if inside(s, 2):
                    context(s - 2, (u - 2) % BPT)
                if inside(s, 1):
                    if u == 2 and (not isinstance(s, int) or s >= BPT):
                        pe.wait_ge(o_ok, s // BPT if isinstance(s, int) else (s - u) // BPT)
                    transpose_probs(s - 1, (u - 1) % BPT)
            transpose_context(0, 0)
            transpose_context(1, 1)
            run(pe, step)

        @block.scalar
        def _(act):
            def prepare(b, u):
                p = u % 2
                act.wait_ge(kvT_ready, b + 1)
                wait(act, sc_ready, NJ * (b - 1))
                act.activation(kvT_hi[:, p, 0:2 * P], psum[:, KT, 0:2 * P], ACT.Copy).then_inc(kvT_hi_ok, 1)
                act.activation(q_hi[:, p, :], q[:, b, :], ACT.Copy).then_inc(q_hi_ok, 1)

            def context_rows_hi(b, u):
                act.wait_ge(rot, b + 1)
                wait(act, c_ready, b - KVB + 1)
                act.activation(kv_hi[:, u, :, :], kvr[:, u % 2, :, :], ACT.Copy).then_inc(kv_hi_ok, 1)

            def exponentials(b, u):
                p = u % 2
                for j in range(NJ):
                    act.wait_ge(low_ok, NJ * b + j + 1)
                    if j == 0:
                        wait(act, pt_ready, b - 1)
                    act.activation(pr[:, p, j, 0:L], psum[:, SC + j, 0:L], ACT.Exp, bias=low[:, p, j:j + 1],
                                   accum_out=total[:, p, j:j + 1]).then_inc(exp_ok, 1)

            def probs_hi(b, u):
                act.wait_ge(pt_ready, b + 1)
                wait(act, c_ready, b)
                for c in range(2):
                    act.activation(pT_hi[:, c, :], psum[:, PT0 + c, :], ACT.Copy).then_inc(pt_hi_ok, 1)
                act.activation(pT_tail[:], psum[0:3, KT, :], ACT.Copy).then_inc(ptail_ok, 1)

            def context_hi(b, u):
                act.wait_ge(c_ready, b + 1)
                if u == 0:
                    wait(act, o_ready, b // BPT)
                act.activation(cT_hi[:, :, u * S:(u + 1) * S], psum[:, CT, :].rearrange("p (h s) -> p h s", s=S),
                               ACT.Copy).then_inc(c_hi_ok, 1)

            def step(s, u):
                if inside(s, 2):
                    probs_hi(s - 2, (u - 2) % BPT)
                if inside(s, 0):
                    exponentials(s, u)
                if inside(s, -2):
                    prepare(s + 2, (u + 2) % BPT)
                if inside(s, 2):
                    context_hi(s - 2, (u - 2) % BPT)
                if inside(s, -2):
                    context_rows_hi(s + 2, (u + 2) % BPT)
            for b in range(2):
                prepare(b, b)
                context_rows_hi(b, b)
            run(act, step)

        @block.vector
        def _(v):
            def prepare(b, u):
                p = u % 2
                v.wait_ge(kvT_hi_ok, b + 1)
                v.tensor_tensor(kvT_lo[:, p, 0:2 * P], psum[:, KT, 0:2 * P], kvT_hi[:, p, 0:2 * P].bitcast(F32),
                                ALU.subtract).then_inc(kvT_ok, 1)

            def maxima(b, u):
                p = u % 2
                for j in range(NJ):
                    v.wait_ge(sc_ready, NJ * b + j + 1)
                    v.tensor_reduce(low[:, p, j:j + 1], psum[:, SC + j, 0:L], AX_X, ALU.max, negate=True).then_inc(low_ok, 1)

            def normalise(b, u):
                p = u % 2
                v.wait_ge(exp_ok, NJ * (b + 1))
                v.reciprocal(scale[:, p, :], total[:, p, :]).then_inc(inv_ok, 1)
                v.wait_ge(inv_ok, b + 1)
                for j in range(NJ):
                    v.tensor_scalar(pr[:, p, j, 0:L], pr[:, p, j, 0:L], scale[:, p, j:j + 1], None,
                                    ALU.mult).then_inc(pr_ok, 1)
                v.wait_ge(pr_ok, NJ * (b + 1))
                v.tensor_copy(prr[:, p, :, 2 * P + 1:2 * P + 2], pr[:, p, :, 2 * P:2 * P + 1]).then_inc(p_split, 1)
                v.wait_ge(p_split, 2 * b + 1)
                v.tensor_tensor(pr[:, p, :, 2 * P + 2:2 * P + 3], pr[:, p, :, 2 * P:2 * P + 1],
                                pr[:, p, :, 2 * P + 1:2 * P + 2], ALU.subtract).then_inc(p_split, 1)
                v.wait_ge(p_split, 2 * b + 2)
                v.tensor_copy(pr[:, p, :, 2 * P:2 * P + 1], pr[:, p, :, 2 * P + 1:2 * P + 2]).then_inc(p_tail, 1)

            def probs_lo(b, u):
                for c in range(2):
                    v.wait_ge(pt_hi_ok, 2 * b + c + 1)
                    v.tensor_tensor(pT_lo[:, c, :], psum[:, PT0 + c, :], pT_hi[:, c, :].bitcast(F32),
                                    ALU.subtract).then_inc(pt_ok, 1)

            def context_lo(b, u):
                v.wait_ge(c_hi_ok, b + 1)
                cols = slice(u * S, (u + 1) * S)
                v.tensor_tensor(cT_lo[:, :, cols], psum[:, CT, :].rearrange("p (h s) -> p h s", s=S),
                                cT_hi[:, :, cols].bitcast(F32), ALU.subtract).then_inc(c_ok, 1)

            def step(s, u):
                if inside(s, 2):
                    probs_lo(s - 2, (u - 2) % BPT)
                if inside(s, 0):
                    maxima(s, u)
                if inside(s, -2):
                    prepare(s + 2, (u + 2) % BPT)
                if inside(s, 0):
                    normalise(s, u)
                if u == 2 and (not isinstance(s, int) or s >= BPT):
                    t = s // BPT - 1 if isinstance(s, int) else (s - u) // BPT - 1
                    v.wait_ge(o_ready, t + 1)
                    v.tensor_tensor(x[:, bass.ds(t, 1), :], x[:, bass.ds(t, 1), :],
                                    psum[:, PT0:PT0 + 1, :], ALU.add).then_inc(o_ok, 1)
                if inside(s, 2):
                    context_lo(s - 2, (u - 2) % BPT)
            prepare(0, 0)
            prepare(1, 1)
            run(v, step)


def phase_store(nc, d, g):
    with ExitStack() as ctx:
        n = Names(nc, ctx, "store")
        stored = n.sem("stored")
        block = ctx.enter_context(nc.Block())

        @block.sync
        def _(sp):
            sp.dma_start(d["out"].rearrange("(t p) d -> p t d", p=P), g["x"][:]).then_inc(stored, 16)
            sp.wait_ge(stored, 16)


DI, HD, NST, NH, NX = 1024, 64, 64, 16, 4
REP = NH // NX
FOLDS = 3
ZC = DI // P
FEATS = 2 * ZC + 4
Z0, C0, X0, B0 = 0, ZC, 2 * ZC, 2 * ZC + 2


LOW = 32
TINY = 2.0 ** -126


def project_programs(nc, n, d, g, mlp, feat, bias, cumS):
    psum, xT_hi, xT_lo, ident = g["psum"], g["xT_hi"], g["xT_lo"], g["ident"]
    DTT, DT, CM, TR = 4, 6, 7, 4
    n = Names(nc, n.ctx, "proj")
    raw, w_hi, w_lo = mlp.raw1[:, 0, :, :], mlp.w1_hi[:, 0, 0, :, :], mlp.w1_lo[:, 0, 0, :, :]
    slot = [slice(0, P), slice(P, 2 * P)]
    wdt = n.sb("wdt", [P, DC, NH])
    wdt_hi, wdt_lo = n.sb("wdt_hi", [P, DC, NH], F32R), n.sb("wdt_lo", [P, DC, NH], F32R)
    head = n.sb("head", [P, 2, TT, NH])
    tri = n.sb("tri", [P, P])
    b2 = mlp.raw2[:, 0, :]
    negA, pre, mag, u, w1, wm, dt, lndt = (n.sb(x, [P, TT, NH]) for x in ("negA", "pre", "mag", "u", "w1", "wm", "dt", "lndt"))
    cum = n.sb("cum", [P, TT, LOW + NH])
    cumT_hi = mlp.h_hi[0:LOW + NH, 0, :]
    dtT = mlp.s1[0:NH, :, :]
    loaded, w_hi_ok, w_ok, f_ready, f_kept = [n.sem("loaded0"), n.sem("loaded1")], n.sem("w_hi_ok"), n.sem("w_ok"), n.sem("f_ready"), n.sem("f_kept")
    small, dt_w, dt_ready, b2_in, x_plus = n.sem("small"), n.sem("dt_w"), n.sem("dt_ready"), n.sem("b2_in"), n.sem("x_plus")
    dtT_ready, dtT_ok = n.sem("dtT_ready"), n.sem("dtT_ok")
    chain, a_chain, zeros = n.sem("chain"), n.sem("a_chain"), n.sem("zeros")
    cum_ready, cum_ok, cumT_ready, cumT_hi_ok, cumS_ok = (n.sem(x) for x in ("cum_ready", "cum_ok", "cumT_ready", "cumT_hi_ok", "cumS_ok"))
    EARLY = 8

    def sync_first(sp):
        for dst, src in ((wdt[:], d["w_dt"]), (head[:], d["head"]), (tri[:], d["tri"])):
            sp.dma_start(dst, src).then_inc(small, 16)

    def sync(sp):
        def load(k, p):
            wait(sp, w_ok, k - 1)
            sp.dma_start(raw[:, :, slot[p]], d["w_feat"][k]).then_inc(loaded[p], 16)
        sp.wait_ge(mlp.w_ok, mlp.all_split)
        load(0, 0)
        load(1, 1)
        sp.dma_start(b2, d["fc2_b"]).then_inc(b2_in, 16)
        with sp.Fori(1, FEATS // 2) as i:
            load(2 * i, 0)
            load(2 * i + 1, 1)

    def gpsimd(pool):
        pool.memset(cumS[:].bitcast(F32), 0.0).then_inc(zeros, 1)
        pool.memset(cum[:], 0.0).then_inc(zeros, 1)
        pool.wait_ge(b2_in, 16)
        pool.wait_ge(mlp.dn_ok, mlp.all_down)
        for t in range(TT):
            pool.tensor_tensor(g["x"][:, t, :], g["x"][:, t, :], b2, ALU.add).then_inc(x_plus, 1)

    def tensor(pe):
        def chunk(k, p):
            pe.wait_ge(w_ok, k + 1)
            for half in range(NHALF):
                bank = 2 * p + half
                wait(pe, f_kept, 2 * (k - 2) + half + 1)
                cols = slice(half * HALF, (half + 1) * HALF)
                for c in range(DC):
                    m = passes(pe, psum[:, bank, :], w_hi[:, c, slot[p]], w_lo[:, c, slot[p]],
                               xT_hi[:, c, cols], xT_lo[:, c, cols], c == 0, c == DC - 1)
                m.then_inc(f_ready, 1)
        pe.wait_ge(mlp.act_ok, mlp.all_up)
        for k in range(EARLY):
            chunk(k, k % 2)
            if k == 0:
                pe.wait_ge(mlp.dn_ok, mlp.all_down)
                pe.wait_ge(dt_w, 2)
                for half in range(NHALF):
                    cols = slice(half * HALF, (half + 1) * HALF)
                    for c in range(DC):
                        m = passes(pe, psum[0:NH, DTT + half, :], wdt_hi[:, c, :], wdt_lo[:, c, :],
                                   xT_hi[:, c, cols], xT_lo[:, c, cols], c == 0, c == DC - 1)
                m.then_inc(dtT_ready, 1)
            if k == 1:
                pe.wait_ge(dtT_ok, 1)
                for t in range(TT):
                    m = pe.transpose(psum[:, DT, t * NH:(t + 1) * NH], dtT[:, t // 4, (t % 4) * P:(t % 4 + 1) * P], ident[0:NH, 0:NH])
                m.then_inc(dt_ready, 1)
            if k == 3:
                pe.wait_ge(chain, DT_STEPS)
                pe.matmul(psum[:, CM, 0:TT * NH], tri[:], pre[:].rearrange("p t h -> p (t h)"), start=True,
                          stop=True).then_inc(cum_ready, 1)
            if k == 5:
                pe.wait_ge(cum_ok, 2)
                for t in range(TT):
                    m = pe.transpose(psum[0:LOW + NH, TR + t // 4, (t % 4) * P:(t % 4 + 1) * P], cum[:, t, :], ident[:])
                m.then_inc(cumT_ready, 1)
        with pe.Fori(EARLY // 2, FEATS // 2) as i:
            chunk(2 * i, 0)
            chunk(2 * i + 1, 1)

    def split_hi(act, k, p):
        act.wait_ge(loaded[p], 16 * (k // 2 + 1) if isinstance(k, int) else 8 * (k - p) + 16)
        wait(act, f_ready, 2 * (k - 1))
        act.activation(w_hi[:, :, slot[p]], raw[:, :, slot[p]], ACT.Copy).then_inc(w_hi_ok, 1)

    def scalar_first(act):
        act.wait_ge(mlp.dn_ready, mlp.all_down - TT)
        split_hi(act, 0, 0)
        split_hi(act, 1, 1)

    def scalar(act):
        def keep_z(k, p):
            for half in range(NHALF):
                act.wait_ge(f_ready, 2 * k + half + 1)
                act.activation(feat[:, k, half * HALF:(half + 1) * HALF], psum[:, 2 * p + half, :],
                               ACT.Silu).then_inc(f_kept, 1)

        def keep(k, p):
            for half in range(NHALF):
                act.wait_ge(f_ready, 2 * k + half + 1)
                act.activation(feat[:, bass.ds(k, 1), half * HALF:(half + 1) * HALF],
                               psum[:, 2 * p + half:2 * p + half + 1, :], ACT.Copy).then_inc(f_kept, 1)
        for k in range(ZC):
            keep_z(k, k % 2)
            split_hi(act, k + 2, k % 2)
            if k == 0:
                act.wait_ge(dtT_ready, 1)
                act.activation(dtT, psum[0:NH, DTT:DTT + NHALF, :], ACT.Copy).then_inc(dtT_ok, 1)
            if k == 1:
                act.wait_ge(small, 48)
                act.activation(negA[:], head[:, 1, :, :], ACT.Exp).then_inc(a_chain, 1)
                act.wait_ge(chain, 2)
                act.activation(u[:], mag[:], ACT.Exp, scale=-1.0).then_inc(a_chain, 1)
                act.wait_ge(chain, 3)
                act.activation(wm[:], w1[:], ACT.Ln).then_inc(a_chain, 1)
                act.wait_ge(chain, DT_STEPS)
                act.activation(lndt[:], w1[:], ACT.Ln).then_inc(a_chain, 1)
        with act.Fori(ZC // 2, FEATS // 2 - 1) as i:
            for p in range(2):
                keep(2 * i + p, p)
                split_hi(act, 2 * i + p + 2, p)
        keep(FEATS - 2, 0)
        keep(FEATS - 1, 1)

    def split(v, k, p):
        v.wait_ge(w_hi_ok, k + 1)
        v.tensor_tensor(w_lo[:, :, slot[p]], raw[:, :, slot[p]], w_hi[:, :, slot[p]].bitcast(F32),
                        ALU.subtract).then_inc(w_ok, 1)

    def vector_first(v):
        split(v, 0, 0)
        split(v, 1, 1)
        v.wait_ge(small, 48)
        v.tensor_copy(wdt_hi[:], wdt[:]).then_inc(dt_w, 1)
        v.wait_ge(dt_w, 1)
        v.tensor_tensor(wdt_lo[:], wdt[:], wdt_hi[:].bitcast(F32), ALU.subtract).then_inc(dt_w, 1)

    def vector(v):
        steps = [0]

        def link(i):
            steps[0] += 1
            i.then_inc(chain, 1)
            v.wait_ge(chain, steps[0])

        def dt_path():
            v.wait_ge(dt_ready, 1)
            link(v.tensor_tensor(pre[:], psum[:, DT, 0:TT * NH].rearrange("p (t h) -> p t h", h=NH), head[:, 0, :, :], ALU.add))
            link(v.scalar_tensor_tensor(out=mag[:], in0=pre[:], scalar=-1.0, in1=pre[:], op0=ALU.mult, op1=ALU.max))
            v.wait_ge(a_chain, 2)
            link(v.tensor_scalar(w1[:], u[:], 1.0, None, ALU.add))
            link(v.tensor_scalar(mag[:], w1[:], -1.0, None, ALU.add))
            v.wait_ge(a_chain, 3)
            link(v.tensor_tensor(wm[:], wm[:], u[:], ALU.mult))
            link(v.tensor_scalar(w1[:], mag[:], 0.0, None, ALU.is_equal))
            link(v.tensor_tensor(mag[:], mag[:], w1[:], ALU.add))
            link(v.reciprocal(mag[:], mag[:]))
            link(v.tensor_tensor(wm[:], wm[:], mag[:], ALU.mult))
            link(v.tensor_tensor(w1[:], w1[:], u[:], ALU.mult))
            link(v.tensor_tensor(wm[:], wm[:], w1[:], ALU.add))
            link(v.scalar_tensor_tensor(out=dt[:], in0=pre[:], scalar=0.0, in1=wm[:], op0=ALU.max, op1=ALU.add))
            link(v.scalar_tensor_tensor(out=pre[:], in0=dt[:], scalar=-1.0, in1=negA[:], op0=ALU.mult, op1=ALU.mult))
            link(v.tensor_scalar(w1[:], dt[:], TINY, None, ALU.max))
            assert steps[0] == DT_STEPS

        def keep_cum():
            v.wait_ge(cum_ready, 1)
            v.wait_ge(a_chain, 4)
            v.wait_ge(zeros, 2)
            sums = psum[:, CM, 0:TT * NH].rearrange("p (t h) -> p t h", h=NH)
            v.tensor_copy(cum[:, :, 0:NH], sums).then_inc(cum_ok, 1)
            v.tensor_copy(cum[:, :, LOW:LOW + NH], sums).then_inc(cum_ok, 1)
            v.tensor_tensor(bias[:], lndt[:], sums, ALU.subtract).then_inc(cum_ok, 1)

        def split_cumT():
            both = psum[0:LOW + NH, TR:TR + 2, :].rearrange("h b k -> h (b k)")
            v.wait_ge(cumT_ready, 1)
            v.tensor_copy(cumT_hi, both).then_inc(cumT_hi_ok, 1)
            v.wait_ge(cumT_hi_ok, 1)
            v.tensor_copy(cumS[0:NH, :], cumT_hi[0:NH, :].bitcast(F32)).then_inc(cumS_ok, 1)
            v.tensor_tensor(cumS[LOW:LOW + NH, :], both[LOW:LOW + NH, :], cumT_hi[LOW:LOW + NH, :].bitcast(F32),
                            ALU.subtract).then_inc(cumS_ok, 1)
        for k in range(2, EARLY):
            split(v, k, k % 2)
            if k == 3:
                dt_path()
            if k == 5:
                keep_cum()
            if k == 7:
                split_cumT()
        with v.Fori(EARLY // 2, FEATS // 2) as i:
            split(v, 2 * i, 0)
            split(v, 2 * i + 1, 1)
    made = Parts()
    made.sync_first, made.scalar_first, made.vector_first = sync_first, scalar_first, vector_first
    made.sync, made.gpsimd, made.tensor, made.scalar, made.vector = sync, gpsimd, tensor, scalar, vector
    return made


DT_STEPS = 14


def phase_scan(nc, d, g, feat, bias, cumS):
    psum, ident, x = g["psum"], g["ident"], g["x"]
    CU, SB, YB, OB, MB = 0, 2, 4, 6, 7
    with ExitStack() as ctx:
        n = Names(nc, ctx, "scan")
        wo_raw = n.sb("wo_raw", [P, 2, D])
        wo_hi, wo_lo = n.sb("wo_hi", [P, ZC, D], F32R), n.sb("wo_lo", [P, ZC, D], F32R)
        nw, dcol = n.sb("nw", [P, ZC]), n.sb("dcol", [P, ZC])
        mask = n.sb("mask", [P, P])
        masks, ident_r = n.sb("masks", [P, REP, P], F32R), n.sb("ident_r", [P, P], F32R)
        pick = n.sb("pick", [P, NH], F32R)
        ones = n.sb("ones", [P, 2])
        power, ms, rs = n.sb("power", [P, 1]), n.sb("ms", [P, 2]), n.sb("rs", [P, 2])
        C_hi, C_lo = n.sb("C_hi", [P, 2, ZC, P], F32R), n.sb("C_lo", [P, 2, ZC, P], F32R)
        B_hi, B_lo = n.sb("B_hi", [P, 2, 2, P], F32R), n.sb("B_lo", [P, 2, 2, P], F32R)
        xs, tbias = n.sb("xs", [P, 2, P]), n.sb("tbias", [P, 2, NH])
        xt_hi, xt_lo = n.sb("xt_hi", [P, 2, 2 * P], F32R), n.sb("xt_lo", [P, 2, 2 * P], F32R)
        E = n.sb("E", [P, 2, REP, P])
        W_hi, W_lo = n.sb("W_hi", [P, 2, REP, P], F32R), n.sb("W_lo", [P, 2, REP, P], F32R)
        skip = n.sb("skip", [P, 2, REP, P])
        y = n.sb("y", [P, 2, REP, P])
        sq, folded = n.sb("sq", [P, ZC, P]), n.sb("folded", [P, ZC // 2, P])
        y_hi, y_lo = n.sb("y_hi", [P, ZC, P], F32R), n.sb("y_lo", [P, ZC, P], F32R)
        S_ = n.sem
        consts, wo_in, wo_hi_ok, wo_ok, set_up = S_("consts"), [S_("wo_in0"), S_("wo_in1")], S_("wo_hi_ok"), S_("wo_ok"), S_("set_up")
        consts_r = S_("consts_r")
        fold_ok = S_("fold_ok")
        cb_hi_ok, cb_ok, xs_ok, tbias_ok, xt_ready, xt_hi_ok, xt_ok = (S_(k) for k in (
            "cb_hi_ok", "cb_ok", "xs_ok", "tbias_ok", "xt_ready", "xt_hi_ok", "xt_ok"))
        cu_ready, s_ready, e_ok, w_ok, whi_ok, wlo_ok, skip_ok = (S_(k) for k in (
            "cu_ready", "s_ready", "e_ok", "w_ok", "whi_ok", "wlo_ok", "skip_ok"))
        y_ready, yd_ok, yg_ok, sq_ok, yhi_ok, ylo_ok = (S_(k) for k in ("y_ready", "yd_ok", "yg_ok", "sq_ok", "yhi_ok", "ylo_ok"))
        ss_ready, ms_ok, rs_ok, o_ready, o_ok = (S_(k) for k in ("ss_ready", "ms_ok", "rs_ok", "o_ready", "o_ok"))
        block = ctx.enter_context(nc.Block())

        def run(e, slot):
            for t in range(3):
                for k in range(NX):
                    slot(t, t % 2, k)
            with e.Fori(1, TT // 2 - 1) as i:
                for k in range(NX):
                    slot(2 * i + 1, 1, k)
                for k in range(NX):
                    slot(2 * i + 2, 0, k)
            for k in range(NX):
                slot(TT - 1, 1, k)

        def ahead(f, t, p, k, steps):
            c, k = divmod(k + steps, NX)
            if not (isinstance(t, int) and t + c >= TT):
                f(t + c, (p + c) % 2, k)

        def another(t):
            return not (isinstance(t, int) and t == TT - 1)

        def earlier(t):
            return not (isinstance(t, int) and t == 0)

        @block.sync
        def _(sp):
            for dst, src in ((nw[:], d["norm_w"]), (dcol[:], d["d_skip"]), (mask[:], d["mask"])):
                sp.dma_start(dst, src).then_inc(consts, 16)
            for c in range(ZC):
                wait(sp, wo_ok, c - 1)
                sp.dma_start(wo_raw[:, c % 2, :], d["w_out"][c]).then_inc(wo_in[c % 2], 16)

        @block.gpsimd
        def _(pool):
            pool.memset(power[:], -0.5).then_inc(set_up, 1)
            pool.memset(ones[:], 1.0).then_inc(set_up, 1)

            def copy_x(t):
                wait(pool, xt_ready, t)
                wait(pool, skip_ok, 2 * t)
                pool.tensor_copy(xs[:], feat[:, X0:X0 + 2, bass.ds(t * P, P)]).then_inc(xs_ok, 1)

            def split_cb(t, p):
                pool.wait_ge(cb_hi_ok, 2 * t + 1)
                pool.tensor_tensor(C_lo[:, p, :, :], feat[:, C0:C0 + ZC, bass.ds(t * P, P)], C_hi[:, p, :, :].bitcast(F32),
                                   ALU.subtract).then_inc(cb_ok, 1)
                pool.wait_ge(cb_hi_ok, 2 * t + 2)
                pool.tensor_tensor(B_lo[:, p, :, :], feat[:, B0:B0 + 2, bass.ds(t * P, P)], B_hi[:, p, :, :].bitcast(F32),
                                   ALU.subtract).then_inc(cb_ok, 1)

            def skip_path(t, m):
                wait(pool, yg_ok, 2 * t + m - 1)
                pool.wait_ge(xs_ok, t + 1)
                pool.tensor_tensor(skip[:, m, :, :], xs[:, m, :].rearrange("p (o t) -> p o t", o=1).to_broadcast([P, REP, P]),
                                   feat[:, REP * m:REP * (m + 1), bass.ds(t * P, P)], ALU.mult).then_inc(skip_ok, 1)

            def fold_squares(t):
                pool.wait_ge(sq_ok, 2 * (t + 1))
                wait(pool, ss_ready, t)
                steps, half, src = 0, ZC // 2, sq
                while half >= 1:
                    if steps:
                        pool.wait_ge(fold_ok, FOLDS * t + steps)
                    pool.tensor_tensor(folded[:, 0:half, :], src[:, 0:half, :], src[:, half:2 * half, :], ALU.add).then_inc(fold_ok, 1)
                    steps, half, src = steps + 1, half // 2, folded

            def root(t, p):
                pool.wait_ge(ms_ok, t + 1)
                wait(pool, o_ok, t - 1)
                pool.tensor_tensor(rs[:, p:p + 1], ms[:, p:p + 1], power[:], ALU.pow).then_inc(rs_ok, 1)

            def slot(t, p, k):
                if k == 0 and earlier(t):
                    fold_squares(t - 1)
                if k == 0 and another(t):
                    split_cb(t + 1, 1 - p)
                if k == 1:
                    skip_path(t, 1)
                    if another(t):
                        copy_x(t + 1)
                if k == 2 and earlier(t):
                    root(t - 1, 1 - p)
                if k == 3 and another(t):
                    skip_path(t + 1, 0)
            copy_x(0)
            split_cb(0, 0)
            skip_path(0, 0)
            pool.wait_ge(set_up, 2)
            run(pool, slot)
            fold_squares(TT - 1)
            root(TT - 1, 1)

        @block.scalar
        def _(act):
            def out_weight(c):
                act.wait_ge(wo_in[c % 2], 16 * (c // 2 + 1))
                act.activation(wo_hi[:, c, :], wo_raw[:, c % 2, :], ACT.Copy, scale=nw[:, c:c + 1]).then_inc(wo_hi_ok, 1)

            def cb_hi(t, p):
                wait(act, s_ready, NX * (t - 1))
                act.activation(C_hi[:, p, :, :], feat[:, C0:C0 + ZC, bass.ds(t * P, P)], ACT.Copy).then_inc(cb_hi_ok, 1)
                act.activation(B_hi[:, p, :, :], feat[:, B0:B0 + 2, bass.ds(t * P, P)], ACT.Copy).then_inc(cb_hi_ok, 1)

            def x_hi(t, p):
                act.wait_ge(xt_ready, t + 1)
                wait(act, y_ready, NX * (t - 1))
                act.activation(xt_hi[:, p, :], psum[:, MB, 0:2 * P], ACT.Copy).then_inc(xt_hi_ok, 1)

            def exponentials(t, p, k):
                act.wait_ge(cu_ready, NX * t + k + 1)
                act.wait_ge(tbias_ok, t + 1)
                wait(act, wlo_ok, NX * t + k - 1)
                for j in range(REP):
                    h = k * REP + j
                    i = act.activation(E[:, k % 2, j, :], psum[:, CU + k % 2, j * P:(j + 1) * P], ACT.Exp,
                                       bias=tbias[:, p, h:h + 1])
                i.then_inc(e_ok, 1)

            def weights_hi(t, p, k):
                act.wait_ge(w_ok, NX * t + k + 1)
                wait(act, y_ready, NX * t + k - 1)
                act.activation(W_hi[:, k % 2, :, :], E[:, k % 2, :, :], ACT.Copy).then_inc(whi_ok, 1)

            def gated(t, m):
                act.wait_ge(yg_ok, 2 * t + m + 1)
                wait(act, o_ready, 2 * t + m - 1)
                act.activation(y_hi[:, REP * m:REP * (m + 1), :], y[:, m, :, :], ACT.Copy).then_inc(yhi_ok, 1)
                wait(act, fold_ok, FOLDS * t)
                act.activation(sq[:, REP * m:REP * (m + 1), :], y[:, m, :, :], ACT.Square).then_inc(sq_ok, 1)

            def slot(t, p, k):
                ahead(exponentials, t, p, k, 2)
                ahead(weights_hi, t, p, k, 1)
                if k == 0:
                    if earlier(t):
                        gated(t - 1, 1)
                    else:
                        for c in range(ZC // 2):
                            out_weight(c)
                    if another(t):
                        cb_hi(t + 1, 1 - p)
                if k == 1 and not earlier(t):
                    for c in range(ZC // 2, ZC):
                        out_weight(c)
                if k == 2:
                    gated(t, 0)
                    if another(t):
                        x_hi(t + 1, 1 - p)
            cb_hi(0, 0)
            x_hi(0, 0)
            exponentials(0, 0, 0)
            weights_hi(0, 0, 0)
            exponentials(0, 0, 1)
            act.wait_ge(consts, 48)
            run(act, slot)
            gated(TT - 1, 1)

        @block.vector
        def _(v):
            v.wait_ge(consts, 48)
            v.tensor_tensor(pick[:], ident[:, 0:NH], ident[:, LOW:LOW + NH], ALU.add).then_inc(consts_r, 1)
            v.tensor_copy(ident_r[:], ident[:]).then_inc(consts_r, 1)
            for j in range(REP):
                v.tensor_copy(masks[:, j, :], mask[:]).then_inc(consts_r, 1)

            def out_weight(c):
                v.wait_ge(wo_hi_ok, c + 1)
                v.scalar_tensor_tensor(out=wo_lo[:, c, :], in0=wo_raw[:, c % 2, :], scalar=nw[:, c:c + 1],
                                       in1=wo_hi[:, c, :].bitcast(F32), op0=ALU.mult, op1=ALU.subtract).then_inc(wo_ok, 1)

            def tile_bias(t, p):
                wait(v, e_ok, NX * (t - 1))
                v.tensor_copy(tbias[:, p:p + 1, :], bias[:, bass.ds(t, 1), :]).then_inc(tbias_ok, 1)

            def x_lo(t, p):
                v.wait_ge(xt_hi_ok, t + 1)
                v.tensor_tensor(xt_lo[:, p, :], psum[:, MB, 0:2 * P], xt_hi[:, p, :].bitcast(F32), ALU.subtract).then_inc(xt_ok, 1)

            def weigh(t, p, k):
                v.wait_ge(e_ok, NX * t + k + 1)
                v.wait_ge(s_ready, NX * t + k + 1)
                v.tensor_tensor(E[:, k % 2, :, :], psum[:, SB + k % 2, :].rearrange("p (j t) -> p j t", j=REP),
                                E[:, k % 2, :, :], ALU.mult).then_inc(w_ok, 1)

            def weights_lo(t, p, k):
                v.wait_ge(whi_ok, NX * t + k + 1)
                v.tensor_tensor(W_lo[:, k % 2, :, :], E[:, k % 2, :, :], W_hi[:, k % 2, :, :].bitcast(F32),
                                ALU.subtract).then_inc(wlo_ok, 1)

            def gate(t, m):
                v.wait_ge(y_ready, NX * t + 2 * m + 2)
                wait(v, sq_ok, 2 * t + m - 1)
                wait(v, ylo_ok, 2 * t + m - 1)
                for r in range(2):
                    rows = slice(64 * r, 64 * (r + 1))
                    i = v.tensor_tensor(y[rows, m, :, :], psum[rows, YB + r, :].rearrange("p (j t) -> p j t", j=REP),
                                        feat[rows, REP * m:REP * (m + 1), bass.ds(t * P, P)], ALU.mult)
                i.then_inc(yd_ok, 1)
                v.wait_ge(yd_ok, 2 * t + m + 1)
                v.wait_ge(skip_ok, 2 * t + m + 1)
                for j in range(REP):
                    c = REP * m + j
                    i = v.scalar_tensor_tensor(out=y[:, m, j, :], in0=skip[:, m, j, :], scalar=dcol[:, c:c + 1],
                                               in1=y[:, m, j, :], op0=ALU.mult, op1=ALU.add)
                i.then_inc(yg_ok, 1)

            def gated_lo(t, m):
                v.wait_ge(yhi_ok, 2 * t + m + 1)
                v.tensor_tensor(y_lo[:, REP * m:REP * (m + 1), :], y[:, m, :, :],
                                y_hi[:, REP * m:REP * (m + 1), :].bitcast(F32), ALU.subtract).then_inc(ylo_ok, 1)

            def mean_square(t, p):
                v.wait_ge(ss_ready, t + 1)
                v.tensor_scalar(ms[:, p:p + 1], psum[:, MB, 256:257], 1.0 / DI, EPS, ALU.mult, ALU.add).then_inc(ms_ok, 1)

            def add_to_x(t, p):
                v.wait_ge(o_ready, 2 * (t + 1))
                v.wait_ge(rs_ok, t + 1)
                v.scalar_tensor_tensor(out=x[:, bass.ds(t, 1), :], in0=psum[:, OB:OB + 1, :], scalar=rs[:, p:p + 1],
                                       in1=x[:, bass.ds(t, 1), :], op0=ALU.mult, op1=ALU.add).then_inc(o_ok, 1)

            def slot(t, p, k):
                ahead(weigh, t, p, k, 1)
                if k == 0 and another(t):
                    tile_bias(t + 1, 1 - p)
                if k == 0 and earlier(t):
                    gate(t - 1, 1)
                if k == 2:
                    gate(t, 0)
                if k == 2 and earlier(t):
                    add_to_x(t - 1, 1 - p)
                ahead(weights_lo, t, p, k, 1)
                if not earlier(t) and k < 2:
                    for c in range(k * ZC // 2, (k + 1) * ZC // 2):
                        out_weight(c)
                if k == 0 and earlier(t):
                    gated_lo(t - 1, 1)
                if k == 1 and earlier(t):
                    mean_square(t - 1, 1 - p)
                if k == 2:
                    gated_lo(t, 0)
                if k == 3 and another(t):
                    x_lo(t + 1, 1 - p)
            tile_bias(0, 0)
            x_lo(0, 0)
            weigh(0, 0, 0)
            weights_lo(0, 0, 0)
            run(v, slot)
            gate(TT - 1, 1)
            gated_lo(TT - 1, 1)
            mean_square(TT - 1, 1)
            add_to_x(TT - 1, 1)

        @block.tensor
        def _(pe):
            def transpose_x(t):
                pe.wait_ge(xs_ok, t + 1)
                wait(pe, ms_ok, t - 1)
                for c in range(2):
                    m = pe.transpose(psum[:, MB, c * P:(c + 1) * P], xs[:, c, :], ident[:])
                m.then_inc(xt_ready, 1)

            def sums(t, p, k):
                wait(pe, e_ok, NX * t + k - 1)
                bank = psum[:, CU + k % 2, :]
                pe.matmul(bank, ident_r[:], masks[:].rearrange("p j t -> p (j t)"), start=True, stop=False)
                for j in range(REP):
                    h = k * REP + j
                    i = pe.matmul(bank[:, j * P:(j + 1) * P], pick[:, h:h + 1].to_broadcast([P, P]),
                                  cumS[:, bass.ds(t * P, P)], start=False, stop=j == REP - 1)
                i.then_inc(cu_ready, 1)

            def scores(t, p, k):
                pe.wait_ge(cb_ok, 2 * (t + 1))
                wait(pe, w_ok, NX * t + k - 1)
                r, m = 64 * (k % 2), k // 2
                rows, ch = slice(r, r + 64), slice(REP * m, REP * (m + 1))
                passes(pe, psum[:, SB + k % 2, :], B_hi[rows, p, m, :], B_lo[rows, p, m, :], C_hi[rows, p, ch, :],
                       C_lo[rows, p, ch, :], True, True).then_inc(s_ready, 1)

            def outputs(t, p, k):
                pe.wait_ge(xt_ok, t + 1)
                pe.wait_ge(wlo_ok, NX * t + k + 1)
                wait(pe, yd_ok, 2 * t + k // 2)
                cols = slice((k // 2) * P, (k // 2 + 1) * P)
                passes(pe, psum[:, YB + k % 2, :], xt_hi[:, p, cols], xt_lo[:, p, cols], W_hi[:, k % 2, :, :],
                       W_lo[:, k % 2, :, :], True, True).then_inc(y_ready, 1)

            def project(t, m):
                pe.wait_ge(ylo_ok, 2 * t + m + 1)
                if m == 0:
                    wait(pe, o_ok, t)
                for c in range(REP * m, REP * (m + 1)):
                    i = passes(pe, psum[:, OB, :], y_hi[:, c, :], y_lo[:, c, :], wo_hi[:, c, :], wo_lo[:, c, :],
                               c == 0, c == ZC - 1)
                i.then_inc(o_ready, 1)

            def squares(t):
                pe.wait_ge(fold_ok, FOLDS * (t + 1))
                pe.wait_ge(xt_ok, min(t + 2, TT) if isinstance(t, int) else t + 2)
                pe.matmul(psum[:, MB, 256:257], folded[:, 0, :], ones[:, 0:1], start=True, stop=True).then_inc(ss_ready, 1)

            def slot(t, p, k):
                ahead(sums, t, p, k, 3)
                ahead(scores, t, p, k, 2)
                if k == 2 and another(t):
                    transpose_x(t + 1)
                outputs(t, p, k)
                if k == 1 and earlier(t):
                    squares(t - 1)
                    project(t - 1, 1)
                if k == 3:
                    if not earlier(t):
                        pe.wait_ge(wo_ok, ZC)
                    project(t, 0)
            pe.wait_ge(set_up, 2)
            transpose_x(0)
            pe.wait_ge(consts_r, REP + 2)
            sums(0, 0, 0)
            sums(0, 0, 1)
            scores(0, 0, 0)
            sums(0, 0, 2)
            scores(0, 0, 1)
            run(pe, slot)
            squares(TT - 1)
            project(TT - 1, 1)


MG, MC = 8, 2


def phase_ffn(nc, d, g, tag, groups, widths, gated, w1_names, w2_name, tok_w=None, bias=None,
              make_norm=None, make_route=None, make_after=None):
    psum, x, xT_hi, xT_lo = g["psum"], g["x"], g["xT_hi"], g["xT_lo"]
    NC, F, NW = len(widths), sum(widths), len(w1_names)
    UP, DN = 0, 4
    with ExitStack() as ctx:
        n = Names(nc, ctx, tag)
        raw1 = n.sb("raw1", [P, NW, DC, F])
        raw2 = n.sb("raw2", [P, NC, D])
        w1_hi, w1_lo = n.sb("w1_hi", [P, 2, NW, DC, F], F32R), n.sb("w1_lo", [P, 2, NW, DC, F], F32R)
        w2_hi, w2_lo = n.sb("w2_hi", [P, 2, NC, D], F32R), n.sb("w2_lo", [P, 2, NC, D], F32R)
        side = n.sb("side", [P, 2, TT])
        h_hi, h_lo = n.sb("h_hi", [P, NC, TOK], F32R), n.sb("h_lo", [P, NC, TOK], F32R)
        s1 = n.sb("s1", [P, 2, HALF])
        hh = n.sb("hh", [P, 2, HALF]) if gated else s1
        if bias is not None:
            b_all = n.sb("b_all", [P, groups, NC])
        S_ = n.sem
        bias_in, in1, in2 = S_("bias_in"), S_("in1"), S_("in2")
        w_hi_ok, w_ok, side_ok = S_("w_hi_ok"), S_("w_ok"), S_("side_ok")
        up_ready, act_ok, hh_ok, hhi_ok, h_ok = S_("up_ready"), S_("act_ok"), S_("hh_ok"), S_("hhi_ok"), S_("h_ok")
        dn_ready, dn_ok = S_("dn_ready"), S_("dn_ok")
        NWS = NW + 1
        U = NC * NHALF
        UB = 4 // NW
        norm = make_norm(n)
        route = make_route(n) if make_route else None
        after = None
        if make_after:
            own = Parts()
            own.raw1, own.raw2, own.w1_hi, own.w1_lo, own.h_hi, own.s1 = raw1, raw2, w1_hi, w1_lo, h_hi, s1
            own.w_ok, own.act_ok, own.dn_ready, own.dn_ok = w_ok, act_ok, dn_ready, dn_ok
            own.all_split, own.all_up, own.all_down = NWS * groups, U * groups, TT * groups
            after = make_after(n, own)
        block = ctx.enter_context(nc.Block())

        def is_last(k):
            return isinstance(k, int) and k == groups - 1

        def is_first(k):
            return isinstance(k, int) and k == 0

        def loop(e, group):
            group(0, 0)
            group(1, 1)
            if groups > 4:
                with e.Fori(1, groups // 2 - 1) as i:
                    group(2 * i, 0)
                    group(2 * i + 1, 1)
            group(groups - 2, 0)
            group(groups - 1, 1)

        @block.sync
        def _(sp):
            if bias is not None:
                sp.dma_start(b_all[:], d[bias]).then_inc(bias_in, 16)

            def load(k):
                wait(sp, w_ok, NWS * k)
                for i, name in enumerate(w1_names):
                    sp.dma_start(raw1[:, i, :, :], d[name][k]).then_inc(in1, 16)
                for c, wd in enumerate(widths):
                    sp.dma_start(raw2[0:wd, c, :], d[w2_name][k, c * P:c * P + wd, :]).then_inc(in2, 16)
            load(0)
            norm.load(sp)
            if route:
                route.sync(sp)
            if after:
                after.sync_first(sp)
            with sp.Fori(1, groups) as k:
                load(k)
            if after:
                after.sync(sp)

        @block.gpsimd
        def _(pool):
            norm.roots(pool)
            if after:
                after.gpsimd(pool)

        @block.scalar
        def _(act):
            def split(k, p):
                act.wait_ge(in1, 16 * NW * (k + 1))
                wait(act, dn_ready, TT * (k - 1))
                for i in range(NW):
                    act.activation(w1_hi[:, p, i, :, :], raw1[:, i, :, :], ACT.Copy).then_inc(w_hi_ok, 1)
                act.wait_ge(in2, 16 * NC * (k + 1))
                full = sum(1 for wd in widths if wd == P)
                last = act.activation(w2_hi[:, p, 0:full, :], raw2[:, 0:full, :], ACT.Copy)
                if full < NC:
                    last = act.activation(w2_hi[0:widths[-1], p, full, :], raw2[0:widths[-1], full, :], ACT.Copy)
                last.then_inc(w_hi_ok, 1)

            def half_step(k, p, half):
                for c, wd in enumerate(widths):
                    m = half * NC + c
                    act.wait_ge(up_ready, U * k + m + 1)
                    if gated:
                        wait(act, hh_ok, U * k + m - 1)
                        act.activation(s1[0:wd, m % 2, :], psum[0:wd, UP + 2 * (m % 2), :], ACT.Silu).then_inc(act_ok, 1)
                    else:
                        wait(act, h_ok, U * k + m - 1)
                        act.wait_ge(side_ok, k + 1)
                        act.activation(s1[0:wd, m % 2, :], psum[0:wd, UP + m % 4, :], ACT.Gelu_apprx_tanh,
                                       bias=side[0:wd, p, c:c + 1]).then_inc(act_ok, 1)
                        act.wait_ge(act_ok, U * k + m + 1)
                    if m % NC == 0 and not (isinstance(k, int) and k == 0):
                        act.wait_ge(dn_ready, TT * (k - 1) + (half + 1) * (TT // 2))
                    if gated:
                        act.wait_ge(hh_ok, U * k + m + 1)
                    act.activation(h_hi[0:wd, c, half * HALF:(half + 1) * HALF], hh[0:wd, m % 2, :],
                                   ACT.Copy).then_inc(hhi_ok, 1)
                    if route and is_first(k) and m == 0:
                        route.scalar(act)

            def group(k, p):
                half_step(k, p, 0)
                if not is_last(k):
                    split(k + 1, 1 - p)
                elif after:
                    after.scalar_first(act)
                half_step(k, p, 1)
            if norm.affine:
                split(0, 0)
                norm.high_parts(act)
            else:
                norm.high_parts(act)
                split(0, 0)
            if route:
                route.scalar_first(act)
            loop(act, group)
            if after:
                after.scalar(act)

        @block.vector
        def _(v):
            def split(k, p):
                if tok_w is not None:
                    wait(v, dn_ok, TT * (k - 1))
                    if not is_first(k):
                        v.wait_ge(route.done, 1 if isinstance(k, int) and k < NSH else 2)
                    v.tensor_copy(side[:, p, :], tok_w[:, :, bass.ds(k, 1)]).then_inc(side_ok, 1)
                else:
                    if isinstance(k, int) and k == 0:
                        v.wait_ge(bias_in, 16)
                    wait(v, act_ok, U * (k - 1))
                    v.tensor_copy(side[:, p, 0:NC], b_all[:, bass.ds(k, 1), :]).then_inc(side_ok, 1)
                for i in range(NW):
                    v.wait_ge(w_hi_ok, NWS * k + i + 1)
                    v.tensor_tensor(w1_lo[:, p, i, :, :], raw1[:, i, :, :], w1_hi[:, p, i, :, :].bitcast(F32),
                                    ALU.subtract).then_inc(w_ok, 1)
                v.wait_ge(w_hi_ok, NWS * (k + 1))
                full = sum(1 for wd in widths if wd == P)
                last = v.tensor_tensor(w2_lo[:, p, 0:full, :], raw2[:, 0:full, :], w2_hi[:, p, 0:full, :].bitcast(F32),
                                       ALU.subtract)
                if full < NC:
                    wd = widths[-1]
                    last = v.tensor_tensor(w2_lo[0:wd, p, full, :], raw2[0:wd, full, :], w2_hi[0:wd, p, full, :].bitcast(F32),
                                           ALU.subtract)
                last.then_inc(w_ok, 1)

            def half_step(k, p, half):
                for c, wd in enumerate(widths):
                    m = half * NC + c
                    if gated:
                        v.wait_ge(act_ok, U * k + m + 1)
                        wait(v, h_ok, U * k + m - 1)
                        v.tensor_tensor(hh[0:wd, m % 2, :], s1[0:wd, m % 2, :], psum[0:wd, UP + 2 * (m % 2) + 1, :],
                                        ALU.mult).then_inc(hh_ok, 1)
                    v.wait_ge(hhi_ok, U * k + m + 1)
                    v.tensor_tensor(h_lo[0:wd, c, half * HALF:(half + 1) * HALF], hh[0:wd, m % 2, :],
                                    h_hi[0:wd, c, half * HALF:(half + 1) * HALF].bitcast(F32), ALU.subtract).then_inc(h_ok, 1)
                    if route and is_first(k):
                        route.section(v, m)

            def down(k, p):
                for t in range(TT):
                    v.wait_ge(dn_ready, TT * k + t + 1)
                    if tok_w is not None:
                        if t == 0:
                            v.wait_ge(side_ok, k + 1)
                        v.scalar_tensor_tensor(out=x[:, t, :], in0=psum[:, DN + t % 4, :], scalar=side[:, p, t:t + 1],
                                               in1=x[:, t, :], op0=ALU.mult, op1=ALU.add).then_inc(dn_ok, 1)
                    else:
                        v.tensor_tensor(x[:, t, :], x[:, t, :], psum[:, DN + t % 4, :], ALU.add).then_inc(dn_ok, 1)

            def group(k, p):
                half_step(k, p, 0)
                if not is_last(k):
                    split(k + 1, 1 - p)
                elif after:
                    after.vector_first(v)
                half_step(k, p, 1)
                if is_first(k) and norm.affine:
                    v.wait_ge(norm.x_added, TT)
                down(k, p)
            norm.statistics(v)
            norm.normalise(v)
            if route:
                route.vector_first(v)
            split(0, 0)
            loop(v, group)
            if after:
                after.vector(v)

        @block.tensor
        def _(pe):
            def group(k, p):
                pe.wait_ge(w_ok, NWS * (k + 1))
                for half in range(NHALF):
                    if is_first(k):
                        pe.wait_ge(norm.lo_done, TT // NHALF * (half + 1))
                    cols = slice(half * HALF, (half + 1) * HALF)
                    f0 = 0
                    for c, wd in enumerate(widths):
                        m = half * NC + c
                        wait(pe, hh_ok if gated else act_ok, U * k + m - UB + 1)
                        for i in range(NW):
                            bank = UP + (2 * (m % 2) + i if gated else m % 4)
                            for dc in range(DC):
                                last = passes(pe, psum[0:wd, bank, :], w1_hi[:, p, i, dc, f0:f0 + wd],
                                              w1_lo[:, p, i, dc, f0:f0 + wd], xT_hi[:, dc, cols], xT_lo[:, dc, cols],
                                              dc == 0, dc == DC - 1)
                        last.then_inc(up_ready, 1)
                        f0 += wd
                        if route and is_first(k) and m == 0:
                            route.tensor(pe)
                if route and is_first(k):
                    pe.wait_ge(route.chain, 2)
                for t in range(TT):
                    pe.wait_ge(h_ok, U * k + (NC if t < TT // 2 else U))
                    wait(pe, dn_ok, TT * k + t - 3)
                    toks = slice(t * P, (t + 1) * P)
                    for c, wd in enumerate(widths):
                        last = passes(pe, psum[:, DN + t % 4, :], h_hi[0:wd, c, toks], h_lo[0:wd, c, toks],
                                      w2_hi[0:wd, p, c, :], w2_lo[0:wd, p, c, :], c == 0, c == NC - 1)
                    last.then_inc(dn_ready, 1)
            norm.transpose(pe)
            if route:
                pe.wait_ge(norm.lo_done, TT)
                route.tensor_first(pe)
            loop(pe, group)
            if after:
                after.tensor(pe)


NE, NG, FE, NSH = 8, 4, 352, 2
NEX = NE + NSH


def route_programs(n, d, g, tok_w):
    psum, xT_hi, xT_lo = g["psum"], g["xT_hi"], g["xT_lo"]
    LTB, LB = 4, 6
    lgT = n.sb("lgT", [NE, TOK])
    gw = n.sb("gw", [P, DC, NE])
    gw_hi, gw_lo = n.sb("gw_hi", [P, DC, NE], F32R), n.sb("gw_lo", [P, DC, NE], F32R)
    before = n.sb("before", [P, NE, NE])
    lg, best, total = n.sb("lg", [P, TT, NE]), n.sb("best", [P, TT]), n.sb("total", [P, TT])
    grp, grank, masked, rank = n.sb("grp", [P, TT, NG]), n.sb("grank", [P, TT, NG]), n.sb("masked", [P, TT, NE]), n.sb("rank", [P, TT, NE])
    gt, eq = n.sb("gt", [P, TT, NE, NE]), n.sb("eq", [P, TT, NE, NE])
    lgT_ready, lgT_ok = n.sem("lgT_ready"), n.sem("lgT_ok")
    loaded, split, ready, chain, exp_ok, done = (n.sem(k) for k in ("gate_loaded", "gate_split", "logits", "chain", "exp_ok", "routed"))

    def sync(sp):
        sp.dma_start(gw[:], d["gate_weight"]).then_inc(loaded, 16)
        sp.dma_start(before[:], d["before"]).then_inc(loaded, 16)

    def tensor_first(pe):
        pe.wait_ge(split, 2)
        for half in range(NHALF):
            cols = slice(half * HALF, (half + 1) * HALF)
            for c in range(DC):
                m = passes(pe, psum[0:NE, LTB + half, :], gw_hi[:, c, :], gw_lo[:, c, :], xT_hi[:, c, cols], xT_lo[:, c, cols],
                           c == 0, c == DC - 1)
        m.then_inc(lgT_ready, 1)

    def tensor(pe):
        pe.wait_ge(lgT_ok, 1)
        for t in range(TT):
            m = pe.transpose(psum[:, LB, t * NE:(t + 1) * NE], lgT[:, t * P:(t + 1) * P], g["ident"][0:NE, 0:NE])
        m.then_inc(ready, 1)

    def scalar_first(act):
        act.wait_ge(lgT_ready, 1)
        act.activation(lgT[:].rearrange("e (b k) -> e b k", b=NHALF), psum[0:NE, LTB:LTB + NHALF, :], ACT.Copy).then_inc(lgT_ok, 1)

    def scalar(act):
        act.wait_ge(chain, 2)
        act.activation(lg[:], lg[:], ACT.Exp).then_inc(exp_ok, 1)

    def vector_first(v):
        v.memset(tok_w[:, :, 0:NSH], 1.0).then_inc(done, 1)
        v.wait_ge(loaded, 32)
        v.tensor_copy(gw_hi[:], gw[:]).then_inc(split, 1)
        v.wait_ge(split, 1)
        v.tensor_tensor(gw_lo[:], gw[:], gw_hi[:].bitcast(F32), ALU.subtract).then_inc(split, 1)
        v.wait_ge(done, 1)
    steps = [0]

    def section(v, i):
        def link(instruction):
            steps[0] += 1
            instruction.then_inc(chain, 1)
            v.wait_ge(chain, steps[0])

        def per_tile(a, m):
            return a[:].rearrange("p (t o) -> p t o", o=1).to_broadcast([P, TT, m])

        def compare(s, m):
            other = s[:].rearrange("p t (o f) -> p t o f", o=1).to_broadcast([P, TT, m, m])
            own = s[:].rearrange("p t (e o) -> p t e o", o=1).to_broadcast([P, TT, m, m])
            link(v.tensor_tensor(gt[:, :, 0:m, 0:m], other, own, ALU.is_gt))
            link(v.tensor_tensor(eq[:, :, 0:m, 0:m], other, own, ALU.is_equal))

        def count(out, m):
            low = before[:, 0:m, 0:m].rearrange("p (o e) f -> p o e f", o=1).to_broadcast([P, TT, m, m])
            a, b = gt[:, :, 0:m, 0:m], eq[:, :, 0:m, 0:m]
            link(v.tensor_tensor(b, b, low, ALU.mult))
            link(v.tensor_tensor(a, a, b, ALU.add))
            link(v.tensor_reduce(out[:], a, AX_X, ALU.add))
            link(v.tensor_scalar(out[:], out[:], 2.0, None, ALU.is_lt))
        grouped = "p t (g e) -> p t g e"
        if i == 0:
            v.wait_ge(ready, 1)
            logits = psum[:, LB, 0:TT * NE].rearrange("p (t e) -> p t e", e=NE)
            link(v.tensor_reduce(best[:], logits, AX_X, ALU.max))
            link(v.tensor_tensor(lg[:], logits, per_tile(best, NE), ALU.subtract))
        if i == 1:
            v.wait_ge(exp_ok, 1)
            link(v.tensor_reduce(total[:], lg[:], AX_X, ALU.add))
            link(v.reciprocal(total[:], total[:]))
            link(v.tensor_tensor(lg[:], lg[:], per_tile(total, NE), ALU.mult))
            link(v.tensor_reduce(grp[:], lg[:].rearrange(grouped, e=NE // NG), AX_X, ALU.max))
        if i == 2:
            compare(grp, NG)
            count(grank, NG)
        if i == 3:
            link(v.tensor_tensor(masked[:].rearrange(grouped, e=NE // NG), lg[:].rearrange(grouped, e=NE // NG),
                                 grank[:].rearrange("p t (g o) -> p t g o", o=1).to_broadcast([P, TT, NG, NE // NG]), ALU.mult))
            compare(masked, NE)
        if i == 4:
            count(rank, NE)
        if i == 5:
            v.tensor_tensor(tok_w[:, :, NSH:NEX], rank[:], masked[:], ALU.mult).then_inc(done, 1)
    made = Parts()
    made.tensor_first, made.scalar_first, made.vector_first = tensor_first, scalar_first, vector_first
    made.sync, made.tensor, made.scalar, made.section = sync, tensor, scalar, section
    made.done, made.chain = done, chain
    return made


def phase_rest(nc, d, g):
    with ExitStack() as mix:
        a = Names(nc, mix, "mix")
        feat = a.sb("feat", [P, FEATS, TOK])
        bias, cumS = a.sb("bias", [P, TT, NH]), a.sb("cumS", [P, TOK], F32R)
        with ExitStack() as inner:
            m = Names(nc, inner, "second")
            g["xT_hi"], g["xT_lo"] = m.sb("xT_hi", [P, DC, TOK], F32R), m.sb("xT_lo", [P, DC, TOK], F32R)
            once, twice, scaled = (feat[:, TT // 2 * i:TT // 2 * (i + 1), :].rearrange("p f (a k) -> p (f a) k", k=D) for i in range(3))
            phase_ffn(nc, d, g, "mlp", MG, [P] * MC, False, ["fc1"], "fc2", bias="fc1_b",
                      make_norm=lambda n: Norm(n, g, twice, affine=(once, scaled.rearrange("p t (c k) -> p t c k", k=P), d["ln_wb"])),
                      make_after=lambda n, mlp: project_programs(nc, n, d, g, mlp, feat, bias, cumS))
        phase_scan(nc, d, g, feat, bias, cumS)
    with ExitStack() as moe:
        a = Names(nc, moe, "moe")
        g["xT_hi"], g["xT_lo"] = a.sb("xT_hi", [P, DC, TOK], F32R), a.sb("xT_lo", [P, DC, TOK], F32R)
        tok_w, xn = a.sb("tok_w", [P, TT, NEX]), a.sb("xn", [P, TT, D])
        phase_ffn(nc, d, g, "experts", NEX, [P, P, FE - 2 * P], True, ["eg", "eu"], "ed", tok_w=tok_w,
                  make_norm=lambda n: Norm(n, g, xn), make_route=lambda n: route_programs(n, d, g, tok_w))


def more_layout(w):
    import numpy as np
    f32 = np.float32

    def chunk_k(a):
        return a.reshape(DC, P, -1).transpose(1, 0, 2)
    w_in = w["L0_attn_W_in"]
    o = np.cumsum([0, DI, NX * HD, NX * NST, DI, NH])
    z, xb, bp, cp, dtw = (w_in[:, o[i]:o[i + 1]] for i in range(5))
    order = [[REP * 2 * m + j, REP * (2 * m + 1) + j] for m in range(2) for j in range(REP)]
    cols = np.array([[h * HD + i for h in pair for i in range(HD)] for pair in order])
    feats = [z[:, c] for c in cols] + [cp[:, c] for c in cols] + [xb[:, :P], xb[:, P:], bp[:, :P], bp[:, P:]]
    t = np.arange(P)
    mask = np.where((t[:, None] // S == t[None, :] // S) & (t[:, None] <= t[None, :]), 0.0, -1e30).astype(f32)
    per = lambda a: a[cols].T
    return {
        "ln_wb": np.stack([w["L0_attn_ln_w"].reshape(DC, P).T, w["L0_attn_ln_b"].reshape(DC, P).T], 1),
        "w_feat": np.stack([chunk_k(f) for f in feats]),
        "w_dt": chunk_k(dtw),
        "head": np.tile(np.stack([w["L0_attn_dt_bias"], w["L0_attn_A_log"]])[None, :, None, :], (P, 1, TT, 1)),
        "tri": (mask == 0).astype(f32),
        "norm_w": per(w["L0_attn_norm_w"]),
        "d_skip": per(np.repeat(w["L0_attn_D"], HD)),
        "mask": mask,
        "w_out": w["L0_attn_W_out"][cols],
        "fc1": w["L0_attn_fc1_w"].reshape(DC, P, MG, MC * P).transpose(2, 1, 0, 3),
        "fc1_b": w["L0_attn_fc1_b"].reshape(MG, MC, P).transpose(2, 0, 1),
        "fc2": w["L0_attn_fc2_w"].reshape(MG, MC * P, D),
        "fc2_b": np.tile(w["L0_attn_fc2_b"], (P, 1)),
        "gate_weight": chunk_k(w["L0_ffn_gate_weight"].T),
        "before": np.tile((np.arange(NE)[None, :] < np.arange(NE)[:, None]).astype(f32)[None], (P, 1, 1)),
        "eg": experts_in(w["L0_ffn_gate_w"], w["L0_ffn_sh_gate_w"]),
        "eu": experts_in(w["L0_ffn_up_w"], w["L0_ffn_sh_up_w"]),
        "ed": np.concatenate([w["L0_ffn_sh_down_w"].T.reshape(NSH, FE, D), w["L0_ffn_down_w"].transpose(0, 2, 1)]),
    }


def experts_in(routed, shared):
    import numpy as np
    a = np.concatenate([shared.reshape(NSH, FE, D), routed])
    return a.transpose(0, 2, 1).reshape(NEX, DC, P, FE).transpose(0, 2, 1, 3)


def build(nc, d):
    SEMAPHORES.clear()
    with ExitStack() as top:
        n = Names(nc, top, "all")
        d["tail_rows"] = nc.dram_tensor("tail_rows", [B, 3, P], F32, kind="Internal").ap()
        g = {"psum": top.enter_context(nc.psum_tensor("psum", [P, 8, 512], F32)),
             "x": n.sb("x", [P, TT, D]), "ident": n.sb("ident", [P, P]),
             "tailT_hi": n.sb("tailT_hi", [P, B, 2], F32R), "tailT_lo": n.sb("tailT_lo", [P, B, 2], F32R)}
        g["x_loaded"], g["tail_stored"] = [n.sem(f"x_loaded{t}") for t in range(TT)], n.sem("tail_stored")
        phase_context_tail(nc, d, g)
        with ExitStack() as ctx:
            a = Names(nc, ctx, "q")
            q = a.sb("q", [P, B, HS])
            G_hi, G_lo = a.sb("G_hi", [P, H * D], F32R), a.sb("G_lo", [P, H * D], F32R)
            with ExitStack() as inner:
                m = Names(nc, inner, "first")
                g["xT_hi"], g["xT_lo"] = m.sb("xT_hi", [P, DC, TOK], F32R), m.sb("xT_lo", [P, DC, TOK], F32R)
                phase_heads(nc, d, g, q, G_hi, G_lo)
            phase_attention(nc, d, g, q, G_hi, G_lo)
        clear_semaphores(nc)
        phase_rest(nc, d, g)
        phase_store(nc, d, g)


def kernel(**inputs):
    import numpy as np
    import concourse.bacc as bacc
    from concourse.bass_utils import run_bass_kernel_spmd as run

    w = {k: np.asarray(v) for k, v in inputs.items()}
    f32 = np.float32
    inv_freq = (f32(1.0) / np.power(f32(10000.0), np.arange(0, P, 2, dtype=f32) / f32(P), dtype=f32)).astype(f32)
    angle = np.repeat(np.arange(L, dtype=f32)[:, None] * inv_freq[None, :], 2, axis=-1).astype(np.float64)
    cos, sin = np.cos(angle).astype(f32), np.sin(angle).astype(f32)
    sin[:, :P // 2] *= -1
    t = {
        "x": w["x"].reshape(TOK, D),
        "ctx": w["ctx_512"],
        "cos_main": cos[:2 * P].reshape(2, P, P).transpose(1, 0, 2),
        "sin_main": sin[:2 * P].reshape(2, P, P).transpose(1, 0, 2),
        "cos_last": np.tile(cos[L - 1], (B, 1)), "sin_last": np.tile(sin[L - 1], (B, 1)),
        "ident": np.eye(P, dtype=f32),
        "wq": w["L0_xattn_Wq"],
        "kcqT": w["L0_xattn_w_kc_q"].transpose(0, 2, 1),
        "wqrT": w["L0_xattn_W_qr"].transpose(0, 2, 1),
        "wkrT": w["L0_xattn_W_kr"].transpose(0, 2, 1),
        "kckv": w["L0_xattn_w_kc_kv"],
        "woT": w["L0_xattn_Wo"].T,
    }
    t.update(more_layout(w))
    nc = bacc.Bacc("TRN2", target_bir_lowering=False, num_devices=1)
    arrays, d = {}, {}
    for name, a in t.items():
        arrays[f"in_{name}"] = np.ascontiguousarray(a)
        d[name] = nc.dram_tensor(f"in_{name}", a.shape, mybir.dt.from_np(a.dtype), kind="ExternalInput").ap()
    d["out"] = nc.dram_tensor("out", (TOK, D), F32, kind="ExternalOutput").ap()
    build(nc, d)
    r = run(nc, [arrays], core_ids=[0])
    return r.results[0]["out"].reshape(B, S, D)
```

```python
from contextlib import ExitStack

import concourse.bass as bass
from concourse import mybir

F32 = mybir.dt.float32
F32R = mybir.dt.float32r
U32 = mybir.dt.uint32
ALU = mybir.AluOpType
ACT = mybir.ActivationFunctionType
AX_X = mybir.AxisListType.X

P = 128
B, S, D = 32, 32, 512
L = 257
TOK = B * S
TT = TOK // P
DC = D // P
HALF = 512
NHALF = TOK // HALF
BPT = P // S
H, K, CQ, R = 16, 128, 384, 64
QC = CQ // P
HS = H * S
EPS = 1e-5


def wait(e, sem, value):
    if isinstance(value, int) and value <= 0:
        return
    e.wait_ge(sem, value)


def passes(e, out, hi_l, lo_l, hi_r, lo_r, first, last):
    e.matmul(out, hi_l, hi_r, start=first, stop=False)
    e.matmul(out, hi_l, lo_r, start=False, stop=False)
    return e.matmul(out, lo_l, hi_r, start=False, stop=last)


class Names:

    def __init__(self, nc, ctx, tag):
        self.nc, self.ctx, self.tag = nc, ctx, tag

    def sb(self, name, shape, dt=F32):
        return self.ctx.enter_context(self.nc.sbuf_tensor(f"{self.tag}_{name}", shape, dt))

    def sem(self, name):
        made = self.nc.alloc_semaphore(f"{self.tag}_{name}")
        SEMAPHORES.append(made)
        return made


class Parts:
    pass


SEMAPHORES = []


def clear_semaphores(nc):
    nc.clear_and_free_semaphores(list(SEMAPHORES))
    SEMAPHORES.clear()
    nc.all_engine_barrier()


def phase_context_tail(nc, d, g):
    with ExitStack() as ctx:
        n = Names(nc, ctx, "tail")
        row, turned, t2, cosr, sinr = (n.sb(x, [B, P]) for x in ("row", "turned", "t2", "cosr", "sinr"))
        hi, lo = n.sb("hi", [B, P], F32R), n.sb("lo", [B, P], F32R)
        loaded, rotated, split, turned_T = (n.sem(x) for x in ("loaded", "rotated", "split", "turned_T"))
        ps = g["psum"]
        block = ctx.enter_context(nc.Block())

        @block.sync
        def _(sp):
            sp.dma_start(row[:], d["ctx"][:, L - 1, :]).then_inc(loaded, 16)
            sp.dma_start(cosr[:], d["cos_last"]).then_inc(loaded, 16)
            sp.dma_start(sinr[:], d["sin_last"]).then_inc(loaded, 16)
            sp.dma_start(g["ident"][:], d["ident"]).then_inc(loaded, 16)
            for t in range(TT):
                sp.dma_start(g["x"][:, t, :], d["x"][t * P:(t + 1) * P, :]).then_inc(g["x_loaded"][t], 16)
            sp.wait_ge(split, 2)
            for r, part in enumerate((hi, lo, hi)):
                sp.dma_start(d["tail_rows"][:, r, :], part[:].bitcast(F32)).then_inc(g["tail_stored"], 16)

        @block.vector
        def _(v):
            v.wait_ge(loaded, 64)
            v.tensor_tensor(turned[:], row[:], cosr[:], ALU.mult).then_inc(rotated, 1)
            v.tensor_tensor(t2[:, 0:64], row[:, 64:128], sinr[:, 0:64], ALU.mult).then_inc(rotated, 1)
            v.tensor_tensor(t2[:, 64:128], row[:, 0:64], sinr[:, 64:128], ALU.mult).then_inc(rotated, 1)
            v.wait_ge(rotated, 3)
            v.tensor_tensor(turned[:], turned[:], t2[:], ALU.add).then_inc(rotated, 1)
            v.wait_ge(rotated, 4)
            v.tensor_copy(hi[:], turned[:]).then_inc(split, 1)
            v.wait_ge(split, 1)
            v.tensor_tensor(lo[:], turned[:], hi[:].bitcast(F32), ALU.subtract).then_inc(split, 1)
            v.wait_ge(turned_T, 1)
            for c in range(2):
                v.tensor_copy(g["tailT_hi"][:, :, c], ps[:, 0, 0:B]).then_inc(split, 1)
            v.wait_ge(split, 4)
            for c in range(2):
                v.tensor_tensor(g["tailT_lo"][:, :, c], ps[:, 0, 0:B], g["tailT_hi"][:, :, 0].bitcast(F32),
                                ALU.subtract).then_inc(split, 1)

        @block.tensor
        def _(pe):
            pe.wait_ge(rotated, 4)
            pe.transpose(ps[:, 0, 0:B], turned[:], g["ident"][0:B, 0:B]).then_inc(turned_T, 1)


class Norm:
    BANK = 6

    def __init__(self, n, g, xn, loaded=(), affine=None):
        self.g, self.xn, self.loaded, self.affine = g, xn, loaded, affine
        self.rounds = 2 if affine else 1
        self.stats, self.mv = g["stats"], n.sb("mv", [P, TT, 2])
        self.var, self.rstd = n.sb("var", [P, TT, self.rounds]), n.sb("rstd", [P, TT, self.rounds])
        self.power = n.sb("power", [P, TT * self.rounds])
        if affine:
            self.wb = n.sb("wb", [P, 2, DC])
        (self.wb_in, self.power_set, self.stat_done, self.aggr, self.var_done, self.rstd_done, self.first_done, self.normed,
         self.x_added, self.transposed, self.scaled, self.hi_done, self.lo_done) = (n.sem(k) for k in (
             "wb_in", "power_set", "stat_done", "aggr", "var_done", "rstd_done", "first_done", "normed", "x_added",
             "transposed", "scaled", "hi_done", "lo_done"))

    def bank(self, t):
        return self.g["psum"][:, self.BANK + t % 2, :].rearrange("p (c k) -> p c k", c=DC)

    def load(self, sp):
        if self.affine:
            sp.dma_start(self.wb[:], self.affine[2]).then_inc(self.wb_in, 16)

    def roots(self, pool):
        pool.memset(self.power[:], -0.5).then_inc(self.power_set, 1)
        pool.wait_ge(self.power_set, 1)
        for half in range(2):
            tiles = slice(half * TT // 2, (half + 1) * TT // 2)
            pool.wait_ge(self.var_done, self.rounds * (half + 1))
            pool.tensor_tensor(self.rstd[:, tiles, :], self.var[:, tiles, :],
                               self.power[:].rearrange("p (t r) -> p t r", r=self.rounds)[:, tiles, :],
                               ALU.pow).then_inc(self.rstd_done, 1)
        if self.affine:
            x = self.g["x"]
            for t in range(TT):
                pool.wait_ge(self.first_done, t + 1)
                pool.wait_ge(self.normed, t + 1)
                pool.tensor_tensor(x[:, t, :], x[:, t, :], self.affine[0][:, t, :], ALU.add).then_inc(self.x_added, 1)

    def statistics(self, v):
        for half in range(2):
            tiles = range(half * TT // 2, (half + 1) * TT // 2)
            for t in tiles:
                if self.loaded:
                    v.wait_ge(self.loaded[t], 16)
                    v.bn_stats(self.stats[:, t, :], self.g["x"][:, t, :]).then_inc(self.stat_done, 1)
            for t in tiles:
                if self.loaded:
                    v.wait_ge(self.stat_done, t + 1)
                v.bn_aggr(self.mv[:, t, :], self.stats[:, t, :]).then_inc(self.aggr, 1)
            v.wait_ge(self.aggr, (half + 1) * TT // 2)
            these = slice(tiles[0], tiles[-1] + 1)
            v.tensor_scalar(self.var[:, these, 0], self.mv[:, these, 1], EPS, None, ALU.add).then_inc(self.var_done, 1)
            if self.affine:
                v.tensor_scalar(self.var[:, these, 1], self.mv[:, these, 1], 1.0 + EPS, EPS * EPS, ALU.mult,
                                ALU.add).then_inc(self.var_done, 1)

    def normalise(self, v):
        x = self.g["x"]

        def rows(t):
            v.wait_ge(self.rstd_done, 1 + t // (TT // 2))
            for r in range(self.rounds):
                out, done = (self.xn, self.normed) if r == self.rounds - 1 else (self.affine[0], self.first_done)
                v.tensor_scalar(out[:, t, :], x[:, t, :], self.mv[:, t, 0:1], self.rstd[:, t, r:r + 1],
                                ALU.subtract, ALU.mult).then_inc(done, 1)

        def low_part(t):
            toks = slice(t * P, (t + 1) * P)
            src = self.affine[1][:, t, :, :] if self.affine else self.bank(t)
            v.wait_ge(self.hi_done, t + 1)
            v.tensor_tensor(self.g["xT_lo"][:, :, toks], src, self.g["xT_hi"][:, :, toks].bitcast(F32),
                            ALU.subtract).then_inc(self.lo_done, 1)
        lag = 3
        for t in range(TT + lag):
            if t < TT:
                rows(t)
            if t >= lag:
                low_part(t - lag)

    def transpose(self, pe):
        for t in range(TT):
            pe.wait_ge(self.normed, t + 1)
            wait(pe, self.hi_done, t - 1)
            wait(pe, self.lo_done, t - 1)
            for c in range(DC):
                m = pe.transpose(self.g["psum"][:, self.BANK + t % 2, c * P:(c + 1) * P], self.xn[:, t, c * P:(c + 1) * P],
                                 self.g["ident"][:])
            m.then_inc(self.transposed, 1)

    def high_parts(self, act):
        if self.affine:
            act.wait_ge(self.wb_in, 16)
        for t in range(TT):
            act.wait_ge(self.transposed, t + 1)
            src = self.bank(t)
            if self.affine:
                for c in range(DC):
                    act.activation(self.affine[1][:, t, c, :], src[:, c, :], ACT.Identity, scale=self.wb[:, 0, c:c + 1],
                                   bias=self.wb[:, 1, c:c + 1]).then_inc(self.scaled, 1)
                act.wait_ge(self.scaled, DC * (t + 1))
                src = self.affine[1][:, t, :, :]
            act.activation(self.g["xT_hi"][:, :, t * P:(t + 1) * P], src, ACT.Copy).then_inc(self.hi_done, 1)


def phase_heads(nc, d, g, q, G_hi, G_lo):
    psum, xT_hi, xT_lo = g["psum"], g["xT_hi"], g["xT_lo"]
    M1, M2, CB, GB, QB = 0, 1, 2, 3, 4
    with ExitStack() as ctx:
        n = Names(nc, ctx, "heads")
        norm = Norm(n, g, q, loaded=g["x_loaded"])
        wq = n.sb("wq", [P, 2, D])
        kcqT = n.sb("kcqT", [P, 2, QC, P])
        wqr = n.sb("wqr", [P, 2, QC, R])
        wkrT = n.sb("wkrT", [R, 2, P])
        kckv = n.sb("kckv", [P, 2, P])
        woT = n.sb("woT", [P, 2, D])
        m1 = n.sb("m1", [R, P])
        m2 = n.sb("m2", [P, P])
        C_hi = n.sb("C_hi", [P, 2, DC, P], F32R)
        C_lo = n.sb("C_lo", [P, 2, DC, P], F32R)
        loaded = [n.sem(f"loaded{p}") for p in range(2)]
        m1_ready, m1_kept, m2_ready, m2_kept = (n.sem(x) for x in ("m1_ready", "m1_kept", "m2_ready", "m2_kept"))
        c_ready, c_hi_kept, c_kept = (n.sem(x) for x in ("c_ready", "c_hi_kept", "c_kept"))
        g_ready, g_hi_kept, g_kept = (n.sem(x) for x in ("g_ready", "g_hi_kept", "g_kept"))
        q_ready, q_kept = n.sem("q_ready"), n.sem("q_kept")
        block = ctx.enter_context(nc.Block())

        @block.gpsimd
        def _(pool):
            norm.roots(pool)

        @block.sync
        def _(sp):
            def load(h, p):
                wait(sp, g_ready, h - 1)
                rows = bass.ds(h * P, P)
                for dst, src in ((wkrT[:, p, :], d["wkrT"][h]), (wqr[:, p, :, :], d["wqr"][h]), (kcqT[:, p, :, :], d["kcqT"][h]),
                                 (wq[:, p, :], d["wq"][rows, :]), (kckv[:, p, :], d["kckv"][h]),
                                 (woT[:, p, :], d["woT"][rows, :])):
                    sp.dma_start(dst, src).then_inc(loaded[p], 16)
            load(0, 0)
            load(1, 1)
            with sp.Fori(1, H // 2) as i:
                for p in range(2):
                    load(2 * i + p, p)

        def fold_m1(pe, h, p, k):
            pe.wait_ge(loaded[p], 96 * (k + 1))
            wait(pe, m1_kept, h)
            for c in range(QC):
                m = pe.matmul(psum[0:R, M1, 0:P], wqr[:, p, c, :], kcqT[:, p, c, :], start=(c == 0), stop=(c == QC - 1))
            m.then_inc(m1_ready, 1)

        def fold_m2(pe, h, p):
            pe.wait_ge(m1_kept, h + 1)
            pe.matmul(psum[:, M2, 0:P], m1[:], wkrT[:, p, :], start=True, stop=True).then_inc(m2_ready, 1)

        def fold_cg(pe, h, p):
            pe.wait_ge(m2_kept, h + 1)
            wait(pe, c_kept, h)
            wait(pe, g_kept, h)
            for c in range(DC):
                m = pe.matmul(psum[:, CB, c * P:(c + 1) * P], wq[:, p, c * P:(c + 1) * P], m2[:], start=True, stop=True)
            m.then_inc(c_ready, 1)
            pe.matmul(psum[:, GB, :], kckv[:, p, :], woT[:, p, :], start=True, stop=True).then_inc(g_ready, 1)

        def project(pe, h, p, half):
            pe.wait_ge(c_kept, h + 1)
            wait(pe, q_kept, 2 * h + half - 1)
            for c in range(DC):
                cols = slice(half * HALF, (half + 1) * HALF)
                m = passes(pe, psum[:, QB + half, :], C_hi[:, p, c, :], C_lo[:, p, c, :],
                           xT_hi[:, c, cols], xT_lo[:, c, cols], c == 0, c == DC - 1)
            m.then_inc(q_ready, 1)

        @block.tensor
        def _(pe):
            def step(h, p, k_next, fold_next):
                if fold_next:
                    fold_m1(pe, h + 1, 1 - p, k_next)
                project(pe, h, p, 0)
                if fold_next:
                    fold_m2(pe, h + 1, 1 - p)
                project(pe, h, p, 1)
                if fold_next:
                    fold_cg(pe, h + 1, 1 - p)
            fold_m1(pe, 0, 0, 0)
            fold_m2(pe, 0, 0)
            fold_cg(pe, 0, 0)
            norm.transpose(pe)
            pe.wait_ge(norm.lo_done, TT)
            step(0, 0, 0, True)
            step(1, 1, 1, True)
            with pe.Fori(1, H // 2 - 1) as i:
                step(2 * i, 0, i, True)
                step(2 * i + 1, 1, i + 1, True)
            step(H - 2, 0, H // 2 - 1, True)
            step(H - 1, 1, 0, False)

        @block.scalar
        def _(act):
            def step(h, p):
                act.wait_ge(m1_ready, h + 1)
                wait(act, m2_ready, h)
                act.activation(m1[:], psum[0:R, M1, 0:P], ACT.Copy).then_inc(m1_kept, 1)
                act.wait_ge(c_ready, h + 1)
                wait(act, q_ready, 2 * (h - 1))
                act.activation(C_hi[:, p, :, :], psum[:, CB, :].rearrange("p (c k) -> p c k", c=DC),
                               ACT.Copy).then_inc(c_hi_kept, 1)
            step(0, 0)
            norm.high_parts(act)
            step(1, 1)
            with act.Fori(1, H // 2) as i:
                step(2 * i, 0)
                step(2 * i + 1, 1)

        @block.vector
        def _(v):
            def keep_m2(h):
                v.wait_ge(m2_ready, h + 1)
                wait(v, c_ready, h)
                v.tensor_copy(m2[:], psum[:, M2, 0:P]).then_inc(m2_kept, 1)

            def keep_q(h, half):
                v.wait_ge(q_ready, 2 * h + half + 1)
                nb = HALF // S
                v.tensor_copy(q[:, half * nb:(half + 1) * nb, bass.ds(h * S, S)],
                              psum[:, QB + half, :].rearrange("p (b s) -> p b s", s=S)).then_inc(q_kept, 1)

            def step(h, p, fold_next):
                keep_q(h, 0)
                if fold_next:
                    keep_m2(h + 1)
                keep_q(h, 1)
                if fold_next:
                    split_cg(h + 1, 1 - p)

            def split_cg(h, p):
                v.wait_ge(c_hi_kept, h + 1)
                v.tensor_tensor(C_lo[:, p, :, :], psum[:, CB, :].rearrange("p (c k) -> p c k", c=DC),
                                C_hi[:, p, :, :].bitcast(F32), ALU.subtract).then_inc(c_kept, 1)
                v.wait_ge(g_ready, h + 1)
                gcols = bass.ds(h * D, D)
                v.tensor_copy(G_hi[:, gcols], psum[:, GB, :]).then_inc(g_hi_kept, 1)
                v.wait_ge(g_hi_kept, h + 1)
                v.tensor_tensor(G_lo[:, gcols], psum[:, GB, :], G_hi[:, gcols].bitcast(F32),
                                ALU.subtract).then_inc(g_kept, 1)
            norm.statistics(v)
            keep_m2(0)
            split_cg(0, 0)
            norm.normalise(v)
            step(0, 0, True)
            step(1, 1, True)
            with v.Fori(1, H // 2 - 1) as i:
                step(2 * i, 0, True)
                step(2 * i + 1, 1, True)
            step(H - 2, 0, True)
            step(H - 1, 1, False)


def phase_attention(nc, d, g, q, G_hi, G_lo):
    psum, x, ident = g["psum"], g["x"], g["ident"]
    SC, PT0, CT, KT = 0, 4, 6, 7
    LP = L + 1
    NJ = HS // P
    KVB = 4
    with ExitStack() as ctx:
        n = Names(nc, ctx, "att")
        cosb, sinb = n.sb("cosb", [P, 2, P]), n.sb("sinb", [P, 2, P])
        raw = n.sb("raw", [P, 2, P])
        turn = n.sb("turn", [P, 2, P])
        kvr = n.sb("kvr", [P, 2, 2, P])
        kv_hi, kv_lo = n.sb("kv_hi", [P, KVB, 2, P], F32R), n.sb("kv_lo", [P, KVB, 2, P], F32R)
        tail = n.sb("tail", [3, KVB, P], F32R)
        kvT_hi, kvT_lo = n.sb("kvT_hi", [P, 2, LP], F32R), n.sb("kvT_lo", [P, 2, LP], F32R)
        q_hi, q_lo = n.sb("q_hi", [P, 2, HS], F32R), n.sb("q_lo", [P, 2, HS], F32R)
        pr = n.sb("pr", [P, 2, NJ, LP + 2])
        prr = pr[:].bitcast(F32R)
        low = n.sb("low", [P, 2, NJ])
        total, scale = n.sb("total", [P, 2, NJ]), n.sb("scale", [P, 2, NJ])
        pT_hi, pT_lo = n.sb("pT_hi", [P, 2, HS], F32R), n.sb("pT_lo", [P, 2, HS], F32R)
        pT_tail = n.sb("pT_tail", [3, HS], F32R)
        cT_hi, cT_lo = n.sb("cT_hi", [P, H, P], F32R), n.sb("cT_lo", [P, H, P], F32R)
        S_ = n.sem
        tables, raw_in, rot, rot_mid, tail_in = S_("tables"), S_("raw_in"), S_("rot"), S_("rot_mid"), [S_(f"tail_in{i}") for i in range(KVB)]
        rot_a, tail_cols = S_("rot_a"), S_("tail_cols")
        kvT_ready, kvT_hi_ok, kvT_ok, kv_hi_ok, kv_ok = (S_(x) for x in ("kvT_ready", "kvT_hi_ok", "kvT_ok", "kv_hi_ok", "kv_ok"))
        q_hi_ok, q_ok = S_("q_hi_ok"), S_("q_ok")
        sc_ready, low_ok, exp_ok, inv_ok, pr_ok, p_split, p_tail = (S_(x) for x in (
            "sc_ready", "low_ok", "exp_ok", "inv_ok", "pr_ok", "p_split", "p_tail"))
        pt_ready, pt_hi_ok, pt_ok, ptail_ok = (S_(x) for x in ("pt_ready", "pt_hi_ok", "pt_ok", "ptail_ok"))
        c_ready, c_hi_ok, c_ok, o_ready, o_ok = (S_(x) for x in ("c_ready", "c_hi_ok", "c_ok", "o_ready", "o_ok"))
        stats_ok = S_("stats_ok")
        block = ctx.enter_context(nc.Block())

        def run(e, step):
            for u in range(BPT):
                step(u, u)
            with e.Fori(1, B // BPT - 1) as i:
                for u in range(BPT):
                    step(BPT * i + u, u)
            for s in range(B - BPT, B + 3):
                step(s, s % BPT)

        def inside(s, lag):
            return not isinstance(s, int) or 0 <= s - lag < B

        @block.sync
        def _(sp):
            sp.dma_start(cosb[:], d["cos_main"]).then_inc(tables, 16)
            sp.dma_start(sinb[:], d["sin_main"]).then_inc(tables, 16)
            sp.wait_ge(g["tail_stored"], 48)

            def load(b, u):
                wait(sp, rot_a, b)
                sp.dma_start(raw[:], d["ctx"][b, 0:2 * P, :].rearrange("(c p) k -> p c k", p=P)).then_inc(raw_in, 16)

            def load_tail(b, u):
                wait(sp, c_ready, b - KVB + 1)
                sp.dma_start(tail[:, u, :].bitcast(F32), d["tail_rows"][b]).then_inc(tail_in[u], 16)
            for b in range(2 * BPT):
                load(b, b % BPT)
                if b >= 2:
                    load_tail(b - 2, (b - 2) % BPT)
            with sp.Fori(2, B // BPT) as i:
                for u in range(BPT):
                    load(BPT * i + u, u)
                    load_tail(BPT * i + u - 2, (u - 2) % BPT)
            load_tail(B - 2, 2)
            load_tail(B - 1, 3)

        @block.gpsimd
        def _(pool):
            def rotate(b, u):
                p = u % 2
                pool.wait_ge(raw_in, 16 * (b + 1))
                wait(pool, kvT_ready, b - 1)
                wait(pool, kv_ok, b - 1)
                wait(pool, rot, b)
                pool.tensor_tensor(kvr[:, p, :, :], raw[:], cosb[:], ALU.mult).then_inc(rot_mid, 1)
                pool.tensor_tensor(turn[:, :, 0:64], raw[:, :, 64:128], sinb[:, :, 0:64], ALU.mult).then_inc(rot_mid, 1)
                pool.tensor_tensor(turn[:, :, 64:128], raw[:, :, 0:64], sinb[:, :, 64:128], ALU.mult).then_inc(rot_a, 1)
                pool.wait_ge(rot_mid, 2 * (b + 1))
                pool.wait_ge(rot_a, b + 1)
                pool.tensor_tensor(kvr[:, p, :, :], kvr[:, p, :, :], turn[:], ALU.add).then_inc(rot, 1)

            def low_parts(b, u):
                p = u % 2
                wait(pool, sc_ready, NJ * (b - 1))
                pool.tensor_copy(kvT_hi[:, p, 2 * P:LP], g["tailT_hi"][:, bass.ds(b, 1), :]).then_inc(tail_cols, 1)
                pool.tensor_copy(kvT_lo[:, p, 2 * P:LP], g["tailT_lo"][:, bass.ds(b, 1), :]).then_inc(tail_cols, 1)
                pool.wait_ge(q_hi_ok, b + 1)
                pool.tensor_tensor(q_lo[:, p, :], q[:, b, :], q_hi[:, p, :].bitcast(F32), ALU.subtract).then_inc(q_ok, 1)

            def context_rows_lo(b, u):
                p = u % 2
                pool.wait_ge(kv_hi_ok, b + 1)
                pool.tensor_tensor(kv_lo[:, u, :, :], kvr[:, p, :, :], kv_hi[:, u, :, :].bitcast(F32),
                                   ALU.subtract).then_inc(kv_ok, 1)

            def step(s, u):
                if inside(s, -1):
                    context_rows_lo(s + 1, (u + 1) % BPT)
                if inside(s, -3):
                    rotate(s + 3, (u + 3) % BPT)
                if inside(s, -2):
                    low_parts(s + 2, (u + 2) % BPT)
            pool.wait_ge(tables, 32)
            rotate(0, 0)
            rotate(1, 1)
            low_parts(0, 0)
            context_rows_lo(0, 0)
            rotate(2, 2)
            low_parts(1, 1)
            run(pool, step)

        @block.tensor
        def _(pe):
            def transpose_context(b, u):
                pe.wait_ge(rot, b + 1)
                wait(pe, kvT_ok, b)
                wait(pe, ptail_ok, b - 3)
                for c in range(2):
                    m = pe.transpose(psum[:, KT, c * P:(c + 1) * P], kvr[:, u % 2, c, :], ident[:])
                m.then_inc(kvT_ready, 1)

            def scores(b, u, tiles):
                p = u % 2
                pe.wait_ge(q_ok, b + 1)
                pe.wait_ge(kvT_ok, b + 1)
                pe.wait_ge(tail_cols, 2 * (b + 1))
                for j in tiles:
                    wait(pe, exp_ok, NJ * (b - 1) + j + 1)
                    rows = slice(j * P, (j + 1) * P)
                    passes(pe, psum[:, SC + j, 0:LP], q_hi[:, p, rows], q_lo[:, p, rows],
                           kvT_hi[:, p, :], kvT_lo[:, p, :], True, True).then_inc(sc_ready, 1)

            def transpose_probs(b, u):
                p = u % 2
                wait(pe, pt_ok, 2 * b)
                wait(pe, ptail_ok, b)
                pe.wait_ge(kvT_ok, b + 4 if not isinstance(b, int) else min(b + 4, B))
                pe.wait_ge(p_tail, b + 1)
                for j in range(NJ):
                    for c in range(2):
                        pe.transpose(psum[:, PT0 + c, j * P:(j + 1) * P], pr[:, p, j, c * P:(c + 1) * P], ident[:])
                    m = pe.transpose(psum[0:3, KT, j * P:(j + 1) * P], pr[:, p, j, 2 * P:2 * P + 3], ident[:])
                m.then_inc(pt_ready, 1)

            def context(b, u):
                pe.wait_ge(kv_ok, b + 1)
                pe.wait_ge(tail_in[u], 16 * (b // BPT + 1) if isinstance(b, int) else 4 * (b - u) + 16)
                pe.wait_ge(pt_ok, 2 * (b + 1))
                pe.wait_ge(ptail_ok, b + 1)
                wait(pe, c_ok, b)
                for c in range(2):
                    passes(pe, psum[:, CT, :], kv_hi[:, u, c, :], kv_lo[:, u, c, :], pT_hi[:, c, :], pT_lo[:, c, :],
                           c == 0, False)
                pe.matmul(psum[:, CT, :], tail[:, u, :], pT_tail[:], start=False, stop=True).then_inc(c_ready, 1)

            def output(t):
                pe.wait_ge(c_ok, BPT * (t + 1))
                pe.wait_ge(pt_ok, 2 * (BPT * (t + 1) + 1) if not isinstance(t, int) else min(2 * (BPT * (t + 1) + 1), 2 * B))
                for h in range(H):
                    m = passes(pe, psum[:, PT0, :], cT_hi[:, h, :], cT_lo[:, h, :], G_hi[:, h * D:(h + 1) * D],
                               G_lo[:, h * D:(h + 1) * D], h == 0, h == H - 1)
                m.then_inc(o_ready, 1)

            def step(s, u):
                if inside(s, 0):
                    scores(s, u, (0, 1))
                if inside(s, -2):
                    transpose_context(s + 2, (u + 2) % BPT)
                if inside(s, 0):
                    scores(s, u, (2, 3))
                if u == 2 and (not isinstance(s, int) or s >= BPT):
                    t = s // BPT - 1 if isinstance(s, int) else (s - u) // BPT - 1
                    output(t)
                if inside(s, 2):
                    context(s - 2, (u - 2) % BPT)
                if inside(s, 1):
                    if u == 2 and (not isinstance(s, int) or s >= BPT):
                        pe.wait_ge(o_ok, s // BPT if isinstance(s, int) else (s - u) // BPT)
                    transpose_probs(s - 1, (u - 1) % BPT)
            transpose_context(0, 0)
            transpose_context(1, 1)
            run(pe, step)

        @block.scalar
        def _(act):
            def prepare(b, u):
                p = u % 2
                act.wait_ge(kvT_ready, b + 1)
                wait(act, sc_ready, NJ * (b - 1))
                act.activation(kvT_hi[:, p, 0:2 * P], psum[:, KT, 0:2 * P], ACT.Copy).then_inc(kvT_hi_ok, 1)

            def queries_hi(b, u):
                wait(act, sc_ready, NJ * (b - 1))
                act.activation(q_hi[:, u % 2, :], q[:, b, :], ACT.Copy).then_inc(q_hi_ok, 1)

            def context_rows_hi(b, u):
                act.wait_ge(rot, b + 1)
                wait(act, c_ready, b - KVB + 1)
                act.activation(kv_hi[:, u, :, :], kvr[:, u % 2, :, :], ACT.Copy).then_inc(kv_hi_ok, 1)

            def exponentials(b, u):
                p = u % 2
                for j in range(NJ):
                    act.wait_ge(low_ok, NJ * b + j + 1)
                    if j == 0:
                        wait(act, pt_ready, b - 1)
                    act.activation(pr[:, p, j, 0:L], psum[:, SC + j, 0:L], ACT.Exp, bias=low[:, p, j:j + 1],
                                   accum_out=total[:, p, j:j + 1]).then_inc(exp_ok, 1)

            def probs_hi(b, u):
                act.wait_ge(pt_ready, b + 1)
                wait(act, c_ready, b)
                act.activation(pT_tail[:], psum[0:3, KT, :], ACT.Copy).then_inc(ptail_ok, 1)
                for c in range(2):
                    act.activation(pT_hi[:, c, :], psum[:, PT0 + c, :], ACT.Copy).then_inc(pt_hi_ok, 1)

            def context_hi(b, u):
                act.wait_ge(c_ready, b + 1)
                if u == 0:
                    wait(act, o_ready, b // BPT)
                act.activation(cT_hi[:, :, u * S:(u + 1) * S], psum[:, CT, :].rearrange("p (h s) -> p h s", s=S),
                               ACT.Copy).then_inc(c_hi_ok, 1)

            def step(s, u):
                if inside(s, 2):
                    probs_hi(s - 2, (u - 2) % BPT)
                if inside(s, -2):
                    prepare(s + 2, (u + 2) % BPT)
                if inside(s, -2):
                    queries_hi(s + 2, (u + 2) % BPT)
                if inside(s, -1):
                    context_rows_hi(s + 1, (u + 1) % BPT)
                if inside(s, 0):
                    exponentials(s, u)
                if inside(s, 2):
                    context_hi(s - 2, (u - 2) % BPT)
            prepare(0, 0)
            queries_hi(0, 0)
            context_rows_hi(0, 0)
            prepare(1, 1)
            queries_hi(1, 1)
            run(act, step)

        @block.vector
        def _(v):
            def prepare(b, u):
                p = u % 2
                v.wait_ge(kvT_hi_ok, b + 1)
                v.tensor_tensor(kvT_lo[:, p, 0:2 * P], psum[:, KT, 0:2 * P], kvT_hi[:, p, 0:2 * P].bitcast(F32),
                                ALU.subtract).then_inc(kvT_ok, 1)

            def maxima(b, u):
                p = u % 2
                for j in range(NJ):
                    v.wait_ge(sc_ready, NJ * b + j + 1)
                    v.tensor_reduce(low[:, p, j:j + 1], psum[:, SC + j, 0:L], AX_X, ALU.max, negate=True).then_inc(low_ok, 1)

            def normalise(b, u):
                p = u % 2
                for j in range(NJ):
                    if j % 2 == 0:
                        pair = slice(j, j + 2)
                        v.wait_ge(exp_ok, NJ * b + j + 2)
                        v.reciprocal(scale[:, p, pair], total[:, p, pair]).then_inc(inv_ok, 1)
                        v.wait_ge(inv_ok, 2 * b + j // 2 + 1)
                    v.tensor_scalar(pr[:, p, j, 0:L], pr[:, p, j, 0:L], scale[:, p, j:j + 1], None,
                                    ALU.mult).then_inc(pr_ok, 1)
                v.wait_ge(pr_ok, NJ * (b + 1))
                v.tensor_copy(prr[:, p, :, 2 * P + 1:2 * P + 2], pr[:, p, :, 2 * P:2 * P + 1]).then_inc(p_split, 1)
                v.wait_ge(p_split, 2 * b + 1)
                v.tensor_tensor(pr[:, p, :, 2 * P + 2:2 * P + 3], pr[:, p, :, 2 * P:2 * P + 1],
                                pr[:, p, :, 2 * P + 1:2 * P + 2], ALU.subtract).then_inc(p_split, 1)
                v.wait_ge(p_split, 2 * b + 2)
                v.tensor_copy(pr[:, p, :, 2 * P:2 * P + 1], pr[:, p, :, 2 * P + 1:2 * P + 2]).then_inc(p_tail, 1)

            def probs_lo(b, u):
                for c in range(2):
                    v.wait_ge(pt_hi_ok, 2 * b + c + 1)
                    v.tensor_tensor(pT_lo[:, c, :], psum[:, PT0 + c, :], pT_hi[:, c, :].bitcast(F32),
                                    ALU.subtract).then_inc(pt_ok, 1)

            def context_lo(b, u):
                v.wait_ge(c_hi_ok, b + 1)
                cols = slice(u * S, (u + 1) * S)
                v.tensor_tensor(cT_lo[:, :, cols], psum[:, CT, :].rearrange("p (h s) -> p h s", s=S),
                                cT_hi[:, :, cols].bitcast(F32), ALU.subtract).then_inc(c_ok, 1)

            def step(s, u):
                late = None
                if inside(s, 2):
                    probs_lo(s - 2, (u - 2) % BPT)
                if inside(s, -2):
                    prepare(s + 2, (u + 2) % BPT)
                if inside(s, 0):
                    maxima(s, u)
                if inside(s, 0):
                    normalise(s, u)
                if u == 2 and (not isinstance(s, int) or s >= BPT):
                    t = s // BPT - 1 if isinstance(s, int) else (s - u) // BPT - 1
                    v.wait_ge(o_ready, t + 1)
                    v.tensor_tensor(x[:, bass.ds(t, 1), :], x[:, bass.ds(t, 1), :],
                                    psum[:, PT0:PT0 + 1, :], ALU.add).then_inc(o_ok, 1)
                    late = t
                if inside(s, 2):
                    context_lo(s - 2, (u - 2) % BPT)
                if late is not None:
                    v.wait_ge(o_ok, late + 1)
                    v.bn_stats(g["stats"][:, bass.ds(late, 1), :], x[:, bass.ds(late, 1), :]).then_inc(stats_ok, 1)
            prepare(0, 0)
            prepare(1, 1)
            run(v, step)




DI, HD, NST, NH, NX = 1024, 64, 64, 16, 4
REP = NH // NX
ZC = DI // P
FEATS = 2 * ZC + 4
Z0, C0, X0, B0 = 0, ZC, 2 * ZC, 2 * ZC + 2


LOW = 32
TINY = 2.0 ** -126


def project_programs(nc, n, d, g, mlp, feat, bias, cumS):
    psum, xT_hi, xT_lo, ident = g["psum"], g["xT_hi"], g["xT_lo"], g["ident"]
    DTT, DT, CM, TR = 4, 6, 7, 4
    n = Names(nc, n.ctx, "proj")
    raw, w_hi, w_lo = mlp.raw1[:], mlp.w1_hi[:, 0, :, :], mlp.w1_lo[:, 0, :, :]
    slot = [slice(0, P), slice(P, 2 * P)]
    wdt = n.sb("wdt", [P, DC, NH])
    wdt_hi, wdt_lo = n.sb("wdt_hi", [P, DC, NH], F32R), n.sb("wdt_lo", [P, DC, NH], F32R)
    head = n.sb("head", [P, 2, TT, NH])
    tri = n.sb("tri", [P, P])
    b2 = mlp.raw2[:, 0, :]
    negA, pre, mag, u, w1, wm, dt, lndt = (n.sb(x, [P, TT, NH]) for x in ("negA", "pre", "mag", "u", "w1", "wm", "dt", "lndt"))
    cum = n.sb("cum", [P, TT, LOW + NH])
    cumT_hi = mlp.h_hi[0:LOW + NH, 0, :]
    dtT = mlp.s1[0:NH, :, :]
    loaded, w_hi_ok, w_ok, f_ready, f_kept = [n.sem("loaded0"), n.sem("loaded1")], n.sem("w_hi_ok"), n.sem("w_ok"), n.sem("f_ready"), n.sem("f_kept")
    small, dt_w, dt_ready, b2_in, x_plus = n.sem("small"), n.sem("dt_w"), n.sem("dt_ready"), n.sem("b2_in"), n.sem("x_plus")
    dtT_ready, dtT_ok = n.sem("dtT_ready"), n.sem("dtT_ok")
    chain, a_chain, zeros = n.sem("chain"), n.sem("a_chain"), n.sem("zeros")
    cum_ready, cum_ok, cumT_ready, cumT_hi_ok, cumS_ok = (n.sem(x) for x in ("cum_ready", "cum_ok", "cumT_ready", "cumT_hi_ok", "cumS_ok"))
    EARLY = 8

    def sync_first(sp):
        for dst, src in ((wdt[:], d["w_dt"]), (head[:], d["head"]), (tri[:], d["tri"])):
            sp.dma_start(dst, src).then_inc(small, 16)

    def sync(sp):
        def load(k, p):
            wait(sp, w_ok, k - 1)
            sp.dma_start(raw[:, :, slot[p]], d["w_feat"][k]).then_inc(loaded[p], 16)
        sp.wait_ge(mlp.w_ok, mlp.all_split)
        load(0, 0)
        load(1, 1)
        sp.dma_start(b2, d["fc2_b"]).then_inc(b2_in, 16)
        with sp.Fori(1, FEATS // 2) as i:
            load(2 * i, 0)
            load(2 * i + 1, 1)

    def gpsimd(pool):
        pool.memset(cumS[:].bitcast(F32), 0.0).then_inc(zeros, 1)
        pool.memset(cum[:], 0.0).then_inc(zeros, 1)
        pool.wait_ge(b2_in, 16)
        pool.wait_ge(mlp.dn_ok, mlp.all_down)
        for t in range(TT):
            pool.tensor_tensor(g["x"][:, t, :], g["x"][:, t, :], b2, ALU.add).then_inc(x_plus, 1)

    def tensor(pe):
        def chunk(k, p):
            pe.wait_ge(w_ok, k + 1)
            for half in range(NHALF):
                bank = 2 * p + half
                wait(pe, f_kept, 2 * (k - 2) + half + 1)
                cols = slice(half * HALF, (half + 1) * HALF)
                for c in range(DC):
                    m = passes(pe, psum[:, bank, :], w_hi[:, c, slot[p]], w_lo[:, c, slot[p]],
                               xT_hi[:, c, cols], xT_lo[:, c, cols], c == 0, c == DC - 1)
                m.then_inc(f_ready, 1)
        pe.wait_ge(mlp.act_ok, mlp.all_up)
        for k in range(EARLY):
            chunk(k, k % 2)
            if k == 0:
                pe.wait_ge(mlp.dn_ok, mlp.all_down)
                pe.wait_ge(dt_w, 2)
                for half in range(NHALF):
                    cols = slice(half * HALF, (half + 1) * HALF)
                    for c in range(DC):
                        m = passes(pe, psum[0:NH, DTT + half, :], wdt_hi[:, c, :], wdt_lo[:, c, :],
                                   xT_hi[:, c, cols], xT_lo[:, c, cols], c == 0, c == DC - 1)
                m.then_inc(dtT_ready, 1)
            if k == 1:
                pe.wait_ge(dtT_ok, 1)
                for t in range(TT):
                    m = pe.transpose(psum[:, DT, t * NH:(t + 1) * NH], dtT[:, t // 4, (t % 4) * P:(t % 4 + 1) * P], ident[0:NH, 0:NH])
                m.then_inc(dt_ready, 1)
            if k == 3:
                pe.wait_ge(chain, DT_STEPS)
                pe.matmul(psum[:, CM, 0:TT * NH], tri[:], pre[:].rearrange("p t h -> p (t h)"), start=True,
                          stop=True).then_inc(cum_ready, 1)
            if k == 5:
                pe.wait_ge(cum_ok, 2)
                for t in range(TT):
                    m = pe.transpose(psum[0:LOW + NH, TR + t // 4, (t % 4) * P:(t % 4 + 1) * P], cum[:, t, :], ident[:])
                m.then_inc(cumT_ready, 1)
        with pe.Fori(EARLY // 2, FEATS // 2) as i:
            chunk(2 * i, 0)
            chunk(2 * i + 1, 1)

    def split_hi(act, k, p):
        act.wait_ge(loaded[p], 16 * (k // 2 + 1) if isinstance(k, int) else 8 * (k - p) + 16)
        wait(act, f_ready, 2 * (k - 1))
        act.activation(w_hi[:, :, slot[p]], raw[:, :, slot[p]], ACT.Copy).then_inc(w_hi_ok, 1)

    def scalar_first(act):
        act.wait_ge(mlp.dn_ready, mlp.all_down - TT)
        split_hi(act, 0, 0)
        split_hi(act, 1, 1)

    def scalar(act):
        def keep_z(k, p):
            for half in range(NHALF):
                act.wait_ge(f_ready, 2 * k + half + 1)
                act.activation(feat[:, k, half * HALF:(half + 1) * HALF], psum[:, 2 * p + half, :],
                               ACT.Silu).then_inc(f_kept, 1)

        def keep(k, p):
            for half in range(NHALF):
                act.wait_ge(f_ready, 2 * k + half + 1)
                act.activation(feat[:, bass.ds(k, 1), half * HALF:(half + 1) * HALF],
                               psum[:, 2 * p + half:2 * p + half + 1, :], ACT.Copy).then_inc(f_kept, 1)
        for k in range(ZC):
            keep_z(k, k % 2)
            split_hi(act, k + 2, k % 2)
            if k == 0:
                act.wait_ge(dtT_ready, 1)
                act.activation(dtT, psum[0:NH, DTT:DTT + NHALF, :], ACT.Copy).then_inc(dtT_ok, 1)
            if k == 1:
                act.wait_ge(small, 48)
                act.activation(negA[:], head[:, 1, :, :], ACT.Exp).then_inc(a_chain, 1)
                act.wait_ge(chain, 2)
                act.activation(u[:], mag[:], ACT.Exp, scale=-1.0).then_inc(a_chain, 1)
                act.wait_ge(chain, 3)
                act.activation(wm[:], w1[:], ACT.Ln).then_inc(a_chain, 1)
                act.wait_ge(chain, DT_STEPS)
                act.activation(lndt[:], w1[:], ACT.Ln).then_inc(a_chain, 1)
        with act.Fori(ZC // 2, FEATS // 2 - 1) as i:
            for p in range(2):
                keep(2 * i + p, p)
                split_hi(act, 2 * i + p + 2, p)
        keep(FEATS - 2, 0)
        keep(FEATS - 1, 1)

    def split(v, k, p):
        v.wait_ge(w_hi_ok, k + 1)
        v.tensor_tensor(w_lo[:, :, slot[p]], raw[:, :, slot[p]], w_hi[:, :, slot[p]].bitcast(F32),
                        ALU.subtract).then_inc(w_ok, 1)

    def vector_first(v):
        split(v, 0, 0)
        split(v, 1, 1)
        v.wait_ge(small, 48)
        v.tensor_copy(wdt_hi[:], wdt[:]).then_inc(dt_w, 1)
        v.wait_ge(dt_w, 1)
        v.tensor_tensor(wdt_lo[:], wdt[:], wdt_hi[:].bitcast(F32), ALU.subtract).then_inc(dt_w, 1)

    def vector(v):
        steps = [0]

        def link(i):
            steps[0] += 1
            i.then_inc(chain, 1)
            v.wait_ge(chain, steps[0])

        def dt_path():
            v.wait_ge(dt_ready, 1)
            link(v.tensor_tensor(pre[:], psum[:, DT, 0:TT * NH].rearrange("p (t h) -> p t h", h=NH), head[:, 0, :, :], ALU.add))
            link(v.scalar_tensor_tensor(out=mag[:], in0=pre[:], scalar=-1.0, in1=pre[:], op0=ALU.mult, op1=ALU.max))
            v.wait_ge(a_chain, 2)
            link(v.tensor_scalar(w1[:], u[:], 1.0, None, ALU.add))
            link(v.tensor_scalar(mag[:], w1[:], -1.0, None, ALU.add))
            v.wait_ge(a_chain, 3)
            link(v.tensor_tensor(wm[:], wm[:], u[:], ALU.mult))
            link(v.tensor_scalar(w1[:], mag[:], 0.0, None, ALU.is_equal))
            link(v.tensor_tensor(mag[:], mag[:], w1[:], ALU.add))
            link(v.reciprocal(mag[:], mag[:]))
            link(v.tensor_tensor(wm[:], wm[:], mag[:], ALU.mult))
            link(v.tensor_tensor(w1[:], w1[:], u[:], ALU.mult))
            link(v.tensor_tensor(wm[:], wm[:], w1[:], ALU.add))
            link(v.scalar_tensor_tensor(out=dt[:], in0=pre[:], scalar=0.0, in1=wm[:], op0=ALU.max, op1=ALU.add))
            link(v.scalar_tensor_tensor(out=pre[:], in0=dt[:], scalar=-1.0, in1=negA[:], op0=ALU.mult, op1=ALU.mult))
            link(v.tensor_scalar(w1[:], dt[:], TINY, None, ALU.max))
            assert steps[0] == DT_STEPS

        def keep_cum():
            v.wait_ge(cum_ready, 1)
            v.wait_ge(a_chain, 4)
            v.wait_ge(zeros, 2)
            sums = psum[:, CM, 0:TT * NH].rearrange("p (t h) -> p t h", h=NH)
            v.tensor_copy(cum[:, :, 0:NH], sums).then_inc(cum_ok, 1)
            v.tensor_copy(cum[:, :, LOW:LOW + NH], sums).then_inc(cum_ok, 1)
            v.tensor_tensor(bias[:], lndt[:], sums, ALU.subtract).then_inc(cum_ok, 1)

        def split_cumT():
            both = psum[0:LOW + NH, TR:TR + 2, :].rearrange("h b k -> h (b k)")
            v.wait_ge(cumT_ready, 1)
            v.tensor_copy(cumT_hi, both).then_inc(cumT_hi_ok, 1)
            v.wait_ge(cumT_hi_ok, 1)
            v.tensor_copy(cumS[0:NH, :], cumT_hi[0:NH, :].bitcast(F32)).then_inc(cumS_ok, 1)
            v.tensor_tensor(cumS[LOW:LOW + NH, :], both[LOW:LOW + NH, :], cumT_hi[LOW:LOW + NH, :].bitcast(F32),
                            ALU.subtract).then_inc(cumS_ok, 1)
        for k in range(2, EARLY):
            split(v, k, k % 2)
            if k == 3:
                dt_path()
            if k == 5:
                keep_cum()
            if k == 7:
                split_cumT()
        with v.Fori(EARLY // 2, FEATS // 2) as i:
            split(v, 2 * i, 0)
            split(v, 2 * i + 1, 1)
    made = Parts()
    made.sync_first, made.scalar_first, made.vector_first = sync_first, scalar_first, vector_first
    made.sync, made.gpsimd, made.tensor, made.scalar, made.vector = sync, gpsimd, tensor, scalar, vector
    return made


DT_STEPS = 14


def phase_scan(nc, d, g, feat, bias, cumS):
    psum, ident, x = g["psum"], g["ident"], g["x"]
    CU, SB, YB, OB, MB = 0, 2, 4, 6, 7
    with ExitStack() as ctx:
        n = Names(nc, ctx, "scan")
        WR = 4
        wo_raw = n.sb("wo_raw", [P, WR, D])
        wo_hi, wo_lo = n.sb("wo_hi", [P, ZC, D], F32R), n.sb("wo_lo", [P, ZC, D], F32R)
        nw, dcol = n.sb("nw", [P, ZC]), n.sb("dcol", [P, ZC])
        mask = n.sb("mask", [P, P])
        masks, ident_r = n.sb("masks", [P, REP, P], F32R), n.sb("ident_r", [P, P], F32R)
        pick = n.sb("pick", [P, NH], F32R)
        ones = n.sb("ones", [P, 2])
        power, ms, rs = n.sb("power", [P, 1]), n.sb("ms", [P, 2]), n.sb("rs", [P, 2])
        zeros = n.sb("zeros", [P, D])
        C_hi, C_lo = n.sb("C_hi", [P, 2, ZC, P], F32R), n.sb("C_lo", [P, 2, ZC, P], F32R)
        B_hi, B_lo = n.sb("B_hi", [P, 2, 2, P], F32R), n.sb("B_lo", [P, 2, 2, P], F32R)
        xs, tbias = n.sb("xs", [P, 2, P]), n.sb("tbias", [P, 2, NH])
        xt_hi, xt_lo = n.sb("xt_hi", [P, 2, 2 * P], F32R), n.sb("xt_lo", [P, 2, 2 * P], F32R)
        E = n.sb("E", [P, 2, REP, P])
        W_hi, W_lo = n.sb("W_hi", [P, 2, REP, P], F32R), n.sb("W_lo", [P, 2, REP, P], F32R)
        skip = n.sb("skip", [P, 2, REP, P])
        y = n.sb("y", [P, 2, REP, P])
        sq, folded = n.sb("sq", [P, ZC, P]), n.sb("folded", [P, 2, P])
        y_hi, y_lo = n.sb("y_hi", [P, ZC, P], F32R), n.sb("y_lo", [P, ZC, P], F32R)
        S_ = n.sem
        consts, wo_in, wo_hi_ok, wo_ok, set_up = S_("consts"), [S_(f"wo_in{i}") for i in range(WR)], S_("wo_hi_ok"), S_("wo_ok"), S_("set_up")
        consts_r = S_("consts_r")
        pair_ok, fold_ok, zero_set, zeroed, stats_ok = S_("pair_ok"), S_("fold_ok"), S_("zero_set"), S_("zeroed"), S_("stats_ok")
        cb_hi_ok, cb_ok, xs_ok, tbias_ok, xt_ready, xt_hi_ok, xt_ok = (S_(k) for k in (
            "cb_hi_ok", "cb_ok", "xs_ok", "tbias_ok", "xt_ready", "xt_hi_ok", "xt_ok"))
        cu_ready, s_ready, e_ok, w_ok, whi_ok, wlo_ok, skip_ok = (S_(k) for k in (
            "cu_ready", "s_ready", "e_ok", "w_ok", "whi_ok", "wlo_ok", "skip_ok"))
        y_ready, yd_ok, yg_ok, sq_ok, yhi_ok, ylo_ok = (S_(k) for k in ("y_ready", "yd_ok", "yg_ok", "sq_ok", "yhi_ok", "ylo_ok"))
        ss_ready, ms_ok, rs_ok, o_ready, o_ok = (S_(k) for k in ("ss_ready", "ms_ok", "rs_ok", "o_ready", "o_ok"))
        block = ctx.enter_context(nc.Block())

        def run(e, slot):
            for t in range(3):
                for k in range(NX):
                    slot(t, t % 2, k)
            with e.Fori(1, TT // 2 - 1) as i:
                for k in range(NX):
                    slot(2 * i + 1, 1, k)
                for k in range(NX):
                    slot(2 * i + 2, 0, k)
            for k in range(NX):
                slot(TT - 1, 1, k)

        def ahead(f, t, p, k, steps):
            c, k = divmod(k + steps, NX)
            if not (isinstance(t, int) and t + c >= TT):
                f(t + c, (p + c) % 2, k)

        def another(t):
            return not (isinstance(t, int) and t == TT - 1)

        def earlier(t):
            return not (isinstance(t, int) and t == 0)

        def out_chunks(k):
            return range(k * 3, min(k * 3 + 3, ZC))

        @block.sync
        def _(sp):
            for dst, src in ((nw[:], d["norm_w"]), (dcol[:], d["d_skip"]), (mask[:], d["mask"])):
                sp.dma_start(dst, src).then_inc(consts, 16)
            for c in range(ZC):
                wait(sp, wo_ok, c - WR + 1)
                sp.dma_start(wo_raw[:, c % WR, :], d["w_out"][c]).then_inc(wo_in[c % WR], 16)
            sp.wait_ge(zero_set, 1)
            for c in range(NT):
                rows = d["slot_rows"][c * SLOTS:(c + 1) * SLOTS, :].rearrange("(a p) k -> p a k", p=P)
                sp.dma_start(rows, zeros[:].rearrange("p (o k) -> p o k", o=1).to_broadcast([P, SLOTS // P, D])).then_inc(zeroed, 16)
            sp.wait_ge(zeroed, 16 * NT)

        @block.gpsimd
        def _(pool):
            pool.memset(power[:], -0.5).then_inc(set_up, 1)
            pool.memset(ones[:], 1.0).then_inc(set_up, 1)
            pool.memset(zeros[:], 0.0).then_inc(zero_set, 1)

            def copy_x(t):
                wait(pool, xt_ready, t)
                wait(pool, skip_ok, 2 * t)
                pool.tensor_copy(xs[:], feat[:, X0:X0 + 2, bass.ds(t * P, P)]).then_inc(xs_ok, 1)

            def split_cb(t, p):
                pool.wait_ge(cb_hi_ok, 2 * t + 1)
                pool.tensor_tensor(C_lo[:, p, :, :], feat[:, C0:C0 + ZC, bass.ds(t * P, P)], C_hi[:, p, :, :].bitcast(F32),
                                   ALU.subtract).then_inc(cb_ok, 1)
                pool.wait_ge(cb_hi_ok, 2 * t + 2)
                pool.tensor_tensor(B_lo[:, p, :, :], feat[:, B0:B0 + 2, bass.ds(t * P, P)], B_hi[:, p, :, :].bitcast(F32),
                                   ALU.subtract).then_inc(cb_ok, 1)

            def skip_path(t, m):
                wait(pool, yg_ok, 2 * t + m - 1)
                pool.wait_ge(xs_ok, t + 1)
                pool.tensor_tensor(skip[:, m, :, :], xs[:, m, :].rearrange("p (o t) -> p o t", o=1).to_broadcast([P, REP, P]),
                                   feat[:, REP * m:REP * (m + 1), bass.ds(t * P, P)], ALU.mult).then_inc(skip_ok, 1)

            def fold_squares(t, m):
                pool.wait_ge(sq_ok, 2 * t + m + 1)
                wait(pool, ss_ready, t)
                half = sq[:, REP * m:REP * (m + 1), :]
                pool.tensor_tensor(half[:, 0:2, :], half[:, 0:2, :], half[:, 2:4, :], ALU.add).then_inc(pair_ok, 1)
                pool.wait_ge(pair_ok, 2 * t + m + 1)
                pool.tensor_tensor(folded[:, m, :], half[:, 0, :], half[:, 1, :], ALU.add).then_inc(fold_ok, 1)

            def root(t, p):
                pool.wait_ge(ms_ok, t + 1)
                wait(pool, o_ok, t - 1)
                pool.tensor_tensor(rs[:, p:p + 1], ms[:, p:p + 1], power[:], ALU.pow).then_inc(rs_ok, 1)

            def slot(t, p, k):
                if k == 0 and earlier(t):
                    fold_squares(t - 1, 1)
                if k == 0 and another(t):
                    split_cb(t + 1, 1 - p)
                if k == 1:
                    skip_path(t, 1)
                    if another(t):
                        copy_x(t + 1)
                if k == 2 and earlier(t):
                    root(t - 1, 1 - p)
                if k == 3:
                    fold_squares(t, 0)
                if k == 3 and another(t):
                    skip_path(t + 1, 0)
            copy_x(0)
            split_cb(0, 0)
            skip_path(0, 0)
            pool.wait_ge(set_up, 2)
            run(pool, slot)
            fold_squares(TT - 1, 1)
            root(TT - 1, 1)

        @block.scalar
        def _(act):
            def out_weight(c):
                act.wait_ge(wo_in[c % WR], 16 * (c // WR + 1))
                act.activation(wo_hi[:, c, :], wo_raw[:, c % WR, :], ACT.Copy, scale=nw[:, c:c + 1]).then_inc(wo_hi_ok, 1)

            def cb_hi(t, p):
                wait(act, s_ready, NX * (t - 1))
                act.activation(C_hi[:, p, :, :], feat[:, C0:C0 + ZC, bass.ds(t * P, P)], ACT.Copy).then_inc(cb_hi_ok, 1)
                act.activation(B_hi[:, p, :, :], feat[:, B0:B0 + 2, bass.ds(t * P, P)], ACT.Copy).then_inc(cb_hi_ok, 1)

            def x_hi(t, p):
                act.wait_ge(xt_ready, t + 1)
                wait(act, y_ready, NX * (t - 1))
                act.activation(xt_hi[:, p, :], psum[:, MB, 0:2 * P], ACT.Copy).then_inc(xt_hi_ok, 1)

            def exponentials(t, p, k):
                act.wait_ge(cu_ready, NX * t + k + 1)
                act.wait_ge(tbias_ok, t + 1)
                wait(act, wlo_ok, NX * t + k - 1)
                for j in range(REP):
                    h = k * REP + j
                    i = act.activation(E[:, k % 2, j, :], psum[:, CU + k % 2, j * P:(j + 1) * P], ACT.Exp,
                                       bias=tbias[:, p, h:h + 1])
                i.then_inc(e_ok, 1)

            def weights_hi(t, p, k):
                act.wait_ge(w_ok, NX * t + k + 1)
                wait(act, y_ready, NX * t + k - 1)
                act.activation(W_hi[:, k % 2, :, :], E[:, k % 2, :, :], ACT.Copy).then_inc(whi_ok, 1)

            def gated(t, m):
                act.wait_ge(yg_ok, 2 * t + m + 1)
                wait(act, o_ready, 2 * t + m - 1)
                act.activation(y_hi[:, REP * m:REP * (m + 1), :], y[:, m, :, :], ACT.Copy).then_inc(yhi_ok, 1)
                wait(act, fold_ok, 2 * t + m - 1)
                act.activation(sq[:, REP * m:REP * (m + 1), :], y[:, m, :, :], ACT.Square).then_inc(sq_ok, 1)

            def slot(t, p, k):
                ahead(exponentials, t, p, k, 2)
                ahead(weights_hi, t, p, k, 1)
                if k == 0:
                    if earlier(t):
                        gated(t - 1, 1)
                    if another(t):
                        cb_hi(t + 1, 1 - p)
                if not earlier(t) and k < 3:
                    for c in out_chunks(k):
                        out_weight(c)
                if k == 2:
                    gated(t, 0)
                    if another(t):
                        x_hi(t + 1, 1 - p)
            cb_hi(0, 0)
            x_hi(0, 0)
            exponentials(0, 0, 0)
            weights_hi(0, 0, 0)
            exponentials(0, 0, 1)
            act.wait_ge(consts, 48)
            run(act, slot)
            gated(TT - 1, 1)

        @block.vector
        def _(v):
            v.wait_ge(consts, 48)
            v.tensor_tensor(pick[:], ident[:, 0:NH], ident[:, LOW:LOW + NH], ALU.add).then_inc(consts_r, 1)
            v.tensor_copy(ident_r[:], ident[:]).then_inc(consts_r, 1)
            for j in range(REP):
                v.tensor_copy(masks[:, j, :], mask[:]).then_inc(consts_r, 1)

            def out_weight(c):
                v.wait_ge(wo_hi_ok, c + 1)
                v.scalar_tensor_tensor(out=wo_lo[:, c, :], in0=wo_raw[:, c % WR, :], scalar=nw[:, c:c + 1],
                                       in1=wo_hi[:, c, :].bitcast(F32), op0=ALU.mult, op1=ALU.subtract).then_inc(wo_ok, 1)

            def tile_bias(t, p):
                wait(v, e_ok, NX * (t - 1))
                v.tensor_copy(tbias[:, p:p + 1, :], bias[:, bass.ds(t, 1), :]).then_inc(tbias_ok, 1)

            def x_lo(t, p):
                v.wait_ge(xt_hi_ok, t + 1)
                v.tensor_tensor(xt_lo[:, p, :], psum[:, MB, 0:2 * P], xt_hi[:, p, :].bitcast(F32), ALU.subtract).then_inc(xt_ok, 1)

            def weigh(t, p, k):
                v.wait_ge(e_ok, NX * t + k + 1)
                v.wait_ge(s_ready, NX * t + k + 1)
                v.tensor_tensor(E[:, k % 2, :, :], psum[:, SB + k % 2, :].rearrange("p (j t) -> p j t", j=REP),
                                E[:, k % 2, :, :], ALU.mult).then_inc(w_ok, 1)

            def weights_lo(t, p, k):
                v.wait_ge(whi_ok, NX * t + k + 1)
                v.tensor_tensor(W_lo[:, k % 2, :, :], E[:, k % 2, :, :], W_hi[:, k % 2, :, :].bitcast(F32),
                                ALU.subtract).then_inc(wlo_ok, 1)

            def gate(t, m):
                v.wait_ge(y_ready, NX * t + 2 * m + 2)
                wait(v, sq_ok, 2 * t + m - 1)
                wait(v, ylo_ok, 2 * t + m - 1)
                for r in range(2):
                    rows = slice(64 * r, 64 * (r + 1))
                    i = v.tensor_tensor(y[rows, m, :, :], psum[rows, YB + r, :].rearrange("p (j t) -> p j t", j=REP),
                                        feat[rows, REP * m:REP * (m + 1), bass.ds(t * P, P)], ALU.mult)
                i.then_inc(yd_ok, 1)
                v.wait_ge(yd_ok, 2 * t + m + 1)
                v.wait_ge(skip_ok, 2 * t + m + 1)
                for j in range(REP):
                    c = REP * m + j
                    i = v.scalar_tensor_tensor(out=y[:, m, j, :], in0=skip[:, m, j, :], scalar=dcol[:, c:c + 1],
                                               in1=y[:, m, j, :], op0=ALU.mult, op1=ALU.add)
                i.then_inc(yg_ok, 1)

            def gated_lo(t, m):
                v.wait_ge(yhi_ok, 2 * t + m + 1)
                v.tensor_tensor(y_lo[:, REP * m:REP * (m + 1), :], y[:, m, :, :],
                                y_hi[:, REP * m:REP * (m + 1), :].bitcast(F32), ALU.subtract).then_inc(ylo_ok, 1)

            def mean_square(t, p):
                v.wait_ge(ss_ready, t + 1)
                v.tensor_scalar(ms[:, p:p + 1], psum[:, MB, 256:257], 1.0 / DI, EPS, ALU.mult, ALU.add).then_inc(ms_ok, 1)

            def add_to_x(t, p):
                v.wait_ge(o_ready, 2 * (t + 1))
                v.wait_ge(rs_ok, t + 1)
                v.scalar_tensor_tensor(out=x[:, bass.ds(t, 1), :], in0=psum[:, OB:OB + 1, :], scalar=rs[:, p:p + 1],
                                       in1=x[:, bass.ds(t, 1), :], op0=ALU.mult, op1=ALU.add).then_inc(o_ok, 1)

            def statistics(t):
                v.wait_ge(o_ok, t + 1)
                v.bn_stats(g["stats"][:, bass.ds(t, 1), :], x[:, bass.ds(t, 1), :]).then_inc(stats_ok, 1)

            def slot(t, p, k):
                ahead(weigh, t, p, k, 1)
                if k == 0 and another(t):
                    tile_bias(t + 1, 1 - p)
                if k == 0 and earlier(t):
                    gate(t - 1, 1)
                if k == 2:
                    gate(t, 0)
                if k == 2 and earlier(t):
                    add_to_x(t - 1, 1 - p)
                ahead(weights_lo, t, p, k, 1)
                if not earlier(t) and k < 3:
                    for c in out_chunks(k):
                        out_weight(c)
                if k == 0 and earlier(t):
                    gated_lo(t - 1, 1)
                if k == 1 and earlier(t):
                    mean_square(t - 1, 1 - p)
                if k == 2:
                    gated_lo(t, 0)
                if k == 3 and another(t):
                    x_lo(t + 1, 1 - p)
                if k == 3 and earlier(t):
                    statistics(t - 1)
            tile_bias(0, 0)
            x_lo(0, 0)
            weigh(0, 0, 0)
            weights_lo(0, 0, 0)
            run(v, slot)
            gate(TT - 1, 1)
            gated_lo(TT - 1, 1)
            mean_square(TT - 1, 1)
            add_to_x(TT - 1, 1)
            statistics(TT - 1)

        @block.tensor
        def _(pe):
            def transpose_x(t):
                pe.wait_ge(xs_ok, t + 1)
                wait(pe, ms_ok, t - 1)
                for c in range(2):
                    m = pe.transpose(psum[:, MB, c * P:(c + 1) * P], xs[:, c, :], ident[:])
                m.then_inc(xt_ready, 1)

            def sums(t, p, k):
                wait(pe, e_ok, NX * t + k - 1)
                bank = psum[:, CU + k % 2, :]
                pe.matmul(bank, ident_r[:], masks[:].rearrange("p j t -> p (j t)"), start=True, stop=False)
                for j in range(REP):
                    h = k * REP + j
                    i = pe.matmul(bank[:, j * P:(j + 1) * P], pick[:, h:h + 1].to_broadcast([P, P]),
                                  cumS[:, bass.ds(t * P, P)], start=False, stop=j == REP - 1)
                i.then_inc(cu_ready, 1)

            def scores(t, p, k):
                pe.wait_ge(cb_ok, 2 * (t + 1))
                wait(pe, w_ok, NX * t + k - 1)
                r, m = 64 * (k % 2), k // 2
                rows, ch = slice(r, r + 64), slice(REP * m, REP * (m + 1))
                passes(pe, psum[:, SB + k % 2, :], B_hi[rows, p, m, :], B_lo[rows, p, m, :], C_hi[rows, p, ch, :],
                       C_lo[rows, p, ch, :], True, True).then_inc(s_ready, 1)

            def outputs(t, p, k):
                pe.wait_ge(xt_ok, t + 1)
                pe.wait_ge(wlo_ok, NX * t + k + 1)
                wait(pe, yd_ok, 2 * t + k // 2)
                cols = slice((k // 2) * P, (k // 2 + 1) * P)
                passes(pe, psum[:, YB + k % 2, :], xt_hi[:, p, cols], xt_lo[:, p, cols], W_hi[:, k % 2, :, :],
                       W_lo[:, k % 2, :, :], True, True).then_inc(y_ready, 1)

            def project(t, m):
                pe.wait_ge(ylo_ok, 2 * t + m + 1)
                if m == 0:
                    wait(pe, o_ok, t)
                for c in range(REP * m, REP * (m + 1)):
                    i = passes(pe, psum[:, OB, :], y_hi[:, c, :], y_lo[:, c, :], wo_hi[:, c, :], wo_lo[:, c, :],
                               c == 0, c == ZC - 1)
                i.then_inc(o_ready, 1)

            def squares(t):
                pe.wait_ge(fold_ok, 2 * (t + 1))
                pe.wait_ge(xt_ok, min(t + 2, TT) if isinstance(t, int) else t + 2)
                for m in range(2):
                    i = pe.matmul(psum[:, MB, 256:257], folded[:, m, :], ones[:, 0:1], start=m == 0, stop=m == 1)
                i.then_inc(ss_ready, 1)

            def slot(t, p, k):
                ahead(sums, t, p, k, 3)
                ahead(scores, t, p, k, 2)
                if k == 2 and another(t):
                    transpose_x(t + 1)
                outputs(t, p, k)
                if k == 1 and earlier(t):
                    squares(t - 1)
                    project(t - 1, 1)
                if k == 3:
                    if not earlier(t):
                        pe.wait_ge(wo_ok, ZC)
                    project(t, 0)
            pe.wait_ge(set_up, 2)
            transpose_x(0)
            pe.wait_ge(consts_r, REP + 2)
            sums(0, 0, 0)
            sums(0, 0, 1)
            scores(0, 0, 0)
            sums(0, 0, 2)
            scores(0, 0, 1)
            run(pe, slot)
            squares(TT - 1)
            project(TT - 1, 1)


MG, MC = 8, 2


def phase_mlp(nc, d, g, make_norm, make_after):
    psum, x, xT_hi, xT_lo = g["psum"], g["x"], g["xT_hi"], g["xT_lo"]
    F, groups = MC * P, MG
    UP, DN = 0, 4
    with ExitStack() as ctx:
        n = Names(nc, ctx, "mlp")
        raw1 = n.sb("raw1", [P, DC, F])
        raw2 = n.sb("raw2", [P, MC, D])
        w1_hi, w1_lo = n.sb("w1_hi", [P, 2, DC, F], F32R), n.sb("w1_lo", [P, 2, DC, F], F32R)
        w2_hi, w2_lo = n.sb("w2_hi", [P, 2, MC, D], F32R), n.sb("w2_lo", [P, 2, MC, D], F32R)
        side = n.sb("side", [P, 2, MC])
        h_hi, h_lo = n.sb("h_hi", [P, MC, TOK], F32R), n.sb("h_lo", [P, MC, TOK], F32R)
        s1 = n.sb("s1", [P, 2, HALF])
        b_all = n.sb("b_all", [P, groups, MC])
        S_ = n.sem
        bias_in, in1, in2 = S_("bias_in"), S_("in1"), S_("in2")
        w_hi_ok, w_ok, side_ok = S_("w_hi_ok"), S_("w_ok"), S_("side_ok")
        up_ready, act_ok, hhi_ok, h_ok = S_("up_ready"), S_("act_ok"), S_("hhi_ok"), S_("h_ok")
        dn_ready, dn_ok = S_("dn_ready"), S_("dn_ok")
        NWS = 2
        U = MC * NHALF
        norm = make_norm(n)
        own = Parts()
        own.raw1, own.raw2, own.w1_hi, own.w1_lo, own.h_hi, own.s1 = raw1, raw2, w1_hi, w1_lo, h_hi, s1
        own.w_ok, own.act_ok, own.dn_ready, own.dn_ok = w_ok, act_ok, dn_ready, dn_ok
        own.all_split, own.all_up, own.all_down = NWS * groups, U * groups, TT * groups
        after = make_after(n, own)
        block = ctx.enter_context(nc.Block())

        def is_last(k):
            return isinstance(k, int) and k == groups - 1

        def is_first(k):
            return isinstance(k, int) and k == 0

        def loop(e, group):
            group(0, 0)
            group(1, 1)
            with e.Fori(1, groups // 2 - 1) as i:
                group(2 * i, 0)
                group(2 * i + 1, 1)
            group(groups - 2, 0)
            group(groups - 1, 1)

        @block.sync
        def _(sp):
            sp.dma_start(b_all[:], d["fc1_b"]).then_inc(bias_in, 16)

            def load(k):
                wait(sp, w_ok, NWS * k)
                sp.dma_start(raw1[:], d["fc1"][k]).then_inc(in1, 16)
                sp.dma_start(raw2[:], d["fc2"][k]).then_inc(in2, 16)
            load(0)
            norm.load(sp)
            after.sync_first(sp)
            with sp.Fori(1, groups) as k:
                load(k)
            after.sync(sp)

        @block.gpsimd
        def _(pool):
            norm.roots(pool)
            after.gpsimd(pool)

        @block.scalar
        def _(act):
            def split(k, p):
                act.wait_ge(in1, 16 * (k + 1))
                wait(act, dn_ready, TT * (k - 1))
                act.activation(w1_hi[:, p, :, :], raw1[:], ACT.Copy).then_inc(w_hi_ok, 1)
                act.wait_ge(in2, 16 * (k + 1))
                act.activation(w2_hi[:, p, :, :], raw2[:], ACT.Copy).then_inc(w_hi_ok, 1)

            def half_step(k, p, half):
                for c in range(MC):
                    m = half * MC + c
                    act.wait_ge(up_ready, U * k + m + 1)
                    wait(act, h_ok, U * k + m - 1)
                    act.wait_ge(side_ok, k + 1)
                    act.activation(s1[:, m % 2, :], psum[:, UP + m % 4, :], ACT.Gelu_apprx_tanh,
                                   bias=side[:, p, c:c + 1]).then_inc(act_ok, 1)
                    act.wait_ge(act_ok, U * k + m + 1)
                    if c == 0 and not is_first(k):
                        act.wait_ge(dn_ready, TT * (k - 1) + (half + 1) * (TT // 2))
                    act.activation(h_hi[:, c, half * HALF:(half + 1) * HALF], s1[:, m % 2, :], ACT.Copy).then_inc(hhi_ok, 1)

            def group(k, p):
                half_step(k, p, 0)
                if not is_last(k):
                    split(k + 1, 1 - p)
                else:
                    after.scalar_first(act)
                half_step(k, p, 1)
            split(0, 0)
            norm.high_parts(act)
            loop(act, group)
            after.scalar(act)

        @block.vector
        def _(v):
            def split(k, p):
                if is_first(k):
                    v.wait_ge(bias_in, 16)
                wait(v, act_ok, U * (k - 1))
                v.tensor_copy(side[:, p, :], b_all[:, bass.ds(k, 1), :]).then_inc(side_ok, 1)
                v.wait_ge(w_hi_ok, NWS * k + 1)
                v.tensor_tensor(w1_lo[:, p, :, :], raw1[:], w1_hi[:, p, :, :].bitcast(F32), ALU.subtract).then_inc(w_ok, 1)
                v.wait_ge(w_hi_ok, NWS * (k + 1))
                v.tensor_tensor(w2_lo[:, p, :, :], raw2[:], w2_hi[:, p, :, :].bitcast(F32), ALU.subtract).then_inc(w_ok, 1)

            def half_step(k, p, half):
                for c in range(MC):
                    m = half * MC + c
                    v.wait_ge(hhi_ok, U * k + m + 1)
                    v.tensor_tensor(h_lo[:, c, half * HALF:(half + 1) * HALF], s1[:, m % 2, :],
                                    h_hi[:, c, half * HALF:(half + 1) * HALF].bitcast(F32), ALU.subtract).then_inc(h_ok, 1)

            def down(k, p):
                for t in range(TT):
                    v.wait_ge(dn_ready, TT * k + t + 1)
                    v.tensor_tensor(x[:, t, :], x[:, t, :], psum[:, DN + t % 4, :], ALU.add).then_inc(dn_ok, 1)

            def group(k, p):
                half_step(k, p, 0)
                if not is_last(k):
                    split(k + 1, 1 - p)
                else:
                    after.vector_first(v)
                half_step(k, p, 1)
                if is_first(k):
                    v.wait_ge(norm.x_added, TT)
                down(k, p)
            norm.statistics(v)
            norm.normalise(v)
            split(0, 0)
            loop(v, group)
            after.vector(v)

        @block.tensor
        def _(pe):
            def group(k, p):
                pe.wait_ge(w_ok, NWS * (k + 1))
                for half in range(NHALF):
                    if is_first(k):
                        pe.wait_ge(norm.lo_done, TT // NHALF * (half + 1))
                    cols = slice(half * HALF, (half + 1) * HALF)
                    for c in range(MC):
                        m = half * MC + c
                        wait(pe, act_ok, U * k + m - 3)
                        for dc in range(DC):
                            last = passes(pe, psum[:, UP + m % 4, :], w1_hi[:, p, dc, c * P:(c + 1) * P],
                                          w1_lo[:, p, dc, c * P:(c + 1) * P], xT_hi[:, dc, cols], xT_lo[:, dc, cols],
                                          dc == 0, dc == DC - 1)
                        last.then_inc(up_ready, 1)
                for t in range(TT):
                    pe.wait_ge(h_ok, U * k + (MC if t < TT // 2 else U))
                    wait(pe, dn_ok, TT * k + t - 3)
                    toks = slice(t * P, (t + 1) * P)
                    for c in range(MC):
                        last = passes(pe, psum[:, DN + t % 4, :], h_hi[:, c, toks], h_lo[:, c, toks], w2_hi[:, p, c, :],
                                      w2_lo[:, p, c, :], c == 0, c == MC - 1)
                    last.then_inc(dn_ready, 1)
            norm.transpose(pe)
            loop(pe, group)
            after.tensor(pe)


NE, NG, FE, NSH, TOP = 8, 4, 352, 2, 2
NEX = NE + NSH
WD = [P, P, FE - 2 * P]
NC = len(WD)
SLOTS = 256
NT = (TOP * TOK + NE * (SLOTS - 1)) // SLOTS
EXT = TOK // SLOTS


def route_programs(n, d, g):
    psum, xT_hi, xT_lo = g["psum"], g["xT_hi"], g["xT_lo"]
    LTB, LB = 4, 6
    gw = n.sb("gw", [P, DC, NE])
    gw_hi, gw_lo = n.sb("gw_hi", [P, DC, NE], F32R), n.sb("gw_lo", [P, DC, NE], F32R)
    before = n.sb("before", [P, NE, NE])
    steps_of = n.sb("steps_of", [P, NE, EXT])
    tile_no = n.sb("tile_no", [P, NT, NE])
    earlier = n.sb("earlier", [P, 2, P])
    compared = n.sb("compared", [P, 2, TOK // 2])
    lg, best, total = n.sb("lg", [P, TT, NE]), n.sb("best", [P, TT]), n.sb("total", [P, TT])
    grp, grank = n.sb("grp", [P, TT, NG]), n.sb("grank", [P, TT, NG])
    masked, chosen = n.sb("masked", [P, TT, NE]), n.sb("chosen", [P, TT, NE])
    pos, held, acc = n.sb("pos", [P, TT, NE]), n.sb("held", [P, TT, NE]), n.sb("acc", [P, TT + 1, NE])
    tiles, start, end = n.sb("tiles", [P, NE]), n.sb("start", [P, NE]), n.sb("end", [P, NE])
    expert_f, expert = n.sb("expert_f", [P, NT]), n.sb("expert", [P, NT], U32)
    slot_f, slot, weight = n.sb("slot_f", [P, TOP, TT]), n.sb("slot", [P, TOP, TT], U32), n.sb("weight", [P, TOP, TT])
    lgT = compared[0:NE, :, :]
    gt, eq = (compared[:, i, :].rearrange("p (t e f) -> p t e f", e=NE, f=NE) for i in range(2))
    lgT_ready, lgT_ok = n.sem("lgT_ready"), n.sem("lgT_ok")
    loaded, split, ready, chain, exp_ok = (n.sem(k) for k in ("gate_loaded", "gate_split", "logits", "chain", "exp_ok"))
    chosen_ok, pos_ready, pos_kept, expert_ok, slot_ok, weight_ok = (n.sem(k) for k in (
        "chosen_ok", "pos_ready", "pos_kept", "expert_ok", "slot_ok", "weight_ok"))

    def sync(sp):
        for dst, src in ((gw, "gate_weight"), (before, "before"), (steps_of, "steps_of"), (tile_no, "tile_no"), (earlier, "earlier")):
            sp.dma_start(dst[:], d[src]).then_inc(loaded, 16)

    def tensor_first(pe):
        pe.wait_ge(split, 2)
        for half in range(NHALF):
            cols = slice(half * HALF, (half + 1) * HALF)
            for c in range(DC):
                m = passes(pe, psum[0:NE, LTB + half, :], gw_hi[:, c, :], gw_lo[:, c, :], xT_hi[:, c, cols], xT_lo[:, c, cols],
                           c == 0, c == DC - 1)
        m.then_inc(lgT_ready, 1)

    def tensor(pe, m):
        if m == 0:
            pe.wait_ge(lgT_ok, 1)
            for t in range(TT):
                i = pe.transpose(psum[:, LB, t * NE:(t + 1) * NE], lgT[:, t // 4, (t % 4) * P:(t % 4 + 1) * P], g["ident"][0:NE, 0:NE])
            i.then_inc(ready, 1)
        if m == 2:
            pe.wait_ge(chosen_ok, 1)
            for r in range(2):
                i = pe.matmul(psum[:, LB, r * TT * NE:(r + 1) * TT * NE], earlier[:, r, :], chosen[:].rearrange("p t e -> p (t e)"),
                              start=True, stop=True)
            i.then_inc(pos_ready, 1)

    def scalar_first(act):
        act.wait_ge(lgT_ready, 1)
        act.activation(lgT, psum[0:NE, LTB:LTB + NHALF, :], ACT.Copy).then_inc(lgT_ok, 1)

    def scalar(act):
        act.wait_ge(chain, 2)
        act.activation(lg[:], lg[:], ACT.Exp).then_inc(exp_ok, 1)

    def vector_first(v):
        v.wait_ge(loaded, 80)
        v.tensor_copy(gw_hi[:], gw[:]).then_inc(split, 1)
        v.wait_ge(split, 1)
        v.tensor_tensor(gw_lo[:], gw[:], gw_hi[:].bitcast(F32), ALU.subtract).then_inc(split, 1)
    steps = [0]

    def vector(v, m):
        for part in ((0, 1), (2,), (3, 4), (5,), (), ())[m]:
            section(v, part)

    def section(v, m):
        def link(instruction):
            steps[0] += 1
            instruction.then_inc(chain, 1)
            v.wait_ge(chain, steps[0])

        def per_tile(a, m):
            return a.rearrange("p (t o) -> p t o", o=1).to_broadcast([P, TT, m])

        def compare(s, m):
            other = s[:].rearrange("p t (o f) -> p t o f", o=1).to_broadcast([P, TT, m, m])
            own = s[:].rearrange("p t (e o) -> p t e o", o=1).to_broadcast([P, TT, m, m])
            low = before[:, 0:m, 0:m].rearrange("p (o e) f -> p o e f", o=1).to_broadcast([P, TT, m, m])
            link(v.tensor_tensor(gt[:, :, 0:m, 0:m], other, own, ALU.is_gt))
            link(v.tensor_tensor(eq[:, :, 0:m, 0:m], other, own, ALU.is_equal))
            link(v.tensor_tensor(eq[:, :, 0:m, 0:m], eq[:, :, 0:m, 0:m], low, ALU.mult))

        def fewer_than_two(out, m):
            a, b = gt[:, :, 0:m, 0:m], eq[:, :, 0:m, 0:m]
            link(v.tensor_tensor(a, a, b, ALU.add))
            link(v.tensor_reduce(out[:], a, AX_X, ALU.add))
            return v.tensor_scalar(out[:], out[:], float(TOP), None, ALU.is_lt)
        grouped = "p t (g e) -> p t g e"
        if m == 0:
            v.wait_ge(ready, 1)
            logits = psum[:, LB, 0:TT * NE].rearrange("p (t e) -> p t e", e=NE)
            link(v.tensor_reduce(best[:], logits, AX_X, ALU.max))
            link(v.tensor_tensor(lg[:], logits, per_tile(best[:], NE), ALU.subtract))
            v.wait_ge(exp_ok, 1)
            link(v.tensor_reduce(total[:], lg[:], AX_X, ALU.add))
            link(v.reciprocal(total[:], total[:]))
            link(v.tensor_tensor(lg[:], lg[:], per_tile(total[:], NE), ALU.mult))
            link(v.tensor_reduce(grp[:], lg[:].rearrange(grouped, e=NE // NG), AX_X, ALU.max))
        if m == 1:
            compare(grp, NG)
            link(fewer_than_two(grank, NG))
            link(v.tensor_tensor(masked[:].rearrange(grouped, e=NE // NG), lg[:].rearrange(grouped, e=NE // NG),
                                 grank[:].rearrange("p t (g o) -> p t g o", o=1).to_broadcast([P, TT, NG, NE // NG]), ALU.mult))
        if m == 2:
            compare(masked, NE)
            fewer_than_two(chosen, NE).then_inc(chosen_ok, 1)
            v.wait_ge(chosen_ok, 1)
            link(v.tensor_tensor(masked[:], chosen[:], masked[:], ALU.mult))
        if m == 3:
            v.wait_ge(pos_ready, 1)
            sums = psum[:, LB, 0:2 * TT * NE].rearrange("p (r t e) -> p r t e", r=2, e=NE)
            v.tensor_copy(pos[:], sums[:, 0, :, :]).then_inc(pos_kept, 1)
            v.tensor_copy(held[:], sums[:, 1, :, :]).then_inc(pos_kept, 1)
            link(v.memset(acc[:, 0, :], 0.0))
            v.wait_ge(pos_kept, 2)
            for t in range(TT):
                link(v.tensor_tensor(acc[:, t + 1, :], acc[:, t, :], held[:, t, :], ALU.add))
            full = compared[:, 0, 0:NE * EXT].rearrange("p (e j) -> p e j", j=EXT)
            link(v.tensor_tensor(full, acc[:, TT, :].rearrange("p (e o) -> p e o", o=1).to_broadcast([P, NE, EXT]), steps_of[:], ALU.is_gt))
            link(v.tensor_reduce(tiles[:], full, AX_X, ALU.add))
        if m == 4:
            over = compared[:, 0, 0:NE * NE].rearrange("p (e f) -> p e f", f=NE)
            link(v.tensor_tensor(over, before[:], tiles[:].rearrange("p (o f) -> p o f", o=1).to_broadcast([P, NE, NE]), ALU.mult))
            link(v.tensor_reduce(start[:], over, AX_X, ALU.add))
            link(v.tensor_tensor(end[:], start[:], tiles[:], ALU.add))
            ended = compared[:, 0, 0:NT * NE].rearrange("p (j e) -> p j e", e=NE)
            link(v.tensor_tensor(ended, tile_no[:], end[:].rearrange("p (o e) -> p o e", o=1).to_broadcast([P, NT, NE]), ALU.is_ge))
            link(v.tensor_reduce(expert_f[:], ended, AX_X, ALU.add))
            link(v.tensor_scalar(expert_f[:], expert_f[:], float(NE - 1), float(NSH), ALU.min, ALU.add))
            v.tensor_copy(expert[:], expert_f[:]).then_inc(expert_ok, 1)
            link(v.tensor_tensor(pos[:], pos[:], acc[:, 0:TT, :], ALU.add))
            link(v.scalar_tensor_tensor(out=pos[:], in0=start[:].rearrange("p (o e) -> p o e", o=1).to_broadcast([P, TT, NE]),
                                        scalar=float(SLOTS), in1=pos[:], op0=ALU.mult, op1=ALU.add))
            link(v.scalar_tensor_tensor(out=held[:], in0=pos[:], scalar=-float(NT * SLOTS), in1=chosen[:], op0=ALU.add, op1=ALU.mult))
            link(v.tensor_reduce(slot_f[:, 0, :], held[:], AX_X, ALU.min))
            link(v.tensor_scalar(slot_f[:, 0, :], slot_f[:, 0, :], float(NT * SLOTS), None, ALU.add))
            link(v.tensor_tensor(held[:], pos[:], chosen[:], ALU.mult))
            link(v.tensor_reduce(slot_f[:, 1, :], held[:], AX_X, ALU.max))
            v.tensor_copy(slot[:], slot_f[:]).then_inc(slot_ok, 1)
        if m == 5:
            for i in range(TOP):
                link(v.tensor_tensor(held[:], pos[:], per_tile(slot_f[:, i, :], NE), ALU.is_equal))
                link(v.tensor_tensor(held[:], held[:], masked[:], ALU.mult))
                v.tensor_reduce(weight[:, i, :], held[:], AX_X, ALU.add).then_inc(weight_ok, 1)
                v.wait_ge(weight_ok, i + 1)
    made = Parts()
    made.tensor_first, made.scalar_first, made.vector_first = tensor_first, scalar_first, vector_first
    made.sync, made.tensor, made.scalar, made.vector = sync, tensor, scalar, vector
    made.expert, made.slot, made.weight = expert, slot, weight
    made.pos_kept, made.expert_ok, made.slot_ok, made.weight_ok = pos_kept, expert_ok, slot_ok, weight_ok
    return made


def phase_moe(nc, d, g):
    psum, x = g["psum"], g["x"]
    UP, DN, XB = 0, 4, 6
    with ExitStack() as ctx:
        n = Names(nc, ctx, "moe")
        xT_hi, xT_lo = n.sb("xT_hi", [P, DC, TOK], F32R), n.sb("xT_lo", [P, DC, TOK], F32R)
        g["xT_hi"], g["xT_lo"] = xT_hi, xT_lo
        raw1, raw2 = n.sb("raw1", [P, 2, DC, FE]), n.sb("raw2", [P, NC, D])
        w1_hi, w1_lo = n.sb("w1_hi", [P, 2, 2, DC, FE], F32R), n.sb("w1_lo", [P, 2, 2, DC, FE], F32R)
        w2_hi, w2_lo = n.sb("w2_hi", [P, 2, NC, D], F32R), n.sb("w2_lo", [P, 2, NC, D], F32R)
        h_hi, h_lo = n.sb("h_hi", [P, NC, TOK], F32R), n.sb("h_lo", [P, NC, TOK], F32R)
        s1, hh = n.sb("s1", [P, 2, HALF]), n.sb("hh", [P, 2, HALF])
        tT_hi, tT_lo = n.sb("tT_hi", [P, 2, DC, SLOTS], F32R), n.sb("tT_lo", [P, 2, DC, SLOTS], F32R)
        rows = n.sb("rows", [P, TT, D])
        SR = SLOTS // P
        S_ = n.sem
        in1, in2, w_hi_ok, w_ok = [S_("in_gate"), S_("in_up")], S_("in2"), S_("w_hi_ok"), S_("w_ok")
        up_s, act_s, hh_s, hhi_s, h_s, dn_ready, dn_ok = (S_(k) for k in ("up_s", "act_s", "hh_s", "hhi_s", "h_s", "dn_ready", "dn_ok"))
        up_t, act_t, hh_t, hhi_t, h_t, y_ready, y_ok = (S_(k) for k in ("up_t", "act_t", "hh_t", "hhi_t", "h_t", "y_ready", "y_ok"))
        scattered, x_in, xt_ready, xhi_ok, xlo_ok = S_("scattered"), [S_("x_in0"), S_("x_in1")], S_("xt_ready"), S_("xhi_ok"), S_("xlo_ok")
        y_stored, back, added, stored = [S_("y_stored0"), S_("y_stored1")], [S_(f"back{i}") for i in range(TT)], S_("added"), S_("stored")
        norm = Norm(n, g, rows)
        route = route_programs(n, d, g)
        block = ctx.enter_context(nc.Block())
        NW = 3
        U = NC * NHALF
        LAST = NT + 1

        def tiles(e, step):
            for j in range(3):
                step(j, j % 2)
            with e.Fori(2, (NT - 1) // 2) as i:
                step(2 * i - 1, 1)
                step(2 * i, 0)
            for j in range(NT - 2, NT):
                step(j, j % 2)

        def exists(j):
            return not isinstance(j, int) or j < NT

        @block.sync
        def _(sp):
            def load(k, e):
                for i, name in enumerate(("eg", "eu")):
                    wait(sp, w_ok, NW * (k - 1) + i + 1)
                    sp.dma_start(raw1[:, i, :, :], d[name][e]).then_inc(in1[i], 16)
                wait(sp, w_ok, NW * k)
                sp.dma_start(raw2[:, 0:2, :], d["ed"][e, 0:2 * P, :].rearrange("(c p) k -> p c k", p=P)).then_inc(in2, 16)
                sp.dma_start(raw2[0:WD[2], 2, :], d["ed"][e, 2 * P:FE, :]).then_inc(in2, 16)

            def load_of_tile(j):
                load(j + 1, sp.value_load(route.expert[0:1, bass.ds(j, 1)], min_val=NSH, max_val=NEX - 1))

            def load_rows(j, q):
                wait(sp, xt_ready, j - 1)
                sp.dma_start(rows[:, SR * q:SR * (q + 1), :],
                             d["slot_rows"][bass.ds(j * SLOTS, SLOTS), :].rearrange("(a p) k -> p a k", p=P)).then_inc(x_in[q], 16)
            load(0, 0)
            route.sync(sp)
            sp.wait_ge(route.expert_ok, 1)
            load_of_tile(0)
            sp.wait_ge(scattered, 16 * TOP * TT)
            load_rows(0, 0)
            load_rows(1, 1)

            def step(j, q):
                if exists(j + 1):
                    load_of_tile(j + 1)
                if exists(j + 2):
                    load_rows(j + 2, q)
            tiles(sp, step)
            load(LAST, 1)
            for t in range(TT):
                sp.wait_ge(dn_ok, TT + t + 1)
                sp.dma_start(d["out"][t * P:(t + 1) * P, :], x[:, t, :]).then_inc(stored, 16)
            sp.wait_ge(stored, 16 * TT)

        @block.gpsimd
        def _(pool):
            norm.roots(pool)
            pool.wait_ge(route.slot_ok, 1)
            pool.wait_ge(norm.normed, TT)
            for t in range(TT):
                for i in range(TOP):
                    pool.indirect_dma_start(d["slot_rows"], bass.IndirectOffsetOnAxis(ap=route.slot[:, i, t:t + 1], axis=0),
                                            rows[:, t, :], None).then_inc(scattered, 16)

            def step(j, q):
                pool.wait_ge(y_ok, j + 1)
                pool.dma_start(d["slot_out"][bass.ds(j * SLOTS, SLOTS), :].rearrange("(a p) k -> p a k", p=P),
                               rows[:, TT // 2 + SR * q:TT // 2 + SR * (q + 1), :]).then_inc(y_stored[q], 16)
            tiles(pool, step)
            pool.wait_ge(y_stored[0], 16 * ((NT + 1) // 2))
            pool.wait_ge(y_stored[1], 16 * (NT // 2))
            pool.wait_ge(xt_ready, NT)
            for t in range(TT):
                for i in range(TOP):
                    r = (TOP * t + i) % TT
                    wait(pool, added, TOP * t + i - TT + 1)
                    pool.indirect_dma_start(rows[:, r, :], None, d["slot_out"],
                                            bass.IndirectOffsetOnAxis(ap=route.slot[:, i, t:t + 1], axis=0)).then_inc(back[r], 16)

        @block.tensor
        def _(pe):
            def shared(s):
                k, p = s * LAST, 0
                pe.wait_ge(w_ok, NW * (k + 1))
                if s:
                    pe.wait_ge(hh_t, NC * NT)
                for half in range(NHALF):
                    cols, f0 = slice(half * HALF, (half + 1) * HALF), 0
                    for c, wd in enumerate(WD):
                        m = half * NC + c
                        wait(pe, hh_s, U * s + m - 1)
                        for i in range(2):
                            for dc in range(DC):
                                last = passes(pe, psum[0:wd, UP + 2 * (m % 2) + i, :], w1_hi[:, p, i, dc, f0:f0 + wd],
                                              w1_lo[:, p, i, dc, f0:f0 + wd], xT_hi[:, dc, cols], xT_lo[:, dc, cols],
                                              dc == 0, dc == DC - 1)
                        last.then_inc(up_s, 1)
                        f0 += wd
                        if not s:
                            route.tensor(pe, m)
                if s:
                    pe.wait_ge(y_ok, NT)
                else:
                    pe.wait_ge(route.pos_kept, 2)
                for t in range(TT):
                    pe.wait_ge(h_s, U * s + (NC if t < TT // 2 else U))
                    wait(pe, dn_ok, TT * s + t - 3)
                    toks = slice(t * P, (t + 1) * P)
                    for c, wd in enumerate(WD):
                        last = passes(pe, psum[:, DN + t % 4, :], h_hi[0:wd, c, toks], h_lo[0:wd, c, toks],
                                      w2_hi[0:wd, p, c, :], w2_lo[0:wd, p, c, :], c == 0, c == NC - 1)
                    last.then_inc(dn_ready, 1)

            def transpose_rows(j, q):
                pe.wait_ge(x_in[q], 8 * (j - q) + 16)
                wait(pe, xlo_ok, j)
                for c in range(DC):
                    for a in range(SR):
                        m = pe.transpose(psum[:, XB + c // 2, (c % 2) * SLOTS + a * P:(c % 2) * SLOTS + (a + 1) * P],
                                         rows[:, SR * q + a, c * P:(c + 1) * P], g["ident"][:])
                m.then_inc(xt_ready, 1)

            def step(j, q):
                p = 1 - q
                pe.wait_ge(w_ok, NW * (j + 1) + 2)
                pe.wait_ge(xlo_ok, j + 1)
                f0 = 0
                for c, wd in enumerate(WD):
                    wait(pe, hh_t, NC * (j - 1) + c + 1)
                    for i in range(2):
                        for dc in range(DC):
                            last = passes(pe, psum[0:wd, UP + c, i * SLOTS:(i + 1) * SLOTS], w1_hi[:, p, i, dc, f0:f0 + wd],
                                          w1_lo[:, p, i, dc, f0:f0 + wd], tT_hi[:, q, dc, :], tT_lo[:, q, dc, :],
                                          dc == 0, dc == DC - 1)
                    last.then_inc(up_t, 1)
                    f0 += wd
                if exists(j + 1):
                    transpose_rows(j + 1, 1 - q)
                pe.wait_ge(h_t, NC * (j + 1))
                pe.wait_ge(w_ok, NW * (j + 2))
                wait(pe, y_ok, j)
                for a in range(SR):
                    toks = slice(q * SLOTS + a * P, q * SLOTS + (a + 1) * P)
                    for c, wd in enumerate(WD):
                        last = passes(pe, psum[:, DN + a, :], h_hi[0:wd, c, toks], h_lo[0:wd, c, toks],
                                      w2_hi[0:wd, p, c, :], w2_lo[0:wd, p, c, :], c == 0, c == NC - 1)
                last.then_inc(y_ready, 1)
            norm.transpose(pe)
            pe.wait_ge(norm.lo_done, TT)
            route.tensor_first(pe)
            shared(0)
            pe.wait_ge(dn_ok, TT)
            pe.wait_ge(hh_s, U)
            transpose_rows(0, 0)
            tiles(pe, step)
            shared(1)

        def piece_free(e, k, p):
            if isinstance(k, int) and k == 2:
                e.wait_ge(dn_ready, TT)
            elif not isinstance(k, int) or k > 2:
                e.wait_ge(y_ready, k - 2)

        @block.scalar
        def _(act):
            def split(k, p, i):
                if i == 0:
                    piece_free(act, k, p)
                if i < 2:
                    act.wait_ge(in1[i], 16 * (k + 1))
                    act.activation(w1_hi[:, p, i, :, :], raw1[:, i, :, :], ACT.Copy).then_inc(w_hi_ok, 1)
                else:
                    act.wait_ge(in2, 32 * (k + 1))
                    act.activation(w2_hi[:, p, 0:2, :], raw2[:, 0:2, :], ACT.Copy)
                    act.activation(w2_hi[0:WD[2], p, 2, :], raw2[0:WD[2], 2, :], ACT.Copy).then_inc(w_hi_ok, 1)

            def shared(s):
                for m in range(U):
                    half, c = divmod(m, NC)
                    wd = WD[c]
                    act.wait_ge(up_s, U * s + m + 1)
                    wait(act, hh_s, U * s + m - 1)
                    act.activation(s1[0:wd, m % 2, :], psum[0:wd, UP + 2 * (m % 2), :], ACT.Silu).then_inc(act_s, 1)
                    if s and m == 0:
                        act.wait_ge(y_ready, NT)
                    act.wait_ge(hh_s, U * s + m + 1)
                    act.activation(h_hi[0:wd, c, half * HALF:(half + 1) * HALF], hh[0:wd, m % 2, :], ACT.Copy).then_inc(hhi_s, 1)
                    if not s and m == 0:
                        route.scalar(act)

            def rows_hi(j, q):
                act.wait_ge(xt_ready, j + 1)
                wait(act, y_ready, j - 1)
                act.activation(tT_hi[:, q, :, :], psum[:, XB:XB + 2, :].rearrange("p b (c k) -> p (b c) k", k=SLOTS),
                               ACT.Copy).then_inc(xhi_ok, 1)

            def step(j, q):
                p = 1 - q
                for c, wd in enumerate(WD):
                    if c < 2:
                        split(j + 2, 1 - p, c)
                    m, b = NC * j + c, (q + c) % 2
                    act.wait_ge(up_t, m + 1)
                    if isinstance(j, int) and m < 2:
                        act.wait_ge(dn_ready, TT)
                        act.wait_ge(hh_s, U)
                    wait(act, hh_t, m - 1)
                    act.activation(s1[0:wd, b, 0:SLOTS], psum[0:wd, UP + c, 0:SLOTS], ACT.Silu).then_inc(act_t, 1)
                    if c == 0:
                        wait(act, y_ready, j - 1)
                    act.wait_ge(hh_t, m + 1)
                    act.activation(h_hi[0:wd, c, q * SLOTS:(q + 1) * SLOTS], hh[0:wd, b, 0:SLOTS], ACT.Copy).then_inc(hhi_t, 1)
                if exists(j + 1):
                    rows_hi(j + 1, 1 - q)
                split(j + 2, 1 - p, 2)
            norm.high_parts(act)
            for i in range(NW):
                split(0, 0, i)
            route.scalar_first(act)
            shared(0)
            for i in range(NW):
                split(1, 1, i)
            rows_hi(0, 0)
            tiles(act, step)
            shared(1)

        @block.vector
        def _(v):
            def split(k, p, i):
                if i == 0:
                    piece_free(v, k, p)
                v.wait_ge(w_hi_ok, NW * k + i + 1)
                if i < 2:
                    v.tensor_tensor(w1_lo[:, p, i, :, :], raw1[:, i, :, :], w1_hi[:, p, i, :, :].bitcast(F32), ALU.subtract).then_inc(w_ok, 1)
                else:
                    v.tensor_tensor(w2_lo[:, p, 0:2, :], raw2[:, 0:2, :], w2_hi[:, p, 0:2, :].bitcast(F32), ALU.subtract)
                    v.tensor_tensor(w2_lo[0:WD[2], p, 2, :], raw2[0:WD[2], 2, :], w2_hi[0:WD[2], p, 2, :].bitcast(F32),
                                    ALU.subtract).then_inc(w_ok, 1)

            def shared(s):
                for m in range(U):
                    half, c = divmod(m, NC)
                    wd = WD[c]
                    v.wait_ge(act_s, U * s + m + 1)
                    wait(v, h_s, U * s + m - 1)
                    v.tensor_tensor(hh[0:wd, m % 2, :], s1[0:wd, m % 2, :], psum[0:wd, UP + 2 * (m % 2) + 1, :], ALU.mult).then_inc(hh_s, 1)
                    v.wait_ge(hhi_s, U * s + m + 1)
                    v.tensor_tensor(h_lo[0:wd, c, half * HALF:(half + 1) * HALF], hh[0:wd, m % 2, :],
                                    h_hi[0:wd, c, half * HALF:(half + 1) * HALF].bitcast(F32), ALU.subtract).then_inc(h_s, 1)
                    if not s:
                        route.vector(v, m)
                    if s and m == NC - 1:
                        add_back(0, TT // 2)
                for t in range(TT):
                    v.wait_ge(dn_ready, TT * s + t + 1)
                    if s:
                        v.wait_ge(added, TOP * (t + 1))
                    v.tensor_tensor(x[:, t, :], x[:, t, :], psum[:, DN + t % 4, :], ALU.add).then_inc(dn_ok, 1)
                    if s and t < TT // 2:
                        add_back(TT // 2 + t, TT // 2 + t + 1)
                    if not s and t % 2 and t // 2 < NW:
                        split(1, 1, t // 2)

            def add_back(t0, t1):
                v.wait_ge(route.weight_ok, TOP)
                for t in range(t0, t1):
                    for i in range(TOP):
                        r = (TOP * t + i) % TT
                        v.wait_ge(back[r], 16 * (1 + (TOP * t + i) // TT))
                        wait(v, added, TOP * t + i)
                        v.scalar_tensor_tensor(out=x[:, t, :], in0=rows[:, r, :], scalar=route.weight[:, i, t:t + 1],
                                               in1=x[:, t, :], op0=ALU.mult, op1=ALU.add).then_inc(added, 1)

            def rows_lo(j, q):
                v.wait_ge(xhi_ok, j + 1)
                v.tensor_tensor(tT_lo[:, q, :, :], psum[:, XB:XB + 2, :].rearrange("p b (c k) -> p (b c) k", k=SLOTS),
                                tT_hi[:, q, :, :].bitcast(F32), ALU.subtract).then_inc(xlo_ok, 1)

            def keep_results(j, q):
                v.wait_ge(y_ready, j + 1)
                wait(v, y_stored[q], 8 * (j - q))
                v.tensor_copy(rows[:, TT // 2 + SR * q:TT // 2 + SR * (q + 1), :], psum[:, DN:DN + SR, :]).then_inc(y_ok, 1)

            def step(j, q):
                p = 1 - q
                if not isinstance(j, int) or j > 0:
                    keep_results(j - 1, 1 - q)
                for c, wd in enumerate(WD):
                    if c < 2:
                        split(j + 2, 1 - p, c)
                    m, b = NC * j + c, (q + c) % 2
                    v.wait_ge(act_t, m + 1)
                    wait(v, h_t, m - 1)
                    v.tensor_tensor(hh[0:wd, b, 0:SLOTS], s1[0:wd, b, 0:SLOTS], psum[0:wd, UP + c, SLOTS:2 * SLOTS],
                                    ALU.mult).then_inc(hh_t, 1)
                    v.wait_ge(hhi_t, m + 1)
                    v.tensor_tensor(h_lo[0:wd, c, q * SLOTS:(q + 1) * SLOTS], hh[0:wd, b, 0:SLOTS],
                                    h_hi[0:wd, c, q * SLOTS:(q + 1) * SLOTS].bitcast(F32), ALU.subtract).then_inc(h_t, 1)
                if exists(j + 1):
                    rows_lo(j + 1, 1 - q)
                split(j + 2, 1 - p, 2)
            norm.statistics(v)
            norm.normalise(v)
            route.vector_first(v)
            for i in range(NW):
                split(0, 0, i)
            shared(0)
            rows_lo(0, 0)
            tiles(v, step)
            keep_results(NT - 1, (NT - 1) % 2)
            shared(1)


def phase_rest(nc, d, g):
    with ExitStack() as mix:
        a = Names(nc, mix, "mix")
        feat = a.sb("feat", [P, FEATS, TOK])
        bias, cumS = a.sb("bias", [P, TT, NH]), a.sb("cumS", [P, TOK], F32R)
        with ExitStack() as inner:
            m = Names(nc, inner, "second")
            g["xT_hi"], g["xT_lo"] = m.sb("xT_hi", [P, DC, TOK], F32R), m.sb("xT_lo", [P, DC, TOK], F32R)
            once, twice, scaled = (feat[:, TT // 2 * i:TT // 2 * (i + 1), :].rearrange("p f (a k) -> p (f a) k", k=D) for i in range(3))
            phase_mlp(nc, d, g,
                      make_norm=lambda n: Norm(n, g, twice, affine=(once, scaled.rearrange("p t (c k) -> p t c k", k=P), d["ln_wb"])),
                      make_after=lambda n, mlp: project_programs(nc, n, d, g, mlp, feat, bias, cumS))
        phase_scan(nc, d, g, feat, bias, cumS)
    phase_moe(nc, d, g)


def more_layout(w):
    import numpy as np
    f32 = np.float32

    def chunk_k(a):
        return a.reshape(DC, P, -1).transpose(1, 0, 2)
    w_in = w["L0_attn_W_in"]
    o = np.cumsum([0, DI, NX * HD, NX * NST, DI, NH])
    z, xb, bp, cp, dtw = (w_in[:, o[i]:o[i + 1]] for i in range(5))
    order = [[REP * 2 * m + j, REP * (2 * m + 1) + j] for m in range(2) for j in range(REP)]
    cols = np.array([[h * HD + i for h in pair for i in range(HD)] for pair in order])
    feats = [z[:, c] for c in cols] + [cp[:, c] for c in cols] + [xb[:, :P], xb[:, P:], bp[:, :P], bp[:, P:]]
    t = np.arange(P)
    mask = np.where((t[:, None] // S == t[None, :] // S) & (t[:, None] <= t[None, :]), 0.0, -1e30).astype(f32)
    per = lambda a: a[cols].T
    return {
        "ln_wb": np.stack([w["L0_attn_ln_w"].reshape(DC, P).T, w["L0_attn_ln_b"].reshape(DC, P).T], 1),
        "w_feat": np.stack([chunk_k(f) for f in feats]),
        "w_dt": chunk_k(dtw),
        "head": np.tile(np.stack([w["L0_attn_dt_bias"], w["L0_attn_A_log"]])[None, :, None, :], (P, 1, TT, 1)),
        "tri": (mask == 0).astype(f32),
        "norm_w": per(w["L0_attn_norm_w"]),
        "d_skip": per(np.repeat(w["L0_attn_D"], HD)),
        "mask": mask,
        "w_out": w["L0_attn_W_out"][cols],
        "fc1": w["L0_attn_fc1_w"].reshape(DC, P, MG, MC * P).transpose(2, 1, 0, 3),
        "fc1_b": w["L0_attn_fc1_b"].reshape(MG, MC, P).transpose(2, 0, 1),
        "fc2": w["L0_attn_fc2_w"].reshape(MG, MC, P, D).transpose(0, 2, 1, 3),
        "fc2_b": np.tile(w["L0_attn_fc2_b"], (P, 1)),
        "gate_weight": chunk_k(w["L0_ffn_gate_weight"].T),
        "before": np.tile((np.arange(NE)[None, :] < np.arange(NE)[:, None]).astype(f32)[None], (P, 1, 1)),
        "steps_of": np.tile(np.arange(EXT, dtype=f32) * SLOTS, (P, NE, 1)),
        "tile_no": np.tile(np.arange(NT, dtype=f32)[None, :, None], (P, 1, NE)),
        "earlier": np.stack([(t[:, None] < t[None, :]).astype(f32), np.ones((P, P), f32)], 1),
        "eg": experts_in(w["L0_ffn_gate_w"], w["L0_ffn_sh_gate_w"]),
        "eu": experts_in(w["L0_ffn_up_w"], w["L0_ffn_sh_up_w"]),
        "ed": np.concatenate([w["L0_ffn_sh_down_w"].T.reshape(NSH, FE, D), w["L0_ffn_down_w"].transpose(0, 2, 1)]),
    }


def experts_in(routed, shared):
    import numpy as np
    a = np.concatenate([shared.reshape(NSH, FE, D), routed])
    return a.transpose(0, 2, 1).reshape(NEX, DC, P, FE).transpose(0, 2, 1, 3)


def build(nc, d):
    SEMAPHORES.clear()
    with ExitStack() as top:
        n = Names(nc, top, "all")
        d["tail_rows"] = nc.dram_tensor("tail_rows", [B, 3, P], F32, kind="Internal").ap()
        d["slot_rows"], d["slot_out"] = (nc.dram_tensor(k, [NT * SLOTS, D], F32, kind="Internal").ap() for k in ("slot_rows", "slot_out"))
        g = {"psum": top.enter_context(nc.psum_tensor("psum", [P, 8, 512], F32)),
             "x": n.sb("x", [P, TT, D]), "ident": n.sb("ident", [P, P]), "stats": n.sb("stats", [P, TT, 6]),
             "tailT_hi": n.sb("tailT_hi", [P, B, 2], F32R), "tailT_lo": n.sb("tailT_lo", [P, B, 2], F32R)}
        g["x_loaded"], g["tail_stored"] = [n.sem(f"x_loaded{t}") for t in range(TT)], n.sem("tail_stored")
        phase_context_tail(nc, d, g)
        with ExitStack() as ctx:
            a = Names(nc, ctx, "q")
            q = a.sb("q", [P, B, HS])
            G_hi, G_lo = a.sb("G_hi", [P, H * D], F32R), a.sb("G_lo", [P, H * D], F32R)
            with ExitStack() as inner:
                m = Names(nc, inner, "first")
                g["xT_hi"], g["xT_lo"] = m.sb("xT_hi", [P, DC, TOK], F32R), m.sb("xT_lo", [P, DC, TOK], F32R)
                phase_heads(nc, d, g, q, G_hi, G_lo)
            phase_attention(nc, d, g, q, G_hi, G_lo)
        clear_semaphores(nc)
        phase_rest(nc, d, g)


def kernel(**inputs):
    import numpy as np
    import concourse.bacc as bacc
    from concourse.bass_utils import run_bass_kernel_spmd as run

    w = {k: np.asarray(v) for k, v in inputs.items()}
    f32 = np.float32
    inv_freq = (f32(1.0) / np.power(f32(10000.0), np.arange(0, P, 2, dtype=f32) / f32(P), dtype=f32)).astype(f32)
    angle = np.repeat(np.arange(L, dtype=f32)[:, None] * inv_freq[None, :], 2, axis=-1).astype(np.float64)
    cos, sin = np.cos(angle).astype(f32), np.sin(angle).astype(f32)
    sin[:, :P // 2] *= -1
    t = {
        "x": w["x"].reshape(TOK, D),
        "ctx": w["ctx_512"],
        "cos_main": cos[:2 * P].reshape(2, P, P).transpose(1, 0, 2),
        "sin_main": sin[:2 * P].reshape(2, P, P).transpose(1, 0, 2),
        "cos_last": np.tile(cos[L - 1], (B, 1)), "sin_last": np.tile(sin[L - 1], (B, 1)),
        "ident": np.eye(P, dtype=f32),
        "wq": w["L0_xattn_Wq"],
        "kcqT": w["L0_xattn_w_kc_q"].transpose(0, 2, 1).reshape(H, QC, P, P).transpose(0, 2, 1, 3),
        "wqr": w["L0_xattn_W_qr"].reshape(H, QC, P, R).transpose(0, 2, 1, 3),
        "wkrT": w["L0_xattn_W_kr"].transpose(0, 2, 1),
        "kckv": w["L0_xattn_w_kc_kv"],
        "woT": w["L0_xattn_Wo"].T,
    }
    t.update(more_layout(w))
    nc = bacc.Bacc("TRN2", target_bir_lowering=False, num_devices=1)
    arrays, d = {}, {}
    for name, a in t.items():
        arrays[f"in_{name}"] = np.ascontiguousarray(a)
        d[name] = nc.dram_tensor(f"in_{name}", a.shape, mybir.dt.from_np(a.dtype), kind="ExternalInput").ap()
    d["out"] = nc.dram_tensor("out", (TOK, D), F32, kind="ExternalOutput").ap()
    build(nc, d)
    r = run(nc, [arrays], core_ids=[0])
    return r.results[0]["out"].reshape(B, S, D)
```
